# Optimizing a Trainium2 kernel written in Bass

```python
import numpy as np
import jax
import jax.numpy as jnp

def _softmax(x, axis=-1):
    return jax.nn.softmax(x, axis=axis)

def _gelu(x):
    return jax.nn.gelu(x, approximate=True)

def _silu(x):
    return jax.nn.silu(x)

def _sigmoid(x):
    return jax.nn.sigmoid(x)

def _layernorm(x, axis=-1, eps=1e-05):
    m = jnp.mean(x, axis=axis, keepdims=True)
    v = jnp.var(x, axis=axis, keepdims=True)
    return (x - m) / jnp.sqrt(v + eps)

def _scatter_add(tgt, idx, src, axis=0):
    return tgt.at[idx].add(src)

def _segment_sum(src, seg, n):
    return jax.ops.segment_sum(src, seg, n)
kernel_name = 'mk_conv_attn_hybrid_d2_conv_nchw512_r4_95f944'

def setup_inputs(seed: int=0):
    np.random.seed(seed)
    _w = jnp.asarray

    def _rec_inputs():
        import jax
        import jax.numpy as jnp
        _gk = jax.random.key(seed)
        x = -0.000125 + 0.9999 * jax.random.normal(jax.random.fold_in(_gk, 1), (16, 128, 16, 16), jnp.float32)
        return x
    x = _rec_inputs()

    def _L0_conv_setup():
        import jax, jax.numpy as jnp
        import numpy as np
        B, C, H, W, K = (16, 128, 16, 16, 7)
        LN_EPS = 1e-05
        key = jax.random.key(seed)
        ks = jax.random.split(key, 6)
        x = jax.random.normal(ks[0], (B, C, H, W), dtype=jnp.float32)
        K_w = jax.random.normal(ks[1], (K * K, C), dtype=jnp.float32) * 0.02
        K_b = jnp.zeros((K * K,), dtype=jnp.float32)
        conv0_w = jax.random.normal(ks[2], (C, C), dtype=jnp.float32) * 0.02
        conv0_b = jnp.zeros((C,), dtype=jnp.float32)
        ln_w = jnp.ones((C, K, K), dtype=jnp.float32)
        ln_b = jnp.zeros((C, K, K), dtype=jnp.float32)
        conv1_w = jax.random.normal(ks[3], (C, C), dtype=jnp.float32) * 0.02
        conv1_b = jnp.zeros((C,), dtype=jnp.float32)
        return {'x': x, 'K_w': K_w, 'K_b': K_b, 'conv0_w': conv0_w, 'conv0_b': conv0_b, 'ln_w': ln_w, 'ln_b': ln_b, 'conv1_w': conv1_w, 'conv1_b': conv1_b}
    _L0_conv_all = _L0_conv_setup()
    _L0_conv_in = {k: v for k, v in _L0_conv_all.items() if k in ('K_w', 'K_b', 'conv0_w', 'conv0_b', 'ln_w', 'ln_b', 'conv1_w', 'conv1_b')}
    del _L0_conv_all

    def _L1_attn_setup():
        import jax, jax.numpy as jnp
        import numpy as np
        key = jax.random.key(seed)
        x = jax.random.normal(key, (8, 512, 128), dtype=jnp.float32)
        return {'x': x}
    _L1_attn_all = _L1_attn_setup()
    _L1_attn_in = {k: v for k, v in _L1_attn_all.items() if k in ()}
    del _L1_attn_all

    def _L1_ffn_setup():
        import jax, jax.numpy as jnp
        import numpy as np
        B, S, D = (4, 512, 128)
        E, H, K = (8, 256, 2)

        def _moe_forward(x, router_w, router_b, w1, b1, wg, bg, wv, bv, w2, b2):
            b, s, d = x.shape
            xf = x.reshape(-1, d)
            T = xf.shape[0]
            scores = xf @ router_w + router_b
            probs = jax.nn.softmax(scores, axis=-1)
            topk_p, topk_i = jax.lax.top_k(probs, K)
            gates = jnp.zeros((T, E), xf.dtype).at[jnp.arange(T)[:, None], topk_i].set(topk_p)
            h = jnp.einsum('td,edh->teh', xf, w1) + b1[None]
            gated = jax.nn.silu(jnp.einsum('teh,ehf->tef', h, wg) + bg[None]) * (jnp.einsum('teh,ehf->tef', h, wv) + bv[None])
            y = jnp.einsum('tef,efd->ted', gated, w2) + b2[None]
            out = jnp.einsum('ted,te->td', y, gates)
            return out.reshape(b, s, d)
        key = jax.random.key(seed)
        ks = jax.random.split(key, 8)
        s_in = 0.02
        return {'x': jax.random.normal(ks[0], (B, S, D), jnp.float32), 'router_w': jax.random.normal(ks[1], (D, E), jnp.float32) * s_in, 'router_b': jnp.zeros((E,), jnp.float32), 'w1': jax.random.normal(ks[2], (E, D, H), jnp.float32) * s_in, 'b1': jnp.zeros((E, H), jnp.float32), 'wg': jax.random.normal(ks[3], (E, H, H), jnp.float32) * s_in, 'bg': jnp.zeros((E, H), jnp.float32), 'wv': jax.random.normal(ks[4], (E, H, H), jnp.float32) * s_in, 'bv': jnp.zeros((E, H), jnp.float32), 'w2': jax.random.normal(ks[5], (E, H, D), jnp.float32) * s_in, 'b2': jnp.zeros((E, D), jnp.float32)}
    _L1_ffn_all = _L1_ffn_setup()
    _L1_ffn_in = {k: v for k, v in _L1_ffn_all.items() if k in ('router_w', 'router_b', 'w1', 'b1', 'wg', 'bg', 'wv', 'bv', 'w2', 'b2')}
    del _L1_ffn_all
    return {'x': x, 'L0_conv_K_w': _L0_conv_in['K_w'], 'L0_conv_K_b': _L0_conv_in['K_b'], 'L0_conv_conv0_w': _L0_conv_in['conv0_w'], 'L0_conv_conv0_b': _L0_conv_in['conv0_b'], 'L0_conv_ln_w': _L0_conv_in['ln_w'], 'L0_conv_ln_b': _L0_conv_in['ln_b'], 'L0_conv_conv1_w': _L0_conv_in['conv1_w'], 'L0_conv_conv1_b': _L0_conv_in['conv1_b'], 'L1_ffn_router_w': _L1_ffn_in['router_w'], 'L1_ffn_router_b': _L1_ffn_in['router_b'], 'L1_ffn_w1': _L1_ffn_in['w1'], 'L1_ffn_b1': _L1_ffn_in['b1'], 'L1_ffn_wg': _L1_ffn_in['wg'], 'L1_ffn_bg': _L1_ffn_in['bg'], 'L1_ffn_wv': _L1_ffn_in['wv'], 'L1_ffn_bv': _L1_ffn_in['bv'], 'L1_ffn_w2': _L1_ffn_in['w2'], 'L1_ffn_b2': _L1_ffn_in['b2']}

def reference(x, L0_conv_K_w, L0_conv_K_b, L0_conv_conv0_w, L0_conv_conv0_b, L0_conv_ln_w, L0_conv_ln_b, L0_conv_conv1_w, L0_conv_conv1_b, L1_ffn_router_w, L1_ffn_router_b, L1_ffn_w1, L1_ffn_b1, L1_ffn_wg, L1_ffn_bg, L1_ffn_wv, L1_ffn_bv, L1_ffn_w2, L1_ffn_b2):
    import jax
    import jax.numpy as jnp

    def _L0_conv_ref(x, K_w, K_b, conv0_w, conv0_b, ln_w, ln_b, conv1_w, conv1_b):
        import jax, jax.numpy as jnp
        import numpy as np
        B, C, H, W, K = (16, 128, 16, 16, 7)
        LN_EPS = 1e-05
        b, c, h, w = x.shape
        kk = K_w.shape[0]
        k = int(round(kk ** 0.5))
        hw = h * w
        query = x.reshape(b, c, hw)
        key = jnp.einsum('bchw,oc->bohw', x, K_w) + K_b[None, :, None, None]
        key = key.reshape(b, kk, hw).transpose(0, 2, 1)
        key = jax.nn.softmax(key, axis=1)
        filters = jnp.einsum('bcn,bnk->bck', query, key).reshape(b, c, k, k)
        filters = jnp.einsum('bcij,oc->boij', filters, conv0_w) + conv0_b[None, :, None, None]
        mean = jnp.mean(filters, axis=(1, 2, 3), keepdims=True)
        var = jnp.var(filters, axis=(1, 2, 3), keepdims=True)
        filters = (filters - mean) * jax.lax.rsqrt(var + LN_EPS)
        filters = filters * ln_w[None] + ln_b[None]
        filters = jax.nn.relu(filters)
        filters = jnp.einsum('bcij,oc->boij', filters, conv1_w) + conv1_b[None, :, None, None]
        wgt = filters.reshape(b * c, 1, k, k)
        x_r = x.reshape(1, b * c, h, w)
        pad = k // 2
        out = jax.lax.conv_general_dilated(x_r, wgt, window_strides=(1, 1), padding=[(pad, pad), (pad, pad)], feature_group_count=b * c, dimension_numbers=('NCHW', 'OIHW', 'NCHW'))
        return out.reshape(b, c, h, w)

    def _L1_attn_ref(x):
        import jax, jax.numpy as jnp
        import numpy as np
        q = jnp.tanh(x)
        scale = 1.0 / jnp.sqrt(jnp.asarray(x.shape[-1], dtype=x.dtype))
        scores = jnp.einsum('bsd,btd->bst', q, q) * scale
        a = jax.nn.softmax(scores, axis=-1)
        return jnp.einsum('bst,btd->bsd', a, x)

    def _L1_ffn_ref(x, router_w, router_b, w1, b1, wg, bg, wv, bv, w2, b2):
        import jax, jax.numpy as jnp
        import numpy as np
        B, S, D = (4, 512, 128)
        E, H, K = (8, 256, 2)

        def _moe_forward(x, router_w, router_b, w1, b1, wg, bg, wv, bv, w2, b2):
            b, s, d = x.shape
            xf = x.reshape(-1, d)
            T = xf.shape[0]
            scores = xf @ router_w + router_b
            probs = jax.nn.softmax(scores, axis=-1)
            topk_p, topk_i = jax.lax.top_k(probs, K)
            gates = jnp.zeros((T, E), xf.dtype).at[jnp.arange(T)[:, None], topk_i].set(topk_p)
            h = jnp.einsum('td,edh->teh', xf, w1) + b1[None]
            gated = jax.nn.silu(jnp.einsum('teh,ehf->tef', h, wg) + bg[None]) * (jnp.einsum('teh,ehf->tef', h, wv) + bv[None])
            y = jnp.einsum('tef,efd->ted', gated, w2) + b2[None]
            out = jnp.einsum('ted,te->td', y, gates)
            return out.reshape(b, s, d)
        return _moe_forward(x, router_w, router_b, w1, b1, wg, bg, wv, bv, w2, b2)

    def _gn(v, G=32, eps=1e-05):
        B_, C_, H_, W_ = v.shape
        g = v.reshape(B_, G, C_ // G, H_, W_)
        m = jnp.mean(g, axis=(2, 3, 4), keepdims=True)
        s = jnp.var(g, axis=(2, 3, 4), keepdims=True)
        return ((g - m) / jnp.sqrt(s + eps)).reshape(v.shape)

    def _ln_c(v, eps=1e-06):
        m = jnp.mean(v, axis=1, keepdims=True)
        s = jnp.var(v, axis=1, keepdims=True)
        return (v - m) / jnp.sqrt(s + eps)

    def _ln_t(v, eps=1e-05):
        m = jnp.mean(v, axis=-1, keepdims=True)
        s = jnp.var(v, axis=-1, keepdims=True)
        return (v - m) / jnp.sqrt(s + eps)

    def _to_tokens(v):
        B_, C_, H_, W_ = v.shape
        return v.reshape(B_, C_, H_ * W_).transpose(0, 2, 1)

    def _from_tokens(t, like):
        B_, C_, H_, W_ = like.shape
        return t.transpose(0, 2, 1).reshape(B_, C_, H_, W_)
    x = x + _L0_conv_ref(_gn(x), L0_conv_K_w, L0_conv_K_b, L0_conv_conv0_w, L0_conv_conv0_b, L0_conv_ln_w, L0_conv_ln_b, L0_conv_conv1_w, L0_conv_conv1_b)
    t = _to_tokens(x)
    t = t + _L1_attn_ref(_ln_t(t))
    t = t + _L1_ffn_ref(_ln_t(t), L1_ffn_router_w, L1_ffn_router_b, L1_ffn_w1, L1_ffn_b1, L1_ffn_wg, L1_ffn_bg, L1_ffn_wv, L1_ffn_bv, L1_ffn_w2, L1_ffn_b2)
    x = _from_tokens(t, x)
    return x

_drawn_inputs = setup_inputs


def setup_inputs(seed=0):
    import zlib

    import numpy as np

    out = dict(_drawn_inputs(seed))
    spreads = {'L0_conv_K_b': (0.0, 2.0),
     'L0_conv_conv0_b': (0.0, 0.1),
     'L0_conv_ln_w': (1.0, 0.2),
     'L0_conv_ln_b': (0.0, 0.1),
     'L0_conv_conv1_b': (0.0, 0.1),
     'L1_ffn_router_b': (0.0, 0.8),
     'L1_ffn_b1': (0.0, 0.8),
     'L1_ffn_bg': (0.0, 0.8),
     'L1_ffn_bv': (0.0, 0.8),
     'L1_ffn_b2': (0.0, 2.0)}
    factors = {'L1_ffn_router_w': 5.451,
     'L1_ffn_w1': 8.0,
     'L1_ffn_wg': 8.0,
     'L1_ffn_wv': 8.0,
     'L1_ffn_w2': 8.0}
    for name, (base, spread) in spreads.items():
        noise = np.random.default_rng([zlib.crc32(name.encode()), seed]).standard_normal(out[name].shape)
        drawn = base * np.exp(spread * noise) if base else spread * noise
        out[name] = jnp.asarray(drawn.astype(out[name].dtype))
    for name, factor in factors.items():
        out[name] = (out[name] * factor).astype(out[name].dtype)
    return out
```

```python
from contextlib import ExitStack

import numpy as np

import concourse.bass as bass
from concourse import mybir

F32 = mybir.dt.float32
BF16 = mybir.dt.bfloat16
U32 = mybir.dt.uint32
I32 = mybir.dt.int32
ALU = mybir.AluOpType
ACT = mybir.ActivationFunctionType
AX = mybir.AxisListType

P = 128
BATCH, C, SIDE_IN, TAPS = 16, 128, 16, 7
HW = SIDE_IN * SIDE_IN
KK = TAPS * TAPS
KKP = 64
GROUP = C // 32
PAIRS = BATCH // 2
CHUNKS = HW // P
TILES = 2 * CHUNKS
PAIR_TOKENS = 2 * HW
TOKENS = BATCH * HW
EXPERTS, HID = 8, 256
EPS = 1e-5

PAD = TAPS // 2
SIDE = SIDE_IN + PAD
FREQS = (SIDE * SIDE + 1) // 2
HALF = (FREQS + 1) // 2

REGION = TOKENS + P
ROWS = EXPERTS * REGION + P
ROW = C + 4
UNROLL = 8
BLOCKS = -(-(2 * TOKENS // P + EXPERTS - 1) // UNROLL) * UNROLL
SKIP = 1 << 20


def constants():
    k = np.arange(P)
    ident = np.eye(P)
    group = (k[:, None] // GROUP == k[None, :] // GROUP) / GROUP
    mean = np.full((P, P), 1.0 / (C * KK))
    before = (k[:, None] < k[None, :]).astype(np.float64)

    freq = [(0, 0)] + [(u, v) for u in range(SIDE) for v in range(SIDE)
                       if (u, v) < ((-u) % SIDE, (-v) % SIDE)]
    u = np.array([f[0] for f in freq] + [0] * (2 * HALF - FREQS))
    v = np.array([f[1] for f in freq] + [0] * (2 * HALF - FREQS))
    used = np.array([1.0] * FREQS + [0.0] * (2 * HALF - FREQS))
    pos = np.arange(HW)
    angle = 2 * np.pi / SIDE * (np.outer(pos // SIDE_IN, u) + np.outer(pos % SIDE_IN, v))
    tap = np.arange(KK)
    shift = 2 * np.pi / SIDE * (np.outer(PAD - tap // TAPS, u) + np.outer(PAD - tap % TAPS, v))
    weight = used * np.where(np.arange(2 * HALF) == 0, 1.0, 2.0) / SIDE ** 2

    def parts(re, im):
        n = re.shape[0]
        return np.stack([re.reshape(n, 2, HALF), im.reshape(n, 2, HALF)], 2).reshape(n, 4 * HALF)

    fwd = parts(np.cos(angle) * used, -np.sin(angle) * used)
    fwd = fwd.reshape(CHUNKS, P, 4 * HALF).transpose(1, 0, 2).reshape(P, -1)
    tapf = np.zeros((P, 4 * HALF))
    tapf[:KK] = parts(np.cos(shift) * used, -np.sin(shift) * used)
    inv = parts(np.cos(angle) * weight, -np.sin(angle) * weight)
    inv_t = np.zeros((P, 4 * HW))
    inv_t[:HALF] = inv.reshape(HW, 4, HALF).transpose(2, 1, 0).reshape(HALF, -1)
    return {"ident": ident, "group": group, "mean": mean, "before": before,
            "fwd": fwd, "tapf": tapf, "inv": inv_t}


WIDTHS = {"ident": P, "group": P, "mean": P, "before": P, "fwd": CHUNKS * 4 * HALF,
          "tapf": 4 * HALF, "inv": 4 * HW}
STARTS = dict(zip(WIDTHS, np.cumsum([0] + list(WIDTHS.values())).tolist()))
CONST_COLS = sum(WIDTHS.values())


def spread(ap, axis, n):
    ap = ap.unsqueeze(axis)
    shape = list(ap.shape)
    shape[axis] = n
    return ap.broadcast_to(shape)


def build(nc, a, out):
    ctx = ExitStack()

    def sb(name, shape, dt=F32):
        return ctx.enter_context(nc.sbuf_tensor(name, shape, dt))

    def sem(name):
        return ctx.enter_context(nc.semaphore(name))

    with ctx:
        rows_dram = nc.dram_tensor("rows_dram", (ROWS, ROW), F32, kind="Internal").ap()
        moe_dram = nc.dram_tensor("moe_dram", (2 * TOKENS, C), F32, kind="Internal").ap()

        const = sb("const", [P, CONST_COLS])

        def cst(name):
            return const[:, STARTS[name]:STARTS[name] + WIDTHS[name]]

        ident, group_avg, mean_all = cst("ident"), cst("group"), cst("mean")
        fwd = cst("fwd").rearrange("p (h r f) -> p h r f", h=CHUNKS, r=4)
        tapf = cst("tapf").rearrange("p (r f) -> p r f", r=4)
        inv = cst("inv").rearrange("p (r n) -> p r n", r=4)
        before = sb("before", [P, P], BF16)
        ones = sb("ones", [P, P], BF16)
        small = sb("small", [P, a["small"].shape[1]])
        kw_t, c0_t, c1_t = small[:, 0:KKP], small[:, 64:192], small[:, 192:320]
        router_w, ln_w, ln_b = small[:, 320:328], small[:, 328:377], small[:, 377:426]
        key_b, c0_b = small[:, 426:427], small[:, 427:428]
        c1_b = sb("c1_b", [KK, C])
        router_b = sb("router_b", [P, EXPERTS])
        w1t = sb("w1t", [P, 2, 2, C])
        wgv = sb("wgv", [P, 2, 2, 2 * HID])
        b1c = sb("b1c", [P, EXPERTS * 2])
        bgv = sb("bgv", [P, EXPERTS * 4])
        w_all = sb("w_all", [P, EXPERTS * 2 * HID])
        w2_all = sb("w2_all", [P, EXPERTS * 2 * C])
        b2 = sb("b2", [EXPERTS, C])

        xc = sb("xc", [P, 2, PAIR_TOKENS])
        xt = sb("xt", [P, PAIRS, TILES, C])
        gn_raw = sb("gn_raw", [P, 2, 2, 6])
        gn_mv = sb("gn_mv", [P, 2, 2, 2])
        gn_mean = sb("gn_mean", [P, 2, 2])
        gn_dev = sb("gn_dev", [P, 2])
        gn_sq = sb("gn_sq", [P, 2])
        gn_e2 = sb("gn_e2", [P, 2])
        gn_var = sb("gn_var", [P, 2])
        gn_rstd = sb("gn_rstd", [P, 2, 2])
        gbuf = sb("gbuf", [P, 2, PAIR_TOKENS])
        gt = sb("gt", [P, 2, CHUNKS, 2 * C])
        kmax = sb("kmax", [P, 1])
        ksum_b = sb("ksum_b", [P, 1])
        kshift = sb("kshift", [P, 1])
        kexp = sb("kexp", [P, HW])
        ktot = sb("ktot", [P, 1])
        krec = sb("krec", [P, 1])
        kprob = sb("kprob", [P, HW])
        pt = sb("pt", [P, CHUNKS, 2 * KKP])
        fraw = sb("fraw", [P, 2, 2, KK])
        f0 = sb("f0", [P, 2, KK])
        fsum = sb("fsum", [P, 2])
        fcen = sb("fcen", [P, 2, KK])
        fsq = sb("fsq", [P, 2, KK])
        fsqs = sb("fsqs", [P, 2])
        fvar = sb("fvar", [P, 2])
        frstd = sb("frstd", [P, 2])
        flw = sb("flw", [P, 2, KK])
        fln = sb("fln", [P, 2, KK])
        frelu = sb("frelu", [P, 2, KK])
        filt = sb("filt", [KK, 2, C])
        ghat = sb("ghat", [HALF, 2, 4, 2 * C])
        prod = sb("prod", [HALF, 2, 4, 2 * C])
        zhat = sb("zhat", [HALF, 4, 2 * C])
        t1 = sb("t1", [P, 2, TILES, C])
        ln_raw = sb("ln_raw", [P, TILES, 6])
        ln_mv = sb("ln_mv", [P, TILES, 2])
        ln_var = sb("ln_var", [P, TILES])
        ln_rstd = sb("ln_rstd", [P, TILES])
        z = sb("z", [P, TILES, C])
        qt = sb("qt", [P, PAIR_TOKENS])
        e_attn = sb("e_attn", [P, 2, CHUNKS, HW])
        asum = sb("asum", [P, 2, CHUNKS])
        arec = sb("arec", [P, 2, CHUNKS])
        t2 = sb("t2", [P, PAIRS, TILES, C])
        ln2_raw = sb("ln2_raw", [P, TILES, 6])
        ln2_mv = sb("ln2_mv", [P, TILES, 2])
        ln2_var = sb("ln2_var", [P, TILES])
        ln2_rstd = sb("ln2_rstd", [P, TILES])
        row = sb("row", [P, 2, TILES, 2, ROW])
        z2t = sb("z2t", [P, PAIR_TOKENS])
        minus_half = sb("minus_half", [P, TILES])

        iota8 = sb("iota8", [P, EXPERTS])
        dest = sb("dest", [P, PAIRS, TILES, 2], U32)
        logits = sb("logits", [P, TILES, EXPERTS])
        sorted8 = sb("sorted8", [P, TILES, 8])
        index8 = sb("index8", [P, TILES, 8], U32)
        lshift = sb("lshift", [P, TILES, 8])
        lexp = sb("lexp", [P, TILES, 8])
        lsum = sb("lsum", [P, TILES])
        lrec = sb("lrec", [P, TILES])
        chosen = sb("chosen", [P, TILES, 2, EXPERTS])
        either = sb("either", [P, TILES, EXPERTS], BF16)
        base = sb("base", [P, 2, EXPERTS])
        pos = sb("pos", [P, TILES, EXPERTS])
        posk = sb("posk", [P, TILES, 2, EXPERTS])
        slotf = sb("slotf", [P, TILES * 2])
        slot = sb("slot", [P, 2, TILES * 2], U32)

        banks = [ctx.enter_context(nc.psum_tensor(f"bank{i}", [P, 512], F32)) for i in range(8)]
        bank_k, bank_t, bank_b, bank_o, bank_s0, bank_s1, bank_d0, bank_d1 = banks
        bank_s = (bank_s0, bank_s1)
        bank_d = (bank_d0, bank_d1)

        ld_x = [sem("ld_x0"), sem("ld_x1")]
        ld_c1 = sem("ld_c1")
        ld_c2 = sem("ld_c2")
        ld_w = [sem("ld_w0"), sem("ld_w1")]
        ld_b = sem("ld_b")
        const_ready = sem("const_ready")
        iota_ready = sem("iota_ready")
        gn_raw_done, gn_mv_done = sem("gn_raw_done"), sem("gn_mv_done")
        gn_avg, gn_dev_done, gn_sq_done, gn_e2_done = sem("gn_avg"), sem("gn_dev_done"), sem("gn_sq_done"), sem("gn_e2_done")
        gn_avg2, gn_var_done, gn_rstd_done = sem("gn_avg2"), sem("gn_var_done"), sem("gn_rstd_done")
        g_done, keys_done, gt_psum, gt_done = sem("g_done"), sem("keys_done"), sem("gt_psum"), sem("gt_done")
        kmax_done, kshift1, kshift_done, kexp_done = sem("kmax_done"), sem("kshift1"), sem("kshift_done"), sem("kexp_done")
        krec_done, kprob_done, pt_psum, pt_done = sem("krec_done"), sem("kprob_done"), sem("pt_psum"), sem("pt_done")
        fraw_psum, fraw_done = sem("fraw_psum"), sem("fraw_done")
        ghat_psum, ghat_done = sem("ghat_psum"), sem("ghat_done")
        wmul_psum, wmul_done = sem("wmul_psum"), sem("wmul_done")
        wbias_psum, wbias_done = sem("wbias_psum"), sem("wbias_done")
        conv0_psum, f0_done, fsum_done = sem("conv0_psum"), sem("f0_done"), sem("fsum_done")
        fmean_psum, fcen_done, fsq_done, fsqs_done = sem("fmean_psum"), sem("fcen_done"), sem("fsq_done"), sem("fsqs_done")
        fvar_psum, fvar_done, frstd_done = sem("fvar_psum"), sem("fvar_done"), sem("frstd_done")
        flw_done, fln_done, frelu_done = sem("flw_done"), sem("fln_done"), sem("frelu_done")
        filt_psum, filt_done = sem("filt_psum"), sem("filt_done")
        what_psum, prod_done, zhat_done = sem("what_psum"), sem("prod_done"), sem("zhat_done")
        conv_psum, t1_done = sem("conv_psum"), sem("t1_done")
        ln_raw_done, ln_mv_done, ln_var_done, ln_rstd_done = sem("ln_raw_done"), sem("ln_mv_done"), sem("ln_var_done"), sem("ln_rstd_done")
        z_done, zt_psum, qt_done = sem("z_done"), sem("zt_psum"), sem("qt_done")
        score_psum, e_done = sem("score_psum"), sem("e_done")
        arec_done, attn_psum, t2_done = sem("arec_done"), sem("attn_psum"), sem("t2_done")
        ln2_raw_done, ln2_mv_done, ln2_var_done, ln2_rstd_done = sem("ln2_raw_done"), sem("ln2_mv_done"), sem("ln2_var_done"), sem("ln2_rstd_done")
        z2_done, z2t_psum, z2t_done = sem("z2_done"), sem("z2t_psum"), sem("z2t_done")
        logit_psum, logits_done = sem("logit_psum"), sem("logits_done")
        sorted_done, index_done, lshift_done, lexp_done = sem("sorted_done"), sem("index_done"), sem("lshift_done"), sem("lexp_done")
        lsum_done, lrec_done, chosen_done, either_done = sem("lsum_done"), sem("lrec_done"), sem("chosen_done"), sem("either_done")
        rank_psum, pos_done, posk_done, row_done = sem("rank_psum"), sem("pos_done"), sem("posk_done"), sem("row_done")
        base_done, slotf_done = sem("base_done"), sem("slotf_done")
        sent = [sem("sent0"), sem("sent1")]
        stored = sem("stored")

        bias_col = sb("bias_col", [P, EXPERTS * 4])
        rounds = PAIRS + 3

        def stages(i):
            return [p if 0 <= p < PAIRS else None for p in (i, i - 1, i - 2, i - 3)]

        def products(dve, b, q):
            g = ghat[:, b % 2, 2 * q:2 * q + 2, :]
            w = bank_d[q][0:HALF, :].rearrange("p (r c) -> p r c", r=2)
            dve.wait_ge(ghat_done, 2 * b + q + 1)
            dve.wait_ge(what_psum, 2 * b + q + 1)
            if b >= 1:
                dve.wait_ge(conv_psum, b)
            dve.tensor_tensor(prod[:, q, 0:2, :], w, g, ALU.mult)
            dve.tensor_tensor(prod[:, q, 2, :], w[:, 0, :], g[:, 1, :], ALU.mult)
            dve.tensor_tensor(prod[:, q, 3, :], w[:, 1, :], g[:, 0, :], ALU.mult).then_inc(prod_done, 1)
            dve.wait_ge(prod_done, 2 * b + q + 1)
            dve.tensor_tensor(zhat[:, 2 * q, :], prod[:, q, 0, :], prod[:, q, 1, :], ALU.subtract)
            dve.tensor_tensor(zhat[:, 2 * q + 1, :], prod[:, q, 2, :], prod[:, q, 3, :], ALU.add).then_inc(zhat_done, 1)

        def route(dve, d):
            dve.wait_ge(logit_psum, d + 1)
            dve.tensor_tensor(logits[:, :, :], bank_b[:, 0:32].rearrange("p (t e) -> p t e", t=TILES),
                              spread(router_b[:, :], 1, TILES), ALU.add).then_inc(logits_done, 1)
            dve.wait_ge(logits_done, d + 1)
            for t in range(TILES):
                last = dve.max(sorted8[:, t, :], logits[:, t, :])
            last.then_inc(sorted_done, 1)
            dve.wait_ge(sorted_done, d + 1)
            for t in range(TILES):
                last = dve.max_index(index8[:, t, :], sorted8[:, t, :], logits[:, t, :])
            last.then_inc(index_done, 1)
            dve.tensor_tensor(lshift[:, :, :], sorted8[:, :, :], spread(sorted8[:, :, 0], 2, 8), ALU.subtract).then_inc(lshift_done, 1)
            dve.wait_ge(index_done, d + 1)
            for t in range(TILES):
                last = dve.tensor_tensor(chosen[:, t, :, :], spread(iota8[:, :], 1, 2),
                                         spread(index8[:, t, 0:2], 2, EXPERTS), ALU.is_equal)
            last.then_inc(chosen_done, 1)
            dve.wait_ge(chosen_done, d + 1)
            dve.tensor_tensor(either[:, :, :], chosen[:, :, 0, :], chosen[:, :, 1, :], ALU.add).then_inc(either_done, 1)
            dve.wait_ge(lexp_done, d + 1)
            dve.reduce_sum(lsum[:, :], lexp[:, :, :], AX.X).then_inc(lsum_done, 1)
            dve.wait_ge(lsum_done, d + 1)
            dve.reciprocal(lrec[:, :], lsum[:, :]).then_inc(lrec_done, 1)
            dve.wait_ge(lrec_done, d + 1)
            dve.tensor_tensor(row[:, d % 2, :, :, C], lexp[:, :, 0:2], spread(lrec[:, :], 2, 2), ALU.mult)
            dve.wait_ge(rank_psum, d + 1)
            if d == 0:
                dve.wait_ge(iota_ready, 2 + CHUNKS)
            else:
                dve.wait_ge(base_done, d)
            dve.tensor_tensor(base[:, (d + 1) % 2, :], base[:, d % 2, :], bank_b[:, 96:96 + EXPERTS], ALU.add).then_inc(base_done, 1)
            dve.tensor_tensor(pos[:, :, :], bank_b[:, 64:96].rearrange("p (t e) -> p t e", t=TILES),
                              spread(base[:, d % 2, :], 1, TILES), ALU.add).then_inc(pos_done, 1)
            dve.wait_ge(pos_done, d + 1)
            for k in range(2):
                last = dve.tensor_tensor(posk[:, :, k, :], chosen[:, :, k, :], pos[:, :, :], ALU.mult)
            last.then_inc(posk_done, 1)
            dve.wait_ge(posk_done, d + 1)
            dve.reduce_sum(slotf[:, :], posk[:, :, :, :].rearrange("p t k e -> p (t k) e"), AX.X).then_inc(slotf_done, 1)
            dve.wait_ge(slotf_done, d + 1)
            dve.tensor_copy(slot[:, d % 2, :], slotf[:, :]).then_inc(row_done, 1)

        with nc.Block() as block:
            @block.sync
            def _(sp):
                def load_x(p):
                    sp.dma_start(xc[:, p % 2, :].rearrange("c (b n) -> c b n", b=2),
                                 a["x"][2 * p:2 * p + 2].rearrange("b c n -> c b n")).then_inc(ld_x[p % 2], 16)

                def load_w(e):
                    sp.dma_start(wgv[:, e % 2, :, 0:HID],
                                 a["wg"][e].rearrange("(h p) f -> p h f", p=P)).then_inc(ld_w[e % 2], 16)
                    sp.dma_start(wgv[:, e % 2, :, HID:2 * HID],
                                 a["wv"][e].rearrange("(h p) f -> p h f", p=P)).then_inc(ld_w[e % 2], 16)
                    sp.dma_start(w1t[:, e % 2, :, :],
                                 a["w1t"][e].rearrange("(h p) d -> p h d", p=P)).then_inc(ld_w[e % 2], 16)

                load_x(0)
                sp.dma_start(const[:, 0:STARTS["fwd"]], a["const"][:, 0:STARTS["fwd"]]).then_inc(ld_c1, 16)
                sp.dma_start(small[:, :], a["small"]).then_inc(ld_c1, 16)
                load_x(1)
                load_w(0)
                sp.dma_start(const[:, STARTS["fwd"]:CONST_COLS], a["const"][:, STARTS["fwd"]:CONST_COLS]).then_inc(ld_c2, 16)
                sp.dma_start(xt[:, 0:2], a["xt"][:, 0:2]).then_inc(ld_c2, 16)
                load_w(1)
                sp.dma_start(xt[:, 2:PAIRS], a["xt"][:, 2:PAIRS]).then_inc(ld_c2, 16)
                sp.dma_start(w2_all[:, :], a["w2"]).then_inc(ld_b, 16)
                for p in range(2, PAIRS):
                    sp.wait_ge(g_done, p - 1)
                    load_x(p)
                    sp.wait_ge(wbias_psum, p - 1)
                    load_w(p)

            @block.gpsimd
            def _(pool):
                pool.memset(minus_half[:, :], -0.5)
                pool.memset(row[:, :, :, :, C:ROW], 0.0)
                pool.iota(iota8[:, :], pattern=[[1, EXPERTS]], base=0, channel_multiplier=0,
                          allow_small_or_imprecise_dtypes=True).then_inc(iota_ready, 1)
                pool.iota(base[:, 0, :], pattern=[[REGION, EXPERTS]], base=0, channel_multiplier=0,
                          allow_small_or_imprecise_dtypes=True).then_inc(iota_ready, 1)
                for h in range(CHUNKS):
                    pool.iota(dest[:, :, h * 2:h * 2 + 2, :],
                              pattern=[[PAIR_TOKENS, PAIRS], [HW, 2], [TOKENS, 2]],
                              base=h * P, channel_multiplier=1).then_inc(iota_ready, 1)
                pool.wait_ge(iota_ready, 2 + CHUNKS)

                for i in range(rounds):
                    n, pa, b, d = stages(i)
                    if d is not None:
                        pool.wait_ge(ln_var_done, d + 1)
                        pool.tensor_tensor(ln_rstd[:, :], ln_var[:, :], minus_half[:, :], ALU.pow).then_inc(ln_rstd_done, 1)
                    if b is not None:
                        pool.wait_ge(fvar_done, b + 1)
                        pool.tensor_tensor(frstd[:, :], fvar[:, :], minus_half[:, 0:2], ALU.pow).then_inc(frstd_done, 1)
                    if n is not None:
                        pool.wait_ge(gn_var_done, n + 1)
                        if n >= 2:
                            pool.wait_ge(g_done, n - 1)
                        pool.tensor_tensor(gn_rstd[:, n % 2, :], gn_var[:, :], minus_half[:, 0:2], ALU.pow).then_inc(gn_rstd_done, 1)
                    if d is not None:
                        pool.wait_ge(ln2_var_done, d + 1)
                        pool.tensor_tensor(ln2_rstd[:, :], ln2_var[:, :], minus_half[:, :], ALU.pow).then_inc(ln2_rstd_done, 1)
                        pool.wait_ge(row_done, d + 1)
                        for t in range(TILES):
                            for k in range(2):
                                pool.indirect_dma_start(
                                    rows_dram, bass.IndirectOffsetOnAxis(ap=slot[:, d % 2, 2 * t + k:2 * t + k + 1], axis=0),
                                    row[:, d % 2, t, k, :], None).then_inc(sent[d % 2], 16)

            @block.scalar
            def _(act):
                act.dma_start(c1_b[:, :], a["c1_b"].partition_broadcast(KK)).then_inc(ld_b, 16)
                act.dma_start(router_b[:, :], a["router_b"].partition_broadcast(P)).then_inc(ld_b, 16)
                act.dma_start(b1c[:, :], a["b1c"]).then_inc(ld_b, 16)
                act.dma_start(bgv[:, :], a["bgv"]).then_inc(ld_b, 16)
                act.dma_start(b2[:, :], a["b2"]).then_inc(ld_b, 16)
                for i in range(rounds):
                    n, pa, b, d = stages(i)
                    if pa is not None:
                        act.wait_ge(gt_psum, pa + 1)
                        if pa >= 2:
                            act.wait_ge(fraw_psum, pa - 1)
                            act.wait_ge(ghat_psum, 2 * (pa - 1))
                        act.activation(gt[:, pa % 2, :, :].rearrange("p h c -> p (h c)"), bank_t[:, :], ACT.Copy).then_inc(gt_done, 1)
                    if d is not None:
                        act.wait_ge(zt_psum, d + 1)
                        if d >= 1:
                            act.wait_ge(score_psum, 2 * d)
                        act.activation(qt[:, :], bank_t[:, :], ACT.Tanh).then_inc(qt_done, 1)
                    if n is not None:
                        act.wait_ge(wmul_psum, n + 1)
                        act.activation(w_all[:, n * 2 * HID:(n + 1) * 2 * HID], bank_d0[:, :], ACT.Copy).then_inc(wmul_done, 1)
                    if pa is not None:
                        act.wait_ge(kshift_done, pa + 1)
                        if pa >= 1:
                            act.wait_ge(kprob_done, pa)
                        act.activation(kexp[:, :], bank_k[:, 0:HW], ACT.Exp, bias=kshift[:, 0:1], accum_out=ktot[:, 0:1]).then_inc(kexp_done, 1)
                    if d is not None:
                        for s in range(2):
                            act.wait_ge(score_psum, 2 * d + s + 1)
                            if d >= 1 and s == 0:
                                act.wait_ge(attn_psum, d)
                                act.wait_ge(arec_done, d)
                            for h in range(CHUNKS):
                                act.activation(e_attn[:, s, h, :], bank_s[s][:, h * HW:(h + 1) * HW], ACT.Exp,
                                               scale=float(C) ** -0.5, accum_out=asum[:, s, h:h + 1]).then_inc(e_done, 1)
                    if pa is not None:
                        for q in range(2):
                            act.wait_ge(ghat_psum, 2 * pa + q + 1)
                            if pa >= 2 and q == 0:
                                act.wait_ge(prod_done, 2 * (pa - 1))
                            act.activation(ghat[:, pa % 2, 2 * q:2 * q + 2, :].rearrange("p r c -> p (r c)"),
                                           bank_s[q][0:HALF, :], ACT.Copy).then_inc(ghat_done, 1)
                    if d is not None:
                        act.wait_ge(z2t_psum, d + 1)
                        if d >= 1:
                            act.wait_ge(logit_psum, d)
                        act.activation(z2t[:, :], bank_t[:, :], ACT.Copy).then_inc(z2t_done, 1)
                        act.wait_ge(lshift_done, d + 1)
                        if d >= 1:
                            act.wait_ge(row_done, d)
                        act.activation(lexp[:, :, :].rearrange("p t e -> p (t e)"),
                                       lshift[:, :, :].rearrange("p t e -> p (t e)"), ACT.Exp).then_inc(lexp_done, 1)

            @block.vector
            def _(dve):
                dve.memset(ones[:, :], 1.0)
                dve.wait_ge(ld_c1, 32)
                dve.tensor_copy(before[:, :], cst("before")).then_inc(const_ready, 1)

                def layer_norm_stats(src, raw, mv, var, raw_done, mv_done, var_done, p):
                    for t in range(TILES):
                        last = dve.bn_stats(raw[:, t, :], src[:, t, :])
                    last.then_inc(raw_done, 1)
                    dve.wait_ge(raw_done, p + 1)
                    for t in range(TILES):
                        last = dve.bn_aggr(mv[:, t, :], raw[:, t, :])
                    last.then_inc(mv_done, 1)
                    dve.wait_ge(mv_done, p + 1)
                    dve.tensor_scalar(var[:, :], mv[:, :, 1], EPS, None, ALU.add).then_inc(var_done, 1)

                for i in range(rounds):
                    n, pa, b, d = stages(i)
                    if pa is not None:
                        dve.wait_ge(gn_rstd_done, pa + 1)
                        if pa >= 2:
                            dve.wait_ge(keys_done, pa - 1)
                            dve.wait_ge(gt_psum, pa - 1)
                        for s in range(2):
                            last = dve.tensor_scalar(gbuf[:, pa % 2, s * HW:(s + 1) * HW], xc[:, pa % 2, s * HW:(s + 1) * HW],
                                                     gn_mean[:, pa % 2, s:s + 1], gn_rstd[:, pa % 2, s:s + 1],
                                                     ALU.subtract, ALU.mult)
                        last.then_inc(g_done, 1)
                    if d is not None:
                        dve.wait_ge(t1_done, d + 1)
                        layer_norm_stats(t1[:, d % 2], ln_raw, ln_mv, ln_var, ln_raw_done, ln_mv_done, ln_var_done, d)
                    if b is not None:
                        dve.wait_ge(conv0_psum, b + 1)
                        dve.tensor_scalar(f0[:, :, :], bank_b[:, 0:2 * KK].rearrange("p (s k) -> p s k", s=2), c0_b, None, ALU.add).then_inc(f0_done, 1)
                        dve.wait_ge(f0_done, b + 1)
                        dve.reduce_sum(fsum[:, :], f0[:, :, :], AX.X).then_inc(fsum_done, 1)
                    if pa is not None:
                        dve.wait_ge(keys_done, pa + 1)
                        if pa >= 1:
                            dve.wait_ge(kexp_done, pa)
                        dve.reduce_max(kmax[:, :], bank_k[:, 0:HW], AX.X).then_inc(kmax_done, 1)
                        dve.wait_ge(kmax_done, pa + 1)
                        dve.tensor_tensor(ksum_b[:, :], kmax[:, :], key_b, ALU.add).then_inc(kshift1, 1)
                        dve.wait_ge(kshift1, pa + 1)
                        dve.tensor_tensor(kshift[:, :], key_b, ksum_b[:, :], ALU.subtract).then_inc(kshift_done, 1)
                    if d is not None:
                        dve.wait_ge(ln_rstd_done, d + 1)
                        if d >= 1:
                            dve.wait_ge(attn_psum, d)
                        for t in range(TILES):
                            last = dve.tensor_scalar(z[:, t, :], t1[:, d % 2, t, :], ln_mv[:, t, 0:1], ln_rstd[:, t:t + 1],
                                                     ALU.subtract, ALU.mult)
                        last.then_inc(z_done, 1)
                    if b is not None:
                        dve.wait_ge(fmean_psum, b + 1)
                        dve.tensor_tensor(fcen[:, :, :], f0[:, :, :], spread(bank_b[:, 128:130], 2, KK), ALU.subtract).then_inc(fcen_done, 1)
                        dve.wait_ge(fcen_done, b + 1)
                        dve.tensor_tensor(fsq[:, :, :], fcen[:, :, :], fcen[:, :, :], ALU.mult).then_inc(fsq_done, 1)
                        dve.tensor_tensor(flw[:, :, :], fcen[:, :, :], spread(ln_w, 1, 2), ALU.mult).then_inc(flw_done, 1)
                        dve.wait_ge(fsq_done, b + 1)
                        dve.reduce_sum(fsqs[:, :], fsq[:, :, :], AX.X).then_inc(fsqs_done, 1)
                    if n is not None:
                        dve.wait_ge(ld_x[n % 2], 16 * (n // 2 + 1))
                        for s in range(2):
                            last = dve.bn_stats(gn_raw[:, n % 2, s, :], xc[:, n % 2, s * HW:(s + 1) * HW])
                        last.then_inc(gn_raw_done, 1)
                        dve.wait_ge(gn_raw_done, n + 1)
                        for s in range(2):
                            last = dve.bn_aggr(gn_mv[:, n % 2, s, :], gn_raw[:, n % 2, s, :])
                        last.then_inc(gn_mv_done, 1)
                    if pa is not None:
                        dve.wait_ge(kexp_done, pa + 1)
                        dve.reciprocal(krec[:, :], ktot[:, :]).then_inc(krec_done, 1)
                        dve.wait_ge(krec_done, pa + 1)
                        if pa >= 1:
                            dve.wait_ge(pt_psum, pa)
                        dve.tensor_scalar(kprob[:, :], kexp[:, :], krec[:, 0:1], None, ALU.mult).then_inc(kprob_done, 1)
                    if b is not None:
                        dve.wait_ge(fvar_psum, b + 1)
                        dve.tensor_scalar(fvar[:, :], bank_b[:, 132:134], EPS, None, ALU.add).then_inc(fvar_done, 1)
                    if n is not None:
                        dve.wait_ge(gn_avg, n + 1)
                        dve.tensor_copy(gn_mean[:, n % 2, :], bank_d1[:, 0:2])
                        dve.tensor_tensor(gn_dev[:, :], gn_mv[:, n % 2, :, 0], bank_d1[:, 0:2], ALU.subtract).then_inc(gn_dev_done, 1)
                        dve.wait_ge(gn_dev_done, n + 1)
                        dve.tensor_tensor(gn_sq[:, :], gn_dev[:, :], gn_dev[:, :], ALU.mult).then_inc(gn_sq_done, 1)
                        dve.wait_ge(gn_sq_done, n + 1)
                        dve.tensor_tensor(gn_e2[:, :], gn_sq[:, :], gn_mv[:, n % 2, :, 1], ALU.add).then_inc(gn_e2_done, 1)
                    if pa is not None:
                        dve.wait_ge(pt_psum, pa + 1)
                        if pa >= 1:
                            dve.wait_ge(fraw_psum, pa)
                        dve.tensor_copy(pt[:, :, :].rearrange("p h k -> p (h k)"), bank_k[:, HW:2 * HW]).then_inc(pt_done, 1)
                    if n is not None:
                        dve.wait_ge(gn_avg2, n + 1)
                        dve.tensor_scalar(gn_var[:, :], bank_d1[:, 4:6], EPS, None, ALU.add).then_inc(gn_var_done, 1)
                    if b is not None:
                        dve.wait_ge(frstd_done, b + 1)
                        dve.wait_ge(flw_done, b + 1)
                        for s in range(2):
                            last = dve.scalar_tensor_tensor(fln[:, s, :], flw[:, s, :], frstd[:, s:s + 1], ln_b, ALU.mult, ALU.add)
                        last.then_inc(fln_done, 1)
                        dve.wait_ge(fln_done, b + 1)
                        dve.tensor_scalar(frelu[:, :, :], fln[:, :, :], 0.0, None, ALU.max).then_inc(frelu_done, 1)
                    if pa is not None:
                        dve.wait_ge(fraw_psum, pa + 1)
                        if pa >= 2:
                            dve.wait_ge(conv0_psum, pa - 1)
                        dve.tensor_copy(fraw[:, pa % 2, :, :], bank_k[:, 0:2 * KKP].rearrange("p (s k) -> p s k", s=2)[:, :, 0:KK]).then_inc(fraw_done, 1)
                    if n is not None:
                        dve.wait_ge(wbias_psum, n + 1)
                        if n == 0:
                            dve.wait_ge(ld_b, 96)
                        dve.tensor_tensor(bias_col[:, 4 * n:4 * n + 4], bank_d1[:, 8:12], bgv[:, 4 * n:4 * n + 4], ALU.add).then_inc(wbias_done, 1)
                    if b is not None:
                        dve.wait_ge(filt_psum, b + 1)
                        if b >= 1:
                            dve.wait_ge(what_psum, 2 * b)
                        dve.tensor_tensor(filt[:, :, :], bank_b[0:KK, 256:512].rearrange("k (s c) -> k s c", s=2),
                                          spread(c1_b[:, :], 1, 2), ALU.add).then_inc(filt_done, 1)
                    if d is not None:
                        dve.wait_ge(e_done, 4 * (d + 1))
                        dve.reciprocal(arec[:, :, :], asum[:, :, :]).then_inc(arec_done, 1)
                        dve.wait_ge(arec_done, d + 1)
                        dve.wait_ge(attn_psum, d + 1)
                        for t in range(TILES):
                            h, s = divmod(t, 2)
                            last = dve.scalar_tensor_tensor(t2[:, d, t, :], bank_o[:, t * C:(t + 1) * C], arec[:, s, h:h + 1],
                                                            t1[:, d % 2, t, :], ALU.mult, ALU.add)
                        last.then_inc(t2_done, 1)
                        dve.wait_ge(t2_done, d + 1)
                        layer_norm_stats(t2[:, d], ln2_raw, ln2_mv, ln2_var, ln2_raw_done, ln2_mv_done, ln2_var_done, d)
                    if b is not None:
                        products(dve, b, 0)
                    if d is not None:
                        dve.wait_ge(ln2_rstd_done, d + 1)
                        if d >= 2:
                            dve.wait_ge(sent[d % 2], 16 * 8 * (d // 2))
                        for t in range(TILES):
                            last = dve.tensor_scalar(row[:, d % 2, t, 0, 0:C], t2[:, d, t, :], ln2_mv[:, t, 0:1], ln2_rstd[:, t:t + 1],
                                                     ALU.subtract, ALU.mult)
                        last.then_inc(z2_done, 1)
                    if b is not None:
                        products(dve, b, 1)
                    if d is not None:
                        dve.wait_ge(z2_done, d + 1)
                        dve.tensor_copy(row[:, d % 2, :, 1, 0:C], row[:, d % 2, :, 0, 0:C])
                        if d == 0:
                            dve.wait_ge(iota_ready, 2 + CHUNKS)
                        dve.tensor_copy(row[:, d % 2, :, :, C + 1:C + 2].bitcast(U32), dest[:, d, :, :].rearrange("p t (k o) -> p t k o", o=1))
                    if d is not None:
                        route(dve, d)
                    if b is not None:
                        dve.wait_ge(conv_psum, b + 1)
                        if b >= 2:
                            dve.wait_ge(t2_done, b - 1)
                        if b == 0:
                            dve.wait_ge(ld_c2, 48)
                        dve.tensor_tensor(t1[:, b % 2, :, :].rearrange("p t c -> p (t c)"), bank_o[:, :],
                                          xt[:, b, :, :].rearrange("p t c -> p (t c)"), ALU.add).then_inc(t1_done, 1)

            @block.tensor
            def _(pe):
                pe.wait_ge(ld_c1, 32)
                pe.wait_ge(const_ready, 1)
                for i in range(rounds):
                    n, pa, b, d = stages(i)
                    if pa is not None:
                        pe.wait_ge(g_done, pa + 1)
                        if pa >= 3:
                            pe.wait_ge(z2t_done, pa - 2)
                        elif pa >= 1:
                            pe.wait_ge(gt_done, pa)
                        for h in range(CHUNKS):
                            for s in range(2):
                                last = pe.transpose(bank_t[:, h * 2 * C + s * C:h * 2 * C + (s + 1) * C],
                                                    gbuf[:, pa % 2, s * HW + h * P:s * HW + (h + 1) * P], ident)
                        last.then_inc(gt_psum, 1)
                        if pa >= 1:
                            pe.wait_ge(fraw_done, pa)
                        for s in range(2):
                            last = pe.matmul(bank_k[s * KKP:(s + 1) * KKP, 0:HW], kw_t, gbuf[:, pa % 2, s * HW:(s + 1) * HW], start=True, stop=True)
                        last.then_inc(keys_done, 1)
                    if b is not None:
                        pe.wait_ge(fraw_done, b + 1)
                        if i - 4 >= 0:
                            pe.wait_ge(pos_done, i - 3)
                        if b >= 1:
                            pe.wait_ge(filt_done, b)
                        pe.matmul(bank_b[:, 0:2 * KK], c0_t, fraw[:, b % 2, :, :].rearrange("p s k -> p (s k)"), start=True, stop=True).then_inc(conv0_psum, 1)
                    if n is not None:
                        pe.wait_ge(ld_w[n % 2], 48 * (n // 2 + 1))
                        if i >= 3:
                            pe.wait_ge(prod_done, 2 * (i - 2))
                        if n >= 1:
                            pe.wait_ge(wmul_done, n)
                        for h in range(2):
                            last = pe.matmul(bank_d0[:, :], w1t[:, n % 2, h, :], wgv[:, n % 2, h, :], start=(h == 0), stop=(h == 1))
                        last.then_inc(wmul_psum, 1)
                    if d is not None:
                        pe.wait_ge(z_done, d + 1)
                        if pa is not None:
                            pe.wait_ge(gt_done, pa + 1)
                        if pa is None and d >= 1:
                            pe.wait_ge(z2t_done, d)
                        for t in range(TILES):
                            h, s = divmod(t, 2)
                            last = pe.transpose(bank_t[:, s * HW + h * P:s * HW + (h + 1) * P], z[:, t, :], ident)
                        last.then_inc(zt_psum, 1)
                    if b is not None:
                        pe.wait_ge(fsum_done, b + 1)
                        pe.matmul(bank_b[:, 128:130], mean_all, fsum[:, :], start=True, stop=True).then_inc(fmean_psum, 1)
                    if n is not None:
                        pe.wait_ge(gn_mv_done, n + 1)
                        if n >= 1:
                            pe.wait_ge(wbias_done, n)
                        if i >= 3:
                            pe.wait_ge(prod_done, 2 * (i - 2))
                        pe.matmul(bank_d1[:, 0:2], group_avg, gn_mv[:, n % 2, :, 0], start=True, stop=True).then_inc(gn_avg, 1)
                    if d is not None:
                        pe.wait_ge(qt_done, d + 1)
                        pe.wait_ge(ghat_done, 2 * min(i - 1, PAIRS))
                        if d >= 1:
                            pe.wait_ge(e_done, 4 * d)
                        for s in range(2):
                            for h in range(CHUNKS):
                                last = pe.matmul(bank_s[s][:, h * HW:(h + 1) * HW], qt[:, s * HW + h * P:s * HW + (h + 1) * P],
                                                 qt[:, s * HW:(s + 1) * HW], start=True, stop=True)
                            last.then_inc(score_psum, 1)
                    if b is not None:
                        pe.wait_ge(fsqs_done, b + 1)
                        pe.matmul(bank_b[:, 132:134], mean_all, fsqs[:, :], start=True, stop=True).then_inc(fvar_psum, 1)
                    if n is not None:
                        pe.wait_ge(gn_e2_done, n + 1)
                        pe.matmul(bank_d1[:, 4:6], group_avg, gn_e2[:, :], start=True, stop=True).then_inc(gn_avg2, 1)
                    if pa is not None:
                        pe.wait_ge(kprob_done, pa + 1)
                        for h in range(CHUNKS):
                            last = pe.transpose(bank_k[:, HW + h * P:HW + (h + 1) * P], kprob[:, h * P:(h + 1) * P], ident)
                        last.then_inc(pt_psum, 1)
                    if d is not None:
                        pe.wait_ge(e_done, 4 * (d + 1))
                        pe.wait_ge(t1_done, min(i - 2, PAIRS))
                        for h in range(CHUNKS):
                            for s in range(2):
                                for k in range(CHUNKS):
                                    last = pe.matmul(bank_o[:, (h * 2 + s) * C:(h * 2 + s + 1) * C], e_attn[:, s, k, h * P:(h + 1) * P],
                                                     z[:, k * 2 + s, :], start=(k == 0), stop=(k == CHUNKS - 1))
                        last.then_inc(attn_psum, 1)
                    if n is not None:
                        pe.wait_ge(gn_var_done, n + 1)
                        if n == 0:
                            pe.wait_ge(ld_b, 96)
                        for q in range(4):
                            for h in range(2):
                                last = pe.matmul(bank_d1[:, 8 + q:9 + q], wgv[:, n % 2, h, q * P:(q + 1) * P], b1c[:, 2 * n + h:2 * n + h + 1],
                                                 start=(h == 0), stop=(h == 1))
                        last.then_inc(wbias_psum, 1)
                    if b is not None:
                        pe.wait_ge(frelu_done, b + 1)
                        for s in range(2):
                            last = pe.matmul(bank_b[0:KK, 256 + s * C:256 + (s + 1) * C], frelu[:, s, :], c1_t, start=True, stop=True)
                        last.then_inc(filt_psum, 1)
                    if pa is not None:
                        pe.wait_ge(pt_done, pa + 1)
                        pe.wait_ge(gt_done, pa + 1)
                        for s in range(2):
                            for h in range(CHUNKS):
                                last = pe.matmul(bank_k[:, s * KKP:(s + 1) * KKP], gt[:, pa % 2, h, s * C:(s + 1) * C],
                                                 pt[:, h, s * KKP:(s + 1) * KKP], start=(h == 0), stop=(h == CHUNKS - 1))
                        last.then_inc(fraw_psum, 1)
                    if b is not None:
                        pe.wait_ge(filt_done, b + 1)
                        if b == 0:
                            pe.wait_ge(ld_c2, 48)
                        pe.wait_ge(wmul_done, min(i + 1, PAIRS))
                        pe.wait_ge(wbias_done, min(i + 1, PAIRS))
                        if b >= 1:
                            pe.wait_ge(prod_done, 2 * b)
                        for q in range(2):
                            for r in range(2):
                                last = pe.matmul(bank_d[q][0:HALF, r * 2 * C:(r + 1) * 2 * C], tapf[0:KK, 2 * q + r, :],
                                                 filt[:, :, :].rearrange("k s c -> k (s c)"), start=True, stop=True)
                            last.then_inc(what_psum, 1)
                    if pa is not None:
                        if pa == 0:
                            pe.wait_ge(ld_c2, 48)
                        for q in range(2):
                            if d is not None:
                                pe.wait_ge(e_done, 4 * d + 2 * (q + 1))
                            elif pa >= 1:
                                pe.wait_ge(ghat_done, 2 * (pa - 1) + q + 1)
                            for r in range(2):
                                for h in range(CHUNKS):
                                    last = pe.matmul(bank_s[q][0:HALF, r * 2 * C:(r + 1) * 2 * C], fwd[:, h, 2 * q + r, :],
                                                     gt[:, pa % 2, h, :], start=(h == 0), stop=(h == CHUNKS - 1))
                            last.then_inc(ghat_psum, 1)
                    if d is not None:
                        pe.wait_ge(z2_done, d + 1)
                        pe.wait_ge(qt_done, d + 1)
                        for t in range(TILES):
                            last = pe.transpose(bank_t[:, t * P:(t + 1) * P], row[:, d % 2, t, 0, 0:C], ident)
                        last.then_inc(z2t_psum, 1)
                    if b is not None:
                        pe.wait_ge(zhat_done, 2 * (b + 1))
                        if d is not None:
                            pe.wait_ge(t2_done, d + 1)
                        elif b >= 1:
                            pe.wait_ge(t1_done, b)
                        for h in range(CHUNKS):
                            for r in range(4):
                                last = pe.matmul(bank_o[:, h * 2 * C:(h + 1) * 2 * C], inv[0:HALF, r, h * P:(h + 1) * P],
                                                 zhat[:, r, :], start=(r == 0), stop=(r == 3))
                        last.then_inc(conv_psum, 1)
                    if d is not None:
                        pe.wait_ge(z2t_done, d + 1)
                        pe.wait_ge(filt_done, min(i - 1, PAIRS))
                        if d >= 1:
                            pe.wait_ge(pos_done, d)
                        for t in range(TILES):
                            last = pe.matmul(bank_b[:, t * EXPERTS:(t + 1) * EXPERTS], z2t[:, t * P:(t + 1) * P], router_w, start=True, stop=True)
                        last.then_inc(logit_psum, 1)
                        pe.wait_ge(either_done, d + 1)
                        for t in range(TILES):
                            for u in range(t):
                                pe.matmul(bank_b[:, 64 + t * EXPERTS:64 + (t + 1) * EXPERTS], ones[:, :], either[:, u, :], start=(u == 0), stop=False)
                            pe.matmul(bank_b[:, 64 + t * EXPERTS:64 + (t + 1) * EXPERTS], before[:, :], either[:, t, :], start=(t == 0), stop=True)
                        for u in range(TILES):
                            last = pe.matmul(bank_b[:, 96:96 + EXPERTS], ones[:, :], either[:, u, :], start=(u == 0), stop=(u == TILES - 1))
                        last.then_inc(rank_psum, 1)

        experts(nc, ctx, sb, sem, a, out, dict(
            rows_dram=rows_dram, moe_dram=moe_dram, ident=ident, ones=ones, iota8=iota8, base=base, bias_col=bias_col,
            b2=b2, w_all=w_all, w2_all=w2_all, t2=t2, first=xt, banks=banks, sent=sent, ld_b=ld_b))


def experts(nc, ctx, sb, sem, a, out, g):
    rows_dram, moe_dram, ident, ones, banks = g["rows_dram"], g["moe_dram"], g["ident"], g["ones"], g["banks"]
    iota8, base, w_all, w2_all, t2, y_first = g["iota8"], g["base"], g["w_all"], g["w2_all"], g["t2"], g["first"]
    bias_col, b2 = g["bias_col"], g["b2"]
    E, NB, U = EXPERTS, BLOCKS, UNROLL
    NTHR = TOKENS // P
    ZERO = EXPERTS * REGION

    region = sb("region", [P, E])
    threshold = sb("threshold", [P, NTHR])
    block_no = sb("block_no", [P, NB])
    channel = sb("channel", [P, 1])
    count = sb("count", [P, E])
    more = sb("more", [P, E, NTHR])
    nblk = sb("nblk", [P, E])
    upto = sb("upto", [P, E, E])
    cumt = sb("cumt", [P, E, E])
    cum = sb("cum", [P, E])
    cum_before = sb("cum_before", [P, E])
    offset = sb("offset", [P, E])
    past = sb("past", [P, NB, E])
    expert = sb("expert", [P, NB])
    mine = sb("mine", [P, NB, E])
    used = sb("used", [P, NB])
    offs = sb("offs", [P, NB, E])
    start = sb("start", [P, NB])
    jz = sb("jz", [P, NB])
    ujz = sb("ujz", [P, NB])
    start2 = sb("start2", [P, NB])
    table = sb("table", [P, 2, NB], I32)
    pad_at = sb("pad_at", [P, E], U32)
    pad_row = sb("pad_row", [P, ROW])

    def parts_of(name, rows):
        return [sb(f"{name}_full", [rows, P]), sb(f"{name}_rest", [rows, 2, P]), sb(f"{name}_part", [rows, 3, P], BF16)]

    bias_full, bias_rest, bias_part = parts_of("bias", 4 * E)
    _, b2_rest, b2_part = parts_of("b2", E)
    bias_rows = sb("bias_rows", [3, E * 2 * HID], BF16)
    b2_rows = sb("b2_rows", [3, E * C], BF16)

    xs = sb("xs", [P, U, ROW])
    xst = sb("xst", [P, 2, P])
    silu = sb("silu", [P, 2, HID])
    gated = sb("gated", [P, 2, HID])
    gatedt = sb("gatedt", [P, 2, HID])
    ys = sb("ys", [P, U, C])
    y_second = sb("y_second", [P, PAIRS, TILES, C])
    bank_x, bank_h, bank_g, bank_y = banks[0:2], banks[2:4], banks[4:6], banks[6:8]

    names = ("consts table_step table_ready pads_sent bias_psum bias_ready bias_sent chain "
             "xst_psum xst_done h_psum silu_done gated_done gt_psum gt_done y_psum ys_done "
             "sending sum1_done sum_done stored").split()
    S = {n: sem("moe_" + n) for n in names}
    xs_loaded = [sem(f"moe_xs_loaded{u}") for u in range(U)]
    ys_sent = [sem(f"moe_ys_sent{u}") for u in range(U)]
    y_loaded = [sem(f"moe_y_loaded{p}") for p in range(PAIRS)]

    def over_blocks(eng, step):
        turns = NB // U
        for u in range(U):
            step(u, u, 0, True, False)
        with eng.Fori(1, turns - 1) as it:
            for u in range(U):
                step(it * U + u, u, it, False, False)
        for u in range(U):
            step((turns - 1) * U + u, u, turns - 1, False, True)

    with nc.Block() as block:
        @block.gpsimd
        def _(pool):
            pool.memset(pad_row[:, :], 0.0)
            pool.iota(region[:, :], pattern=[[REGION, E]], base=0, channel_multiplier=0, allow_small_or_imprecise_dtypes=True)
            pool.iota(threshold[:, :], pattern=[[P, NTHR]], base=0, channel_multiplier=0, allow_small_or_imprecise_dtypes=True)
            pool.iota(block_no[:, :], pattern=[[1, NB]], base=0, channel_multiplier=0, allow_small_or_imprecise_dtypes=True)
            pool.iota(jz[:, :], pattern=[[P, NB]], base=-ZERO, channel_multiplier=0, allow_small_or_imprecise_dtypes=True)
            pool.iota(channel[:, :], pattern=[[0, 1]], base=0, channel_multiplier=1, allow_small_or_imprecise_dtypes=True).then_inc(S["consts"], 1)
            pool.wait_ge(S["consts"], 1)
            pool.iota(pad_row[:, C + 1:C + 2].bitcast(U32), pattern=[[0, 1]], base=SKIP, channel_multiplier=0).then_inc(S["consts"], 1)
            pool.wait_ge(S["consts"], 2)
            pool.dma_start(rows_dram[ZERO:ZERO + P, :], pad_row[:, :]).then_inc(S["pads_sent"], 16)
            pool.wait_ge(S["table_ready"], 1)
            for e in range(E):
                pool.indirect_dma_start(rows_dram, bass.IndirectOffsetOnAxis(ap=pad_at[:, e:e + 1], axis=0),
                                        pad_row[:, :], None).then_inc(S["pads_sent"], 16)

            def send(j, u, it, first, last):
                pool.wait_ge(S["ys_done"], j + 1)
                pool.sem_inc(S["sending"], 1)
                pool.indirect_dma_start(moe_dram, bass.IndirectOffsetOnAxis(ap=xs[:, u, C + 1:C + 2].bitcast(U32), axis=0),
                                        ys[:, u, :], None, bounds_check=2 * TOKENS - 1, oob_is_err=False).then_inc(ys_sent[u], 16)

            over_blocks(pool, send)

        @block.sync
        def _(sp):
            for s in range(2):
                sp.wait_ge(g["sent"][s], 16 * 2 * TILES * (PAIRS // 2))
            sp.wait_ge(S["pads_sent"], 16 * (E + 1))
            sp.wait_ge(S["table_ready"], 2)

            def load(j, u, it, first, last):
                if not first:
                    sp.wait_ge(ys_sent[u], 16 * it)
                row0 = sp.value_load(table[0:1, 0, bass.ds(j, 1)], min_val=0, max_val=ZERO)
                sp.dma_start(xs[:, u, :], rows_dram[bass.ds(row0, P), :]).then_inc(xs_loaded[u], 16)

            over_blocks(sp, load)
            for u in range(U):
                sp.wait_ge(ys_sent[u], 16 * (NB // U))
            halves = moe_dram.rearrange("(k p b h n) c -> k p n h b c", k=2, b=2, h=CHUNKS, n=P)
            for p in range(PAIRS):
                for k, dst in ((0, y_first), (1, y_second)):
                    for h in range(CHUNKS):
                        sp.dma_start(dst[:, p, 2 * h:2 * h + 2, :], halves[k, p, :, h]).then_inc(y_loaded[p], 16)
            outs = out.rearrange("(p b h n) c -> p n h b c", b=2, h=CHUNKS, n=P)
            for p in range(PAIRS):
                sp.wait_ge(S["sum_done"], p + 1)
                for h in range(CHUNKS):
                    sp.dma_start(outs[p, :, h], y_second[:, p, 2 * h:2 * h + 2, :]).then_inc(S["stored"], 16)
            sp.wait_ge(S["stored"], 16 * CHUNKS * PAIRS)

        @block.scalar
        def _(act):
            act.wait_ge(S["bias_ready"], 2)
            for k in range(3):
                act.dma_start(bias_rows[k:k + 1, :].rearrange("o (r f) -> o r f", f=P), bias_part[:, k, :]).then_inc(S["bias_sent"], 16)
                act.dma_start(b2_rows[k:k + 1, :].rearrange("o (r f) -> o r f", f=P), b2_part[:, k, :]).then_inc(S["bias_sent"], 16)

            def xst_copy(j, v, first):
                act.wait_ge(S["xst_psum"], j + 1)
                if not first:
                    act.wait_ge(S["h_psum"], j - 1)
                act.activation(xst[:, v, :], bank_x[v][:, 0:P], ACT.Copy).then_inc(S["xst_done"], 1)

            def step(j, u, it, first, last):
                if first and u == 0:
                    xst_copy(0, 0, True)
                if not (last and u == U - 1):
                    xst_copy(j + 1, (u + 1) % 2, first and u < 1)
                act.wait_ge(S["h_psum"], j + 1)
                if not (first and u < 2):
                    act.wait_ge(S["gated_done"], j - 1)
                act.activation(silu[:, u % 2, :], bank_h[u % 2][:, 0:HID], ACT.Silu).then_inc(S["silu_done"], 1)

            over_blocks(act, step)

        @block.vector
        def _(dve):
            n = [0]

            def then(instruction):
                n[0] += 1
                instruction.then_inc(S["chain"], 1)
                dve.wait_ge(S["chain"], n[0])

            dve.wait_ge(S["consts"], 1)
            then(dve.tensor_tensor(count[:, :], base[:, 0, :], region[:, :], ALU.subtract))
            dve.tensor_scalar(pad_at[:, :], base[:, 0, :], channel[:, 0:1], None, ALU.add).then_inc(S["table_ready"], 1)
            then(dve.tensor_tensor(more[:, :, :], spread(count[:, :], 2, NTHR), spread(threshold[:, :], 1, E), ALU.is_gt))
            then(dve.reduce_sum(nblk[:, :], more[:, :, :], AX.X))
            then(dve.tensor_tensor(upto[:, :, :], spread(iota8[:, :], 2, E), spread(iota8[:, :], 1, E), ALU.is_ge))
            then(dve.tensor_tensor(cumt[:, :, :], upto[:, :, :], spread(nblk[:, :], 1, E), ALU.mult))
            then(dve.reduce_sum(cum[:, :], cumt[:, :, :], AX.X))
            then(dve.tensor_tensor(cum_before[:, :], cum[:, :], nblk[:, :], ALU.subtract))
            then(dve.scalar_tensor_tensor(offset[:, :], cum_before[:, :], -float(P), region[:, :], ALU.mult, ALU.add))
            then(dve.tensor_tensor(past[:, :, :], spread(block_no[:, :], 2, E), spread(cum[:, :], 1, NB), ALU.is_ge))
            then(dve.reduce_sum(expert[:, :], past[:, :, :], AX.X))
            then(dve.tensor_tensor(mine[:, :, :], spread(expert[:, :], 2, E), spread(iota8[:, :], 1, NB), ALU.is_equal))
            then(dve.reduce_sum(used[:, :], mine[:, :, :], AX.X))
            then(dve.tensor_tensor(offs[:, :, :], mine[:, :, :], spread(offset[:, :], 1, NB), ALU.mult))
            then(dve.reduce_sum(start[:, :], offs[:, :, :], AX.X))
            then(dve.tensor_tensor(ujz[:, :], used[:, :], jz[:, :], ALU.mult))
            then(dve.tensor_tensor(start2[:, :], start[:, :], ujz[:, :], ALU.add))
            dve.tensor_scalar(table[:, 0, :], start2[:, :], float(ZERO), None, ALU.add)
            dve.tensor_scalar(table[:, 1, :], expert[:, :], float(E - 1), None, ALU.min).then_inc(S["table_ready"], 1)

            for full, rest, part in ((bias_full, bias_rest, bias_part), (b2, b2_rest, b2_part)):
                if full is bias_full:
                    dve.wait_ge(S["bias_psum"], 1)
                    then(dve.tensor_copy(full[:, :], bank_x[0][0:4 * E, 0:P]))
                then(dve.tensor_copy(part[:, 0, :], full[:, :]))
                then(dve.tensor_tensor(rest[:, 0, :], full[:, :], part[:, 0, :], ALU.subtract))
                then(dve.tensor_copy(part[:, 1, :], rest[:, 0, :]))
                then(dve.tensor_tensor(rest[:, 1, :], rest[:, 0, :], part[:, 1, :], ALU.subtract))
                dve.tensor_copy(part[:, 2, :], rest[:, 1, :]).then_inc(S["bias_ready"], 1)

            def gatedt_copy(j, v, early):
                dve.wait_ge(S["gt_psum"], j + 1)
                if not early:
                    dve.wait_ge(S["y_psum"], j - 1)
                dve.tensor_copy(gatedt[:, v, :], bank_g[v][:, 0:HID]).then_inc(S["gt_done"], 1)

            def scale(j, u, it, early, first_use):
                dve.wait_ge(S["y_psum"], j + 1)
                if not first_use:
                    dve.wait_ge(ys_sent[u], 16 * it)
                dve.tensor_scalar(ys[:, u, :], bank_y[u % 2][:, 0:C], xs[:, u, C:C + 1], None, ALU.mult).then_inc(S["ys_done"], 1)

            def step(j, u, it, first, last):
                if not (first and u < 1):
                    gatedt_copy(j - 1, (u - 1) % 2, first and u < 3)
                dve.wait_ge(S["silu_done"], j + 1)
                if not (first and u < 2):
                    dve.wait_ge(S["gt_psum"], j - 1)
                dve.tensor_tensor(gated[:, u % 2, :], bank_h[u % 2][:, HID:2 * HID], silu[:, u % 2, :], ALU.mult).then_inc(S["gated_done"], 1)
                if not (first and u < 2):
                    scale(j - 2, (u - 2) % U, it if u >= 2 else it - 1, False, first or (it == 1 if isinstance(it, int) else False) and u < 2)

            turns = NB // U

            def steps(it, first, last):
                for u in range(U):
                    step(it * U + u, u, it, first, last)

            steps(0, True, False)
            steps(1, False, False)
            with dve.Fori(2, turns - 1) as it:
                steps(it, False, False)
            steps(turns - 1, False, True)
            gatedt_copy(NB - 1, 1, False)
            scale(NB - 2, U - 2, turns - 1, False, False)
            scale(NB - 1, U - 1, turns - 1, False, False)

            for p in range(PAIRS):
                dve.wait_ge(y_loaded[p], 16 * 2 * CHUNKS)
                dve.tensor_tensor(t2[:, p, :, :], t2[:, p, :, :], y_first[:, p, :, :], ALU.add).then_inc(S["sum1_done"], 1)
                dve.wait_ge(S["sum1_done"], p + 1)
                dve.tensor_tensor(y_second[:, p, :, :], t2[:, p, :, :], y_second[:, p, :, :], ALU.add).then_inc(S["sum_done"], 1)

        @block.tensor
        def _(pe):
            pe.transpose(bank_x[0][0:4 * E, 0:P], bias_col[:, :], ident).then_inc(S["bias_psum"], 1)
            pe.wait_ge(S["bias_ready"], 1)
            pe.wait_ge(S["bias_sent"], 16 * 6)
            pe.wait_ge(S["table_ready"], 2)

            def x_transpose(j, u, it, early):
                pe.wait_ge(xs_loaded[u], 16 * (it + 1))
                if not early:
                    pe.wait_ge(S["xst_done"], j - 1)
                pe.transpose(bank_x[u % 2][:, 0:P], xs[:, u, 0:C], ident).then_inc(S["xst_psum"], 1)

            def hidden(j, u, early):
                e = pe.value_load(table[0:1, 1, bass.ds(j, 1)], min_val=0, max_val=E - 1)
                if not early:
                    pe.wait_ge(S["gated_done"], j - 1)
                pe.matmul(bank_h[u % 2][:, :], ones[0:3, :], bias_rows[:, bass.ds(e * (2 * HID), 2 * HID)], start=True, stop=False)
                pe.wait_ge(S["xst_done"], j + 1)
                pe.matmul(bank_h[u % 2][:, :], xst[:, u % 2, :], w_all[:, bass.ds(e * (2 * HID), 2 * HID)], start=False, stop=True).then_inc(S["h_psum"], 1)

            def gated_transpose(j, v, early):
                pe.wait_ge(S["gated_done"], j + 1)
                if not early:
                    pe.wait_ge(S["gt_done"], j - 1)
                for h in range(2):
                    last = pe.transpose(bank_g[v][:, h * P:(h + 1) * P], gated[:, v, h * P:(h + 1) * P], ident)
                last.then_inc(S["gt_psum"], 1)

            def down(j, v, early):
                e = pe.value_load(table[0:1, 1, bass.ds(j, 1)], min_val=0, max_val=E - 1)
                if not early:
                    pe.wait_ge(S["ys_done"], j - 1)
                pe.matmul(bank_y[v][:, 0:C], ones[0:3, :], b2_rows[:, bass.ds(e * C, C)], start=True, stop=False)
                pe.wait_ge(S["gt_done"], j + 1)
                for h in range(2):
                    last = pe.matmul(bank_y[v][:, 0:C], gatedt[:, v, h * P:(h + 1) * P], w2_all[:, bass.ds(e * (2 * C) + h * C, C)],
                                     start=False, stop=(h == 1))
                last.then_inc(S["y_psum"], 1)

            def step(j, u, it, first, last):
                if first and u == 0:
                    x_transpose(0, 0, 0, True)
                if not (last and u == U - 1):
                    x_transpose(j + 1, (u + 1) % U, it if u < U - 1 else it + 1, first and u < 1)
                hidden(j, u, first and u < 2)
                if not (first and u < 1):
                    gated_transpose(j - 1, (u - 1) % 2, first and u < 3)
                if not (first and u < 2):
                    down(j - 2, u % 2, first and u < 4)

            over_blocks(pe, step)
            gated_transpose(NB - 1, (NB - 1) % 2, False)
            down(NB - 2, NB % 2, False)
            down(NB - 1, (NB - 1) % 2, False)


def kernel(**inputs):
    import concourse.bacc as bacc
    from concourse.bass_utils import run_bass_kernel_spmd

    f = {k: np.asarray(v) for k, v in inputs.items()}
    x = f["x"].reshape(BATCH, C, HW)
    small = np.zeros((P, 428), np.float32)
    small[:, 0:KK] = f["L0_conv_K_w"].T
    small[:, 64:192] = f["L0_conv_conv0_w"].T
    small[:, 192:320] = f["L0_conv_conv1_w"].T
    small[:, 320:328] = f["L1_ffn_router_w"]
    small[:, 328:377] = f["L0_conv_ln_w"].reshape(C, KK)
    small[:, 377:426] = f["L0_conv_ln_b"].reshape(C, KK)
    small[0:KK, 426] = f["L0_conv_K_b"]
    small[KKP:KKP + KK, 426] = f["L0_conv_K_b"]
    small[:, 427] = f["L0_conv_conv0_b"]
    bgv = np.concatenate([f["L1_ffn_bg"].reshape(EXPERTS, 2, P), f["L1_ffn_bv"].reshape(EXPERTS, 2, P)], 1)
    const = constants()
    arrays = {
        "x": x,
        "xt": x.reshape(PAIRS, 2, C, CHUNKS, P).transpose(4, 0, 3, 1, 2).reshape(P, PAIRS, TILES, C),
        "const": np.concatenate([const[n] for n in WIDTHS], 1).astype(np.float32),
        "small": small,
        "c1_b": f["L0_conv_conv1_b"],
        "router_b": f["L1_ffn_router_b"],
        "w1t": f["L1_ffn_w1"].transpose(0, 2, 1),
        "wg": f["L1_ffn_wg"],
        "wv": f["L1_ffn_wv"],
        "b1c": f["L1_ffn_b1"].reshape(EXPERTS * 2, P).T,
        "bgv": bgv.reshape(EXPERTS * 4, P).T,
        "w2": f["L1_ffn_w2"].reshape(EXPERTS * 2, P, C).transpose(1, 0, 2).reshape(P, EXPERTS * 2 * C),
        "b2": f["L1_ffn_b2"],
    }
    arrays = {k: np.ascontiguousarray(v) for k, v in arrays.items()}
    nc = bacc.Bacc("TRN2", target_bir_lowering=False, num_devices=1)
    aps = {k: nc.dram_tensor("in_" + k, v.shape, mybir.dt.from_np(v.dtype), kind="ExternalInput").ap() for k, v in arrays.items()}
    out = nc.dram_tensor("out", (TOKENS, C), F32, kind="ExternalOutput").ap()
    build(nc, aps, out)
    got = run_bass_kernel_spmd(nc, [{"in_" + k: v for k, v in arrays.items()}], core_ids=[0]).results[0]["out"]
    return got.reshape(BATCH, HW, C).transpose(0, 2, 1).reshape(BATCH, C, SIDE_IN, SIDE_IN)
```

```python
from contextlib import ExitStack

import numpy as np

import concourse.bass as bass
from concourse import mybir

F32 = mybir.dt.float32
BF16 = mybir.dt.bfloat16
U32 = mybir.dt.uint32
I32 = mybir.dt.int32
ALU = mybir.AluOpType
ACT = mybir.ActivationFunctionType
AX = mybir.AxisListType

P = 128
BATCH, C, SIDE_IN, TAPS = 16, 128, 16, 7
HW = SIDE_IN * SIDE_IN
KK = TAPS * TAPS
KKP = 64
GROUP = C // 32
PAIRS = BATCH // 2
CHUNKS = HW // P
TILES = 2 * CHUNKS
PAIR_TOKENS = 2 * HW
TOKENS = BATCH * HW
EXPERTS, HID = 8, 256
EPS = 1e-5

PAD = TAPS // 2
SIDE = SIDE_IN + PAD
FREQS = (SIDE * SIDE + 1) // 2
HALF = (FREQS + 1) // 2

REGION = TOKENS + P
ROWS = EXPERTS * REGION + P
ROW = C + 4
UNROLL = 8
BLOCKS = -(-(2 * TOKENS // P + EXPERTS - 1) // UNROLL) * UNROLL
SKIP = 1 << 20


def constants():
    k = np.arange(P)
    ident = np.eye(P)
    group = (k[:, None] // GROUP == k[None, :] // GROUP) / GROUP
    mean = np.full((P, P), 1.0 / (C * KK))
    before = (k[:, None] < k[None, :]).astype(np.float64)

    freq = [(0, 0)] + [(u, v) for u in range(SIDE) for v in range(SIDE)
                       if (u, v) < ((-u) % SIDE, (-v) % SIDE)]
    u = np.array([f[0] for f in freq] + [0] * (2 * HALF - FREQS))
    v = np.array([f[1] for f in freq] + [0] * (2 * HALF - FREQS))
    used = np.array([1.0] * FREQS + [0.0] * (2 * HALF - FREQS))
    pos = np.arange(HW)
    angle = 2 * np.pi / SIDE * (np.outer(pos // SIDE_IN, u) + np.outer(pos % SIDE_IN, v))
    tap = np.arange(KK)
    shift = 2 * np.pi / SIDE * (np.outer(PAD - tap // TAPS, u) + np.outer(PAD - tap % TAPS, v))
    weight = used * np.where(np.arange(2 * HALF) == 0, 1.0, 2.0) / SIDE ** 2

    def parts(re, im):
        n = re.shape[0]
        return np.stack([re.reshape(n, 2, HALF), im.reshape(n, 2, HALF)], 2).reshape(n, 4 * HALF)

    fwd = parts(np.cos(angle) * used, -np.sin(angle) * used)
    fwd = fwd.reshape(CHUNKS, P, 4 * HALF).transpose(1, 0, 2).reshape(P, -1)
    tapf = np.zeros((P, 4 * HALF))
    tapf[:KK] = parts(np.cos(shift) * used, -np.sin(shift) * used)
    inv = parts(np.cos(angle) * weight, -np.sin(angle) * weight)
    inv_t = np.zeros((P, 4 * HW))
    inv_t[:HALF] = inv.reshape(HW, 4, HALF).transpose(2, 1, 0).reshape(HALF, -1)
    return {"ident": ident, "group": group, "mean": mean, "before": before,
            "fwd": fwd, "tapf": tapf, "inv": inv_t}


WIDTHS = {"ident": P, "group": P, "mean": P, "before": P, "fwd": CHUNKS * 4 * HALF,
          "tapf": 4 * HALF, "inv": 4 * HW}
STARTS = dict(zip(WIDTHS, np.cumsum([0] + list(WIDTHS.values())).tolist()))
CONST_COLS = sum(WIDTHS.values())


def spread(ap, axis, n):
    ap = ap.unsqueeze(axis)
    shape = list(ap.shape)
    shape[axis] = n
    return ap.broadcast_to(shape)


def build(nc, a_in, out):
    ctx = ExitStack()

    def sb(name, shape, dt=F32):
        return ctx.enter_context(nc.sbuf_tensor(name, shape, dt))

    def sem(name):
        return ctx.enter_context(nc.semaphore(name))

    with ctx:
        rows_dram = nc.dram_tensor("rows_dram", (ROWS, ROW), F32, kind="Internal").ap()
        moe_dram = nc.dram_tensor("moe_dram", (2 * TOKENS, C), F32, kind="Internal").ap()

        const = sb("const", [P, CONST_COLS])

        def cst(name):
            return const[:, STARTS[name]:STARTS[name] + WIDTHS[name]]

        ident, group_avg, mean_all = cst("ident"), cst("group"), cst("mean")
        fwd = cst("fwd").rearrange("p (h r f) -> p h r f", h=CHUNKS, r=4)
        tapf = cst("tapf").rearrange("p (r f) -> p r f", r=4)
        inv = cst("inv").rearrange("p (r n) -> p r n", r=4)
        before = sb("before", [P, P], BF16)
        ones = sb("ones", [P, P], BF16)
        small = sb("small", [P, a_in["small"].shape[1]])
        kw_t, c0_t, c1_t = small[:, 0:KKP], small[:, 64:192], small[:, 192:320]
        router_w, ln_w, ln_b = small[:, 320:328], small[:, 328:377], small[:, 377:426]
        key_b, c0_b = small[:, 426:427], small[:, 427:428]
        c1_b = sb("c1_b", [KK, C])
        router_b = sb("router_b", [P, EXPERTS])
        w1t = sb("w1t", [P, 2, 2, C])
        wgv = sb("wgv", [P, 2, 2, 2 * HID])
        b1c = sb("b1c", [P, EXPERTS * 2])
        bgv = sb("bgv", [P, EXPERTS * 4])
        w_all = sb("w_all", [P, EXPERTS * 2 * HID])
        w2_all = sb("w2_all", [P, EXPERTS * 2 * C])
        b2 = sb("b2", [EXPERTS, C])

        xc = sb("xc", [P, 2, PAIR_TOKENS])
        xt = sb("xt", [P, PAIRS, TILES, C])
        gn_raw = sb("gn_raw", [P, 2, 2, 6])
        gn_mv = sb("gn_mv", [P, 2, 2, 2])
        gn_mean = sb("gn_mean", [P, 2, 2])
        gn_dev = sb("gn_dev", [P, 2])
        gn_sq = sb("gn_sq", [P, 2])
        gn_e2 = sb("gn_e2", [P, 2])
        gn_var = sb("gn_var", [P, 2])
        gn_rstd = sb("gn_rstd", [P, 2, 2])
        gbuf = sb("gbuf", [P, 2, PAIR_TOKENS])
        gt = sb("gt", [P, 2, CHUNKS, 2 * C])
        kmax = sb("kmax", [P, 1])
        ksum_b = sb("ksum_b", [P, 1])
        kshift = sb("kshift", [P, 1])
        kexp = sb("kexp", [P, HW])
        ktot = sb("ktot", [P, 1])
        krec = sb("krec", [P, 1])
        kprob = sb("kprob", [P, HW])
        pt = sb("pt", [P, CHUNKS, 2 * KKP])
        fraw = sb("fraw", [P, 2, 2, KK])
        f0 = sb("f0", [P, 2, KK])
        fsum = sb("fsum", [P, 2])
        fcen = sb("fcen", [P, 2, KK])
        fsq = sb("fsq", [P, 2, KK])
        fsqs = sb("fsqs", [P, 2])
        fvar = sb("fvar", [P, 2])
        frstd = sb("frstd", [P, 2])
        flw = sb("flw", [P, 2, KK])
        fln = sb("fln", [P, 2, KK])
        frelu = sb("frelu", [P, 2, KK])
        filt = sb("filt", [KK, 2, C])
        ghat = sb("ghat", [HALF, 2, 4, 2 * C])
        prod = sb("prod", [HALF, 2, 4, 2 * C])
        zhat = sb("zhat", [HALF, 4, 2 * C])
        t1 = sb("t1", [P, 2, TILES, C])
        ln_raw = sb("ln_raw", [P, TILES, 6])
        ln_mv = sb("ln_mv", [P, TILES, 2])
        ln_var = sb("ln_var", [P, TILES])
        ln_rstd = sb("ln_rstd", [P, TILES])
        z = sb("z", [P, TILES, C])
        qt = sb("qt", [P, PAIR_TOKENS])
        e_attn = sb("e_attn", [P, 2, CHUNKS, HW])
        asum = sb("asum", [P, 2, CHUNKS])
        arec = sb("arec", [P, 2, CHUNKS])
        t2 = sb("t2", [P, PAIRS, TILES, C])
        ln2_raw = sb("ln2_raw", [P, TILES, 6])
        ln2_mv = sb("ln2_mv", [P, TILES, 2])
        ln2_var = sb("ln2_var", [P, TILES])
        ln2_rstd = sb("ln2_rstd", [P, TILES])
        row = sb("row", [P, 2, TILES, 2, ROW])
        z2t = sb("z2t", [P, PAIR_TOKENS])
        minus_half = sb("minus_half", [P, TILES])

        iota8 = sb("iota8", [P, EXPERTS])
        dest = sb("dest", [P, PAIRS, TILES, 2], U32)
        logits = sb("logits", [P, TILES, EXPERTS])
        sorted8 = sb("sorted8", [P, TILES, 8])
        index8 = sb("index8", [P, TILES, 8], U32)
        lshift = sb("lshift", [P, TILES, 8])
        lexp = sb("lexp", [P, TILES, 8])
        lsum = sb("lsum", [P, TILES])
        lrec = sb("lrec", [P, TILES])
        chosen = sb("chosen", [P, TILES, 2, EXPERTS])
        either = sb("either", [P, TILES, EXPERTS], BF16)
        base = sb("base", [P, 2, EXPERTS])
        pos = sb("pos", [P, TILES, EXPERTS])
        posk = sb("posk", [P, TILES, 2, EXPERTS])
        slotf = sb("slotf", [P, TILES * 2])
        slot = sb("slot", [P, 2, TILES * 2], U32)

        banks = [ctx.enter_context(nc.psum_tensor(f"bank{i}", [P, 512], F32)) for i in range(8)]
        bank_k, bank_t, bank_b, bank_o, bank_s0, bank_s1, bank_d0, bank_d1 = banks
        bank_s = (bank_s0, bank_s1)
        bank_d = (bank_d0, bank_d1)

        ld_x = [sem("ld_x0"), sem("ld_x1")]
        ld_c1 = sem("ld_c1")
        ld_c2 = sem("ld_c2")
        ld_w = [sem("ld_w0"), sem("ld_w1")]
        ld_b = sem("ld_b")
        const_ready = sem("const_ready")
        iota_ready = sem("iota_ready")
        gn_raw_done, gn_mv_done = sem("gn_raw_done"), sem("gn_mv_done")
        gn_avg, gn_dev_done, gn_sq_done, gn_e2_done = sem("gn_avg"), sem("gn_dev_done"), sem("gn_sq_done"), sem("gn_e2_done")
        gn_avg2, gn_var_done, gn_rstd_done = sem("gn_avg2"), sem("gn_var_done"), sem("gn_rstd_done")
        g_done, keys_done, gt_psum, gt_done = sem("g_done"), sem("keys_done"), sem("gt_psum"), sem("gt_done")
        kmax_done, kshift1, kshift_done, kexp_done = sem("kmax_done"), sem("kshift1"), sem("kshift_done"), sem("kexp_done")
        krec_done, kprob_done, pt_psum, pt_done = sem("krec_done"), sem("kprob_done"), sem("pt_psum"), sem("pt_done")
        row2_done = sem("row2_done")
        fraw_psum, fraw_done = sem("fraw_psum"), sem("fraw_done")
        ghat_psum, ghat_done = sem("ghat_psum"), sem("ghat_done")
        wmul_psum, wmul_done = sem("wmul_psum"), sem("wmul_done")
        wbias_psum, wbias_done = sem("wbias_psum"), sem("wbias_done")
        conv0_psum, f0_done = sem("conv0_psum"), sem("f0_done")
        fmean_psum, fcen_done, fsqs_done = sem("fmean_psum"), sem("fcen_done"), sem("fsqs_done")
        fvar_psum, fvar_done, frstd_done = sem("fvar_psum"), sem("fvar_done"), sem("frstd_done")
        flw_done, fln_done, frelu_done = sem("flw_done"), sem("fln_done"), sem("frelu_done")
        filt_psum, filt_done = sem("filt_psum"), sem("filt_done")
        what_psum, prod_done, zhat_done = sem("what_psum"), sem("prod_done"), sem("zhat_done")
        conv_psum, t1_done = sem("conv_psum"), sem("t1_done")
        ln_raw_done, ln_mv_done, ln_var_done, ln_rstd_done = sem("ln_raw_done"), sem("ln_mv_done"), sem("ln_var_done"), sem("ln_rstd_done")
        z_done, zt_psum, qt_done = sem("z_done"), sem("zt_psum"), sem("qt_done")
        score_psum, e_done = sem("score_psum"), sem("e_done")
        arec_done, attn_psum, t2_done = sem("arec_done"), sem("attn_psum"), sem("t2_done")
        ln2_raw_done, ln2_mv_done, ln2_var_done, ln2_rstd_done = sem("ln2_raw_done"), sem("ln2_mv_done"), sem("ln2_var_done"), sem("ln2_rstd_done")
        z2_done, z2t_psum, z2t_done = sem("z2_done"), sem("z2t_psum"), sem("z2t_done")
        logit_psum, logits_done = sem("logit_psum"), sem("logits_done")
        sorted_done, index_done, lshift_done, lexp_done = sem("sorted_done"), sem("index_done"), sem("lshift_done"), sem("lexp_done")
        lsum_done, lrec_done, chosen_done, either_done = sem("lsum_done"), sem("lrec_done"), sem("chosen_done"), sem("either_done")
        rank_psum, pos_done, posk_done, row_done = sem("rank_psum"), sem("pos_done"), sem("posk_done"), sem("row_done")
        base_done, slotf_done = sem("base_done"), sem("slotf_done")
        sent = [sem("sent0"), sem("sent1")]
        stored = sem("stored")

        bias_col = sb("bias_col", [P, EXPERTS * 4])
        STAGES = 7
        rounds = PAIRS + STAGES - 1

        def stages(i):
            return [p if 0 <= p < PAIRS else None for p in range(i, i - STAGES, -1)]

        def through(i, stage):
            return min(max(i - stage + 1, 0), PAIRS)

        N, A, B, D, E = 0, 1, 2, 4, 5
        CC = 3

        def after(eng, semaphore, count):
            if count > 0:
                eng.wait_ge(semaphore, count)

        with nc.Block() as block:
            @block.sync
            def _(sp):
                def load_x(p):
                    sp.dma_start(xc[:, p % 2, :].rearrange("c (b n) -> c b n", b=2),
                                 a_in["x"][2 * p:2 * p + 2].rearrange("b c n -> c b n")).then_inc(ld_x[p % 2], 16)

                def load_w(e):
                    sp.dma_start(wgv[:, e % 2, :, 0:HID],
                                 a_in["wg"][e].rearrange("(h p) f -> p h f", p=P)).then_inc(ld_w[e % 2], 16)
                    sp.dma_start(wgv[:, e % 2, :, HID:2 * HID],
                                 a_in["wv"][e].rearrange("(h p) f -> p h f", p=P)).then_inc(ld_w[e % 2], 16)
                    sp.dma_start(w1t[:, e % 2, :, :],
                                 a_in["w1t"][e].rearrange("(h p) d -> p h d", p=P)).then_inc(ld_w[e % 2], 16)

                load_x(0)
                sp.dma_start(const[:, 0:STARTS["fwd"]], a_in["const"][:, 0:STARTS["fwd"]]).then_inc(ld_c1, 16)
                sp.dma_start(small[:, :], a_in["small"]).then_inc(ld_c1, 16)
                load_x(1)
                load_w(0)
                sp.dma_start(const[:, STARTS["fwd"]:CONST_COLS], a_in["const"][:, STARTS["fwd"]:CONST_COLS]).then_inc(ld_c2, 16)
                load_w(1)
                sp.dma_start(xt[:, 0:2], a_in["xt"][:, 0:2]).then_inc(ld_c2, 16)
                sp.dma_start(xt[:, 2:PAIRS], a_in["xt"][:, 2:PAIRS]).then_inc(ld_c2, 16)
                sp.dma_start(w2_all[:, :], a_in["w2"]).then_inc(ld_b, 16)
                for p in range(2, PAIRS):
                    sp.wait_ge(g_done, p - 1)
                    load_x(p)
                    sp.wait_ge(wbias_psum, p - 1)
                    load_w(p)

            @block.gpsimd
            def _(pool):
                pool.memset(minus_half[:, :], -0.5)
                pool.memset(row[:, :, :, :, C:ROW], 0.0)
                pool.iota(iota8[:, :], pattern=[[1, EXPERTS]], base=0, channel_multiplier=0,
                          allow_small_or_imprecise_dtypes=True).then_inc(iota_ready, 1)
                pool.iota(base[:, 0, :], pattern=[[REGION, EXPERTS]], base=0, channel_multiplier=0,
                          allow_small_or_imprecise_dtypes=True).then_inc(iota_ready, 1)
                for h in range(CHUNKS):
                    pool.iota(dest[:, :, h * 2:h * 2 + 2, :],
                              pattern=[[PAIR_TOKENS, PAIRS], [HW, 2], [TOKENS, 2]],
                              base=h * P, channel_multiplier=1).then_inc(iota_ready, 1)
                pool.wait_ge(iota_ready, 2 + CHUNKS)

                def dispatch(f, tiles):
                    for t in tiles:
                        for k in range(2):
                            pool.indirect_dma_start(
                                rows_dram, bass.IndirectOffsetOnAxis(ap=slot[:, f % 2, 2 * t + k:2 * t + k + 1], axis=0),
                                row[:, f % 2, t, k, :], None).then_inc(sent[f % 2], 16)

                for i in range(rounds):
                    n, a, b, c, d, e, f = stages(i)
                    if f is not None:
                        pool.wait_ge(row_done, f + 1)
                        pool.wait_ge(row2_done, f + 1)
                        dispatch(f, range(0, TILES // 2))
                    if b is not None:
                        pool.wait_ge(fvar_done, b + 1)
                        pool.tensor_tensor(frstd[:, :], fvar[:, :], minus_half[:, 0:2], ALU.pow).then_inc(frstd_done, 1)
                    if f is not None:
                        dispatch(f, range(TILES // 2, TILES))
                    if n is not None:
                        pool.wait_ge(gn_var_done, n + 1)
                        after(pool, g_done, n - 1)
                        pool.tensor_tensor(gn_rstd[:, n % 2, :], gn_var[:, :], minus_half[:, 0:2], ALU.pow).then_inc(gn_rstd_done, 1)
                    if c is not None:
                        pool.wait_ge(ln_var_done, c + 1)
                        after(pool, z_done, c)
                        pool.tensor_tensor(ln_rstd[:, :], ln_var[:, :], minus_half[:, :], ALU.pow).then_inc(ln_rstd_done, 1)
                    if d is not None:
                        pool.wait_ge(ln2_var_done, d + 1)
                        after(pool, z2_done, d)
                        pool.tensor_tensor(ln2_rstd[:, :], ln2_var[:, :], minus_half[:, :], ALU.pow).then_inc(ln2_rstd_done, 1)

            @block.scalar
            def _(act):
                act.dma_start(c1_b[:, :], a_in["c1_b"].partition_broadcast(KK)).then_inc(ld_b, 16)
                act.dma_start(router_b[:, :], a_in["router_b"].partition_broadcast(P)).then_inc(ld_b, 16)
                act.dma_start(b1c[:, :], a_in["b1c"]).then_inc(ld_b, 16)
                act.dma_start(bgv[:, :], a_in["bgv"]).then_inc(ld_b, 16)
                act.dma_start(b2[:, :], a_in["b2"]).then_inc(ld_b, 16)
                act.wait_ge(ld_c1, 32)
                for i in range(rounds):
                    n, a, b, c, d, e, _ = stages(i)
                    if a is not None:
                        act.wait_ge(gt_psum, a + 1)
                        after(act, fraw_psum, a - 1)
                        after(act, ghat_psum, 2 * (a - 1))
                        act.activation(gt[:, a % 2, :, :].rearrange("p h c -> p (h c)"), bank_t[:, :], ACT.Copy).then_inc(gt_done, 1)
                    if b is not None:
                        act.wait_ge(conv0_psum, b + 1)
                        after(act, fcen_done, b)
                        after(act, fmean_psum, b)
                        for s in range(2):
                            last = act.activation(f0[:, s, :], bank_b[:, s * KK:(s + 1) * KK], ACT.Identity, bias=c0_b,
                                                  accum_out=fsum[:, s:s + 1])
                        last.then_inc(f0_done, 1)
                    if a is not None:
                        act.wait_ge(kshift_done, a + 1)
                        after(act, kprob_done, a)
                        act.activation(kexp[:, :], bank_k[:, 0:HW], ACT.Exp, bias=kshift[:, 0:1], accum_out=ktot[:, 0:1]).then_inc(kexp_done, 1)
                    if e is not None:
                        act.wait_ge(z2t_psum, e + 1)
                        after(act, logit_psum, e)
                        act.activation(z2t[:, :], bank_t[:, :], ACT.Copy).then_inc(z2t_done, 1)
                    if b is not None:
                        act.wait_ge(fcen_done, b + 1)
                        after(act, fvar_psum, b)
                        for s in range(2):
                            last = act.activation(fsq[:, s, :], fcen[:, s, :], ACT.Square, accum_out=fsqs[:, s:s + 1])
                        last.then_inc(fsqs_done, 1)
                        act.wait_ge(ghat_psum, 2 * b + 1)
                        after(act, prod_done, 2 * (b - 1))
                        act.activation(ghat[:, b % 2, 0:2, :].rearrange("p r c -> p (r c)"), bank_s0[0:HALF, :], ACT.Copy).then_inc(ghat_done, 1)
                    if d is not None:
                        act.wait_ge(zt_psum, d + 1)
                        after(act, score_psum, 2 * d)
                        act.activation(qt[:, :], bank_t[:, :], ACT.Tanh).then_inc(qt_done, 1)
                    if e is not None:
                        act.wait_ge(z2_done, e + 1)
                        act.activation(row[:, e % 2, :, 1, 0:C], row[:, e % 2, :, 0, 0:C], ACT.Copy).then_inc(row2_done, 1)
                    if b is not None:
                        act.wait_ge(ghat_psum, 2 * b + 2)
                        act.activation(ghat[:, b % 2, 2:4, :].rearrange("p r c -> p (r c)"), bank_s1[0:HALF, :], ACT.Copy).then_inc(ghat_done, 1)
                    if d is not None:
                        after(act, attn_psum, d)
                        after(act, arec_done, d)
                        for s in range(2):
                            act.wait_ge(score_psum, 2 * d + s + 1)
                            for h in range(CHUNKS):
                                act.activation(e_attn[:, s, h, :], bank_s[s][:, h * HW:(h + 1) * HW], ACT.Exp,
                                               scale=float(C) ** -0.5, accum_out=asum[:, s, h:h + 1]).then_inc(e_done, 1)
                    if e is not None:
                        act.wait_ge(lshift_done, e + 1)
                        after(act, row_done, e)
                        act.activation(lexp[:, :, :].rearrange("p t e -> p (t e)"),
                                       lshift[:, :, :].rearrange("p t e -> p (t e)"), ACT.Exp).then_inc(lexp_done, 1)
                    if a is not None:
                        act.wait_ge(pt_psum, a + 1)
                        after(act, fraw_psum, a)
                        act.activation(pt[:, :, :].rearrange("p h k -> p (h k)"), bank_k[:, HW:2 * HW], ACT.Copy).then_inc(pt_done, 1)
                    if n is not None:
                        act.wait_ge(wmul_psum, n + 1)
                        act.activation(w_all[:, n * 2 * HID:(n + 1) * 2 * HID], bank_d0[:, :], ACT.Copy).then_inc(wmul_done, 1)
                    if a is not None:
                        act.wait_ge(fraw_psum, a + 1)
                        after(act, conv0_psum, a - 1)
                        act.activation(fraw[:, a % 2, :, :], bank_k[:, 0:2 * KKP].rearrange("p (s k) -> p s k", s=2)[:, :, 0:KK],
                                       ACT.Copy).then_inc(fraw_done, 1)

            @block.vector
            def _(dve):
                dve.memset(ones[:, :], 1.0)
                dve.wait_ge(ld_c1, 32)
                dve.tensor_copy(before[:, :], cst("before")).then_inc(const_ready, 1)

                def layer_norm_stats(src, raw, mv, var, raw_done, mv_done, var_done, p):
                    for t in range(TILES):
                        last = dve.bn_stats(raw[:, t, :], src[:, t, :])
                    last.then_inc(raw_done, 1)
                    dve.wait_ge(raw_done, p + 1)
                    for t in range(TILES):
                        last = dve.bn_aggr(mv[:, t, :], raw[:, t, :])
                    last.then_inc(mv_done, 1)
                    dve.wait_ge(mv_done, p + 1)
                    dve.tensor_scalar(var[:, :], mv[:, :, 1], EPS, None, ALU.add).then_inc(var_done, 1)

                def products(c, q):
                    g = ghat[:, c % 2, 2 * q:2 * q + 2, :]
                    w = bank_d[q][0:HALF, :].rearrange("p (r c) -> p r c", r=2)
                    dve.wait_ge(ghat_done, 2 * c + q + 1)
                    dve.wait_ge(what_psum, 2 * c + q + 1)
                    dve.tensor_tensor(prod[:, q, 0:2, :], w, g, ALU.mult)
                    dve.tensor_tensor(prod[:, q, 2, :], w[:, 0, :], g[:, 1, :], ALU.mult)
                    dve.tensor_tensor(prod[:, q, 3, :], w[:, 1, :], g[:, 0, :], ALU.mult).then_inc(prod_done, 1)

                def spectrum(c, q):
                    dve.wait_ge(prod_done, 2 * c + q + 1)
                    after(dve, conv_psum, c)
                    dve.tensor_tensor(zhat[:, 2 * q, :], prod[:, q, 0, :], prod[:, q, 1, :], ALU.subtract)
                    dve.tensor_tensor(zhat[:, 2 * q + 1, :], prod[:, q, 2, :], prod[:, q, 3, :], ALU.add).then_inc(zhat_done, 1)

                for i in range(rounds):
                    n, a, b, c, d, e, _ = stages(i)
                    if d is not None:
                        dve.wait_ge(ln_rstd_done, d + 1)
                        after(dve, attn_psum, d)
                        for t in range(TILES):
                            last = dve.tensor_scalar(z[:, t, :], t1[:, d % 2, t, :], ln_mv[:, t, 0:1], ln_rstd[:, t:t + 1],
                                                     ALU.subtract, ALU.mult)
                        last.then_inc(z_done, 1)
                    if a is not None:
                        dve.wait_ge(keys_done, a + 1)
                        dve.reduce_max(kmax[:, :], bank_k[:, 0:HW], AX.X).then_inc(kmax_done, 1)
                    if e is not None:
                        dve.wait_ge(ln2_rstd_done, e + 1)
                        if e >= 2:
                            dve.wait_ge(sent[e % 2], 16 * 2 * TILES * (e // 2))
                        for t in range(TILES):
                            last = dve.tensor_scalar(row[:, e % 2, t, 0, 0:C], t2[:, e, t, :], ln2_mv[:, t, 0:1], ln2_rstd[:, t:t + 1],
                                                     ALU.subtract, ALU.mult)
                        last.then_inc(z2_done, 1)
                    if a is not None:
                        dve.wait_ge(kmax_done, a + 1)
                        dve.tensor_tensor(ksum_b[:, :], kmax[:, :], key_b, ALU.add).then_inc(kshift1, 1)
                        dve.wait_ge(kshift1, a + 1)
                        after(dve, kexp_done, a)
                        dve.tensor_tensor(kshift[:, :], key_b, ksum_b[:, :], ALU.subtract).then_inc(kshift_done, 1)
                    if c is not None:
                        products(c, 0)
                    if b is not None:
                        dve.wait_ge(fmean_psum, b + 1)
                        after(dve, fsqs_done, b)
                        dve.tensor_tensor(fcen[:, :, :], f0[:, :, :], spread(bank_b[:, 128:130], 2, KK), ALU.subtract).then_inc(fcen_done, 1)
                    if c is not None:
                        spectrum(c, 0)
                    if b is not None:
                        dve.wait_ge(fcen_done, b + 1)
                        dve.tensor_tensor(flw[:, :, :], fcen[:, :, :], spread(ln_w, 1, 2), ALU.mult).then_inc(flw_done, 1)
                    if e is not None:
                        if e == 0:
                            dve.wait_ge(iota_ready, 2 + CHUNKS)
                            dve.wait_ge(ld_b, 96)
                        dve.wait_ge(logit_psum, e + 1)
                        dve.tensor_tensor(logits[:, :, :], bank_b[:, 0:32].rearrange("p (t e) -> p t e", t=TILES),
                                          spread(router_b[:, :], 1, TILES), ALU.add).then_inc(logits_done, 1)
                        dve.tensor_copy(row[:, e % 2, :, :, C + 1:C + 2].bitcast(U32), dest[:, e, :, :].rearrange("p t (k o) -> p t k o", o=1))
                    if a is not None:
                        dve.wait_ge(kexp_done, a + 1)
                        dve.reciprocal(krec[:, :], ktot[:, :]).then_inc(krec_done, 1)
                    if c is not None:
                        products(c, 1)
                    if e is not None:
                        dve.wait_ge(logits_done, e + 1)
                        for t in range(TILES):
                            last = dve.max(sorted8[:, t, :], logits[:, t, :])
                        last.then_inc(sorted_done, 1)
                    if c is not None:
                        spectrum(c, 1)
                    if e is not None:
                        dve.wait_ge(sorted_done, e + 1)
                        for t in range(TILES):
                            last = dve.max_index(index8[:, t, :], sorted8[:, t, :], logits[:, t, :])
                        last.then_inc(index_done, 1)
                        dve.tensor_tensor(lshift[:, :, :], sorted8[:, :, :], spread(sorted8[:, :, 0], 2, 8), ALU.subtract).then_inc(lshift_done, 1)
                    if a is not None:
                        dve.wait_ge(krec_done, a + 1)
                        after(dve, pt_psum, a)
                        dve.tensor_scalar(kprob[:, :], kexp[:, :], krec[:, 0:1], None, ALU.mult).then_inc(kprob_done, 1)
                    if e is not None:
                        dve.wait_ge(index_done, e + 1)
                        for t in range(TILES):
                            last = dve.tensor_tensor(chosen[:, t, :, :], spread(iota8[:, :], 1, 2),
                                                     spread(index8[:, t, 0:2], 2, EXPERTS), ALU.is_equal)
                        last.then_inc(chosen_done, 1)
                    if n is not None:
                        dve.wait_ge(ld_x[n % 2], 16 * (n // 2 + 1))
                        for s in range(2):
                            last = dve.bn_stats(gn_raw[:, n % 2, s, :], xc[:, n % 2, s * HW:(s + 1) * HW])
                        last.then_inc(gn_raw_done, 1)
                    if e is not None:
                        dve.wait_ge(chosen_done, e + 1)
                        dve.tensor_tensor(either[:, :, :], chosen[:, :, 0, :], chosen[:, :, 1, :], ALU.add).then_inc(either_done, 1)
                    if b is not None:
                        dve.wait_ge(fvar_psum, b + 1)
                        dve.tensor_scalar(fvar[:, :], bank_b[:, 132:134], EPS, None, ALU.add).then_inc(fvar_done, 1)
                    if n is not None:
                        dve.wait_ge(gn_raw_done, n + 1)
                        for s in range(2):
                            last = dve.bn_aggr(gn_mv[:, n % 2, s, :], gn_raw[:, n % 2, s, :])
                        last.then_inc(gn_mv_done, 1)
                    if e is not None:
                        dve.wait_ge(lexp_done, e + 1)
                        dve.reduce_sum(lsum[:, :], lexp[:, :, :], AX.X).then_inc(lsum_done, 1)
                    if n is not None:
                        dve.wait_ge(gn_avg, n + 1)
                        dve.tensor_tensor(gn_dev[:, :], gn_mv[:, n % 2, :, 0], bank_d1[:, 0:2], ALU.subtract).then_inc(gn_dev_done, 1)
                        dve.tensor_copy(gn_mean[:, n % 2, :], bank_d1[:, 0:2])
                        dve.wait_ge(gn_dev_done, n + 1)
                        dve.tensor_tensor(gn_sq[:, :], gn_dev[:, :], gn_dev[:, :], ALU.mult).then_inc(gn_sq_done, 1)
                    if e is not None:
                        dve.wait_ge(lsum_done, e + 1)
                        dve.reciprocal(lrec[:, :], lsum[:, :]).then_inc(lrec_done, 1)
                    if n is not None:
                        dve.wait_ge(gn_sq_done, n + 1)
                        dve.tensor_tensor(gn_e2[:, :], gn_sq[:, :], gn_mv[:, n % 2, :, 1], ALU.add).then_inc(gn_e2_done, 1)
                    if b is not None:
                        dve.wait_ge(frstd_done, b + 1)
                        dve.wait_ge(flw_done, b + 1)
                        for s in range(2):
                            last = dve.scalar_tensor_tensor(fln[:, s, :], flw[:, s, :], frstd[:, s:s + 1], ln_b, ALU.mult, ALU.add)
                        last.then_inc(fln_done, 1)
                    if e is not None:
                        dve.wait_ge(lrec_done, e + 1)
                        dve.tensor_tensor(row[:, e % 2, :, :, C], lexp[:, :, 0:2], spread(lrec[:, :], 2, 2), ALU.mult)
                    if b is not None:
                        dve.wait_ge(fln_done, b + 1)
                        dve.tensor_scalar(frelu[:, :, :], fln[:, :, :], 0.0, None, ALU.max).then_inc(frelu_done, 1)
                    if c is not None:
                        dve.wait_ge(conv_psum, c + 1)
                        after(dve, t2_done, c - 1)
                        if c == 0:
                            dve.wait_ge(ld_c2, 48)
                        dve.tensor_tensor(t1[:, c % 2, :, :].rearrange("p t c -> p (t c)"), bank_o[:, :],
                                          xt[:, c, :, :].rearrange("p t c -> p (t c)"), ALU.add).then_inc(t1_done, 1)
                    if e is not None:
                        dve.wait_ge(rank_psum, e + 1)
                        after(dve, base_done, e)
                        dve.tensor_tensor(base[:, (e + 1) % 2, :], base[:, e % 2, :], bank_b[:, 96:96 + EXPERTS], ALU.add).then_inc(base_done, 1)
                        dve.tensor_tensor(pos[:, :, :], bank_b[:, 64:96].rearrange("p (t e) -> p t e", t=TILES),
                                          spread(base[:, e % 2, :], 1, TILES), ALU.add).then_inc(pos_done, 1)
                    if n is not None:
                        dve.wait_ge(gn_avg2, n + 1)
                        dve.tensor_scalar(gn_var[:, :], bank_d1[:, 4:6], EPS, None, ALU.add).then_inc(gn_var_done, 1)
                    if e is not None:
                        dve.wait_ge(pos_done, e + 1)
                        for k in range(2):
                            last = dve.tensor_tensor(posk[:, :, k, :], chosen[:, :, k, :], pos[:, :, :], ALU.mult)
                        last.then_inc(posk_done, 1)
                    if c is not None:
                        dve.wait_ge(t1_done, c + 1)
                        layer_norm_stats(t1[:, c % 2], ln_raw, ln_mv, ln_var, ln_raw_done, ln_mv_done, ln_var_done, c)
                    if n is not None:
                        dve.wait_ge(gn_rstd_done, n + 1)
                        after(dve, keys_done, n - 1)
                        after(dve, gt_psum, n - 1)
                        for s in range(2):
                            last = dve.tensor_scalar(gbuf[:, n % 2, s * HW:(s + 1) * HW], xc[:, n % 2, s * HW:(s + 1) * HW],
                                                     gn_mean[:, n % 2, s:s + 1], gn_rstd[:, n % 2, s:s + 1],
                                                     ALU.subtract, ALU.mult)
                        last.then_inc(g_done, 1)
                    if d is not None:
                        dve.wait_ge(e_done, 4 * (d + 1))
                        dve.reciprocal(arec[:, :, :], asum[:, :, :]).then_inc(arec_done, 1)
                    if e is not None:
                        dve.wait_ge(posk_done, e + 1)
                        dve.reduce_sum(slotf[:, :], posk[:, :, :, :].rearrange("p t k e -> p (t k) e"), AX.X).then_inc(slotf_done, 1)
                    if b is not None:
                        if b == 0:
                            dve.wait_ge(ld_b, 96)
                        dve.wait_ge(filt_psum, b + 1)
                        after(dve, what_psum, 2 * b)
                        dve.tensor_tensor(filt[:, :, :], bank_b[0:KK, 256:512].rearrange("k (s c) -> k s c", s=2),
                                          spread(c1_b[:, :], 1, 2), ALU.add).then_inc(filt_done, 1)
                    if e is not None:
                        dve.wait_ge(slotf_done, e + 1)
                        dve.tensor_copy(slot[:, e % 2, :], slotf[:, :]).then_inc(row_done, 1)
                    if n is not None:
                        if n == 0:
                            dve.wait_ge(ld_b, 96)
                        dve.wait_ge(wbias_psum, n + 1)
                        dve.tensor_tensor(bias_col[:, 4 * n:4 * n + 4], bank_d1[:, 8:12], bgv[:, 4 * n:4 * n + 4], ALU.add).then_inc(wbias_done, 1)
                    if d is not None:
                        dve.wait_ge(arec_done, d + 1)
                        dve.wait_ge(attn_psum, d + 1)
                        for t in range(TILES):
                            h, s = divmod(t, 2)
                            last = dve.scalar_tensor_tensor(t2[:, d, t, :], bank_o[:, t * C:(t + 1) * C], arec[:, s, h:h + 1],
                                                            t1[:, d % 2, t, :], ALU.mult, ALU.add)
                        last.then_inc(t2_done, 1)
                        dve.wait_ge(t2_done, d + 1)
                        layer_norm_stats(t2[:, d], ln2_raw, ln2_mv, ln2_var, ln2_raw_done, ln2_mv_done, ln2_var_done, d)

            @block.tensor
            def _(pe):
                pe.wait_ge(ld_c1, 32)
                pe.wait_ge(const_ready, 1)

                def features_spectrum(b, q):
                    for r in range(2):
                        for h in range(CHUNKS):
                            last = pe.matmul(bank_s[q][0:HALF, r * 2 * C:(r + 1) * 2 * C], fwd[:, h, 2 * q + r, :],
                                             gt[:, b % 2, h, :], start=(h == 0), stop=(h == CHUNKS - 1))
                    last.then_inc(ghat_psum, 1)

                for i in range(rounds):
                    n, a, b, c, d, e, _ = stages(i)
                    if a is not None:
                        pe.wait_ge(g_done, a + 1)
                        after(pe, gt_done, a)
                        after(pe, qt_done, through(i - 1, D))
                        after(pe, z2t_done, through(i - 1, E))
                        for h in range(CHUNKS):
                            for s in range(2):
                                last = pe.transpose(bank_t[:, h * 2 * C + s * C:h * 2 * C + (s + 1) * C],
                                                    gbuf[:, a % 2, s * HW + h * P:s * HW + (h + 1) * P], ident)
                        last.then_inc(gt_psum, 1)
                        after(pe, fraw_done, a)
                        for s in range(2):
                            last = pe.matmul(bank_k[s * KKP:(s + 1) * KKP, 0:HW], kw_t, gbuf[:, a % 2, s * HW:(s + 1) * HW], start=True, stop=True)
                        last.then_inc(keys_done, 1)
                    if b is not None:
                        pe.wait_ge(fraw_done, b + 1)
                        after(pe, filt_done, b)
                        after(pe, pos_done, through(i - 1, E))
                        pe.matmul(bank_b[:, 0:2 * KK], c0_t, fraw[:, b % 2, :, :].rearrange("p s k -> p (s k)"), start=True, stop=True).then_inc(conv0_psum, 1)
                    if c is not None:
                        pe.wait_ge(filt_done, c + 1)
                        if c == 0:
                            pe.wait_ge(ld_c2, 48)
                        after(pe, prod_done, 2 * c)
                        after(pe, wmul_done, through(i - 1, N))
                        after(pe, wbias_done, through(i - 1, N))
                        for q in range(2):
                            for r in range(2):
                                last = pe.matmul(bank_d[q][0:HALF, r * 2 * C:(r + 1) * 2 * C], tapf[0:KK, 2 * q + r, :],
                                                 filt[:, :, :].rearrange("k s c -> k (s c)"), start=True, stop=True)
                            last.then_inc(what_psum, 1)
                    if b is not None:
                        pe.wait_ge(f0_done, b + 1)
                        pe.matmul(bank_b[:, 128:130], mean_all, fsum[:, :], start=True, stop=True).then_inc(fmean_psum, 1)
                        pe.wait_ge(gt_done, b + 1)
                        if b == 0:
                            pe.wait_ge(ld_c2, 48)
                        after(pe, ghat_done, 2 * b)
                        after(pe, e_done, 4 * through(i - 1, D))
                        features_spectrum(b, 0)
                    if e is not None:
                        pe.wait_ge(z2_done, e + 1)
                        after(pe, gt_done, through(i, A))
                        after(pe, qt_done, through(i - 1, D))
                        for t in range(TILES):
                            last = pe.transpose(bank_t[:, t * P:(t + 1) * P], row[:, e % 2, t, 0, 0:C], ident)
                        last.then_inc(z2t_psum, 1)
                    if b is not None:
                        features_spectrum(b, 1)
                    if e is not None:
                        pe.wait_ge(z2t_done, e + 1)
                        after(pe, fcen_done, through(i, B))
                        after(pe, filt_done, through(i - 1, B))
                        after(pe, pos_done, e)
                        for t in range(TILES):
                            last = pe.matmul(bank_b[:, t * EXPERTS:(t + 1) * EXPERTS], z2t[:, t * P:(t + 1) * P], router_w, start=True, stop=True)
                        last.then_inc(logit_psum, 1)
                    if d is not None:
                        pe.wait_ge(z_done, d + 1)
                        after(pe, gt_done, through(i, A))
                        after(pe, z2t_done, through(i, E))
                        after(pe, qt_done, d)
                        for t in range(TILES):
                            h, s = divmod(t, 2)
                            last = pe.transpose(bank_t[:, s * HW + h * P:s * HW + (h + 1) * P], z[:, t, :], ident)
                        last.then_inc(zt_psum, 1)
                    if n is not None:
                        pe.wait_ge(ld_w[n % 2], 48 * (n // 2 + 1))
                        after(pe, prod_done, 2 * through(i, CC) - 1)
                        after(pe, wmul_done, n)
                        for h in range(2):
                            last = pe.matmul(bank_d0[:, :], w1t[:, n % 2, h, :], wgv[:, n % 2, h, :], start=(h == 0), stop=(h == 1))
                        last.then_inc(wmul_psum, 1)
                    if b is not None:
                        pe.wait_ge(fsqs_done, b + 1)
                        after(pe, logits_done, through(i, E))
                        pe.matmul(bank_b[:, 132:134], mean_all, fsqs[:, :], start=True, stop=True).then_inc(fvar_psum, 1)
                    if d is not None:
                        pe.wait_ge(qt_done, d + 1)
                        after(pe, ghat_done, 2 * through(i, B))
                        after(pe, e_done, 4 * d)
                        for s in range(2):
                            for h in range(CHUNKS):
                                last = pe.matmul(bank_s[s][:, h * HW:(h + 1) * HW], qt[:, s * HW + h * P:s * HW + (h + 1) * P],
                                                 qt[:, s * HW:(s + 1) * HW], start=True, stop=True)
                            last.then_inc(score_psum, 1)
                    if a is not None:
                        pe.wait_ge(kprob_done, a + 1)
                        for h in range(CHUNKS):
                            last = pe.transpose(bank_k[:, HW + h * P:HW + (h + 1) * P], kprob[:, h * P:(h + 1) * P], ident)
                        last.then_inc(pt_psum, 1)
                    if n is not None:
                        pe.wait_ge(gn_mv_done, n + 1)
                        after(pe, prod_done, 2 * through(i, CC))
                        after(pe, wbias_done, n)
                        pe.matmul(bank_d1[:, 0:2], group_avg, gn_mv[:, n % 2, :, 0], start=True, stop=True).then_inc(gn_avg, 1)
                    if c is not None:
                        pe.wait_ge(zhat_done, 2 * (c + 1))
                        after(pe, t2_done, through(i - 1, D))
                        after(pe, t1_done, c)
                        for h in range(CHUNKS):
                            for r in range(4):
                                last = pe.matmul(bank_o[:, h * 2 * C:(h + 1) * 2 * C], inv[0:HALF, r, h * P:(h + 1) * P],
                                                 zhat[:, r, :], start=(r == 0), stop=(r == 3))
                        last.then_inc(conv_psum, 1)
                    if e is not None:
                        pe.wait_ge(either_done, e + 1)
                        after(pe, fvar_done, through(i, B))
                        for t in range(TILES):
                            for u in range(t):
                                pe.matmul(bank_b[:, 64 + t * EXPERTS:64 + (t + 1) * EXPERTS], ones[:, :], either[:, u, :], start=(u == 0), stop=False)
                            pe.matmul(bank_b[:, 64 + t * EXPERTS:64 + (t + 1) * EXPERTS], before[:, :], either[:, t, :], start=(t == 0), stop=True)
                        for u in range(TILES):
                            last = pe.matmul(bank_b[:, 96:96 + EXPERTS], ones[:, :], either[:, u, :], start=(u == 0), stop=(u == TILES - 1))
                        last.then_inc(rank_psum, 1)
                    if n is not None:
                        pe.wait_ge(gn_e2_done, n + 1)
                        pe.matmul(bank_d1[:, 4:6], group_avg, gn_e2[:, :], start=True, stop=True).then_inc(gn_avg2, 1)
                    if a is not None:
                        pe.wait_ge(pt_done, a + 1)
                        pe.wait_ge(gt_done, a + 1)
                        for s in range(2):
                            for h in range(CHUNKS):
                                last = pe.matmul(bank_k[:, s * KKP:(s + 1) * KKP], gt[:, a % 2, h, s * C:(s + 1) * C],
                                                 pt[:, h, s * KKP:(s + 1) * KKP], start=(h == 0), stop=(h == CHUNKS - 1))
                        last.then_inc(fraw_psum, 1)
                    if d is not None:
                        pe.wait_ge(e_done, 4 * (d + 1))
                        after(pe, t1_done, through(i, CC))
                        after(pe, t2_done, d)
                        for h in range(CHUNKS):
                            for s in range(2):
                                for k in range(CHUNKS):
                                    last = pe.matmul(bank_o[:, (h * 2 + s) * C:(h * 2 + s + 1) * C], e_attn[:, s, k, h * P:(h + 1) * P],
                                                     z[:, k * 2 + s, :], start=(k == 0), stop=(k == CHUNKS - 1))
                        last.then_inc(attn_psum, 1)
                    if b is not None:
                        pe.wait_ge(frelu_done, b + 1)
                        after(pe, pos_done, through(i, E))
                        for s in range(2):
                            last = pe.matmul(bank_b[0:KK, 256 + s * C:256 + (s + 1) * C], frelu[:, s, :], c1_t, start=True, stop=True)
                        last.then_inc(filt_psum, 1)
                    if n is not None:
                        pe.wait_ge(gn_var_done, n + 1)
                        if n == 0:
                            pe.wait_ge(ld_b, 96)
                        for q in range(4):
                            for h in range(2):
                                last = pe.matmul(bank_d1[:, 8 + q:9 + q], wgv[:, n % 2, h, q * P:(q + 1) * P], b1c[:, 2 * n + h:2 * n + h + 1],
                                                 start=(h == 0), stop=(h == 1))
                        last.then_inc(wbias_psum, 1)

        experts(nc, ctx, sb, sem, out, dict(
            rows_dram=rows_dram, moe_dram=moe_dram, ident=ident, ones=ones, iota8=iota8, base=base, bias_col=bias_col,
            b2=b2, w_all=w_all, w2_all=w2_all, t2=t2, first=xt, banks=banks, sent=sent, ld_b=ld_b))


def experts(nc, ctx, sb, sem, out, g):
    rows_dram, moe_dram, ident, ones, banks = g["rows_dram"], g["moe_dram"], g["ident"], g["ones"], g["banks"]
    iota8, base, w_all, w2_all, t2, y_first = g["iota8"], g["base"], g["w_all"], g["w2_all"], g["t2"], g["first"]
    bias_col, b2 = g["bias_col"], g["b2"]
    E, NB, U = EXPERTS, BLOCKS, UNROLL
    NTHR = TOKENS // P
    ZERO = EXPERTS * REGION

    region = sb("region", [P, E])
    threshold = sb("threshold", [P, NTHR])
    block_no = sb("block_no", [P, NB])
    channel = sb("channel", [P, 1])
    count = sb("count", [P, E])
    more = sb("more", [P, E, NTHR])
    nblk = sb("nblk", [P, E])
    upto = sb("upto", [P, E, E])
    cumt = sb("cumt", [P, E, E])
    cum = sb("cum", [P, E])
    cum_before = sb("cum_before", [P, E])
    offset = sb("offset", [P, E])
    past = sb("past", [P, NB, E])
    expert = sb("expert", [P, NB])
    mine = sb("mine", [P, NB, E])
    used = sb("used", [P, NB])
    offs = sb("offs", [P, NB, E])
    start = sb("start", [P, NB])
    jz = sb("jz", [P, NB])
    ujz = sb("ujz", [P, NB])
    start2 = sb("start2", [P, NB])
    table = sb("table", [P, 2, NB], I32)
    pad_at = sb("pad_at", [P, E], U32)
    pad_row = sb("pad_row", [P, ROW])

    def parts_of(name, rows):
        return [sb(f"{name}_full", [rows, P]), sb(f"{name}_rest", [rows, 2, P]), sb(f"{name}_part", [rows, 3, P], BF16)]

    bias_full, bias_rest, bias_part = parts_of("bias", 4 * E)
    _, b2_rest, b2_part = parts_of("b2", E)
    bias_rows = sb("bias_rows", [3, E * 2 * HID], BF16)
    b2_rows = sb("b2_rows", [3, E * C], BF16)

    xs = sb("xs", [P, U, ROW])
    xst = sb("xst", [P, 2, P])
    silu = sb("silu", [P, 2, HID])
    gated = sb("gated", [P, 2, HID])
    gatedt = sb("gatedt", [P, 2, HID])
    ys = sb("ys", [P, U, C])
    y_second = sb("y_second", [P, PAIRS, TILES, C])
    bank_x, bank_h, bank_g, bank_y = banks[0:2], banks[2:4], banks[4:6], banks[6:8]

    names = ("consts table_step table_ready pads_sent bias_psum bias_ready bias_sent chain "
             "xst_psum xst_done h_psum silu_done gated_done gt_psum gt_done y_psum ys_done "
             "sending sum1_done sum_done stored").split()
    S = {n: sem("moe_" + n) for n in names}
    xs_loaded = [sem(f"moe_xs_loaded{u}") for u in range(U)]
    ys_sent = [sem(f"moe_ys_sent{u}") for u in range(U)]
    y_loaded = [sem(f"moe_y_loaded{p}") for p in range(PAIRS)]

    def over_blocks(eng, step):
        turns = NB // U
        for u in range(U):
            step(u, u, 0, True, False)
        with eng.Fori(1, turns - 1) as it:
            for u in range(U):
                step(it * U + u, u, it, False, False)
        for u in range(U):
            step((turns - 1) * U + u, u, turns - 1, False, True)

    with nc.Block() as block:
        @block.gpsimd
        def _(pool):
            pool.memset(pad_row[:, :], 0.0)
            pool.iota(region[:, :], pattern=[[REGION, E]], base=0, channel_multiplier=0, allow_small_or_imprecise_dtypes=True)
            pool.iota(threshold[:, :], pattern=[[P, NTHR]], base=0, channel_multiplier=0, allow_small_or_imprecise_dtypes=True)
            pool.iota(block_no[:, :], pattern=[[1, NB]], base=0, channel_multiplier=0, allow_small_or_imprecise_dtypes=True)
            pool.iota(jz[:, :], pattern=[[P, NB]], base=-ZERO, channel_multiplier=0, allow_small_or_imprecise_dtypes=True)
            pool.iota(channel[:, :], pattern=[[0, 1]], base=0, channel_multiplier=1, allow_small_or_imprecise_dtypes=True).then_inc(S["consts"], 1)
            pool.wait_ge(S["consts"], 1)
            pool.iota(pad_row[:, C + 1:C + 2].bitcast(U32), pattern=[[0, 1]], base=SKIP, channel_multiplier=0).then_inc(S["consts"], 1)
            pool.wait_ge(S["consts"], 2)
            pool.dma_start(rows_dram[ZERO:ZERO + P, :], pad_row[:, :]).then_inc(S["pads_sent"], 16)
            pool.wait_ge(S["table_ready"], 1)
            for e in range(E):
                pool.indirect_dma_start(rows_dram, bass.IndirectOffsetOnAxis(ap=pad_at[:, e:e + 1], axis=0),
                                        pad_row[:, :], None).then_inc(S["pads_sent"], 16)

            def send(j, u, it, first, last):
                pool.wait_ge(S["ys_done"], j + 1)
                pool.sem_inc(S["sending"], 1)
                pool.indirect_dma_start(moe_dram, bass.IndirectOffsetOnAxis(ap=xs[:, u, C + 1:C + 2].bitcast(U32), axis=0),
                                        ys[:, u, :], None, bounds_check=2 * TOKENS - 1, oob_is_err=False).then_inc(ys_sent[u], 16)

            over_blocks(pool, send)

        @block.sync
        def _(sp):
            for s in range(2):
                sp.wait_ge(g["sent"][s], 16 * 2 * TILES * (PAIRS // 2))
            sp.wait_ge(S["pads_sent"], 16 * (E + 1))
            sp.wait_ge(S["table_ready"], 2)

            def load(j, u, it, first, last):
                if not first:
                    sp.wait_ge(ys_sent[u], 16 * it)
                row0 = sp.value_load(table[0:1, 0, bass.ds(j, 1)], min_val=0, max_val=ZERO)
                sp.dma_start(xs[:, u, :], rows_dram[bass.ds(row0, P), :]).then_inc(xs_loaded[u], 16)

            over_blocks(sp, load)
            for u in range(U):
                sp.wait_ge(ys_sent[u], 16 * (NB // U))
            halves = moe_dram.rearrange("(k p b h n) c -> k p n h b c", k=2, b=2, h=CHUNKS, n=P)
            for p in range(PAIRS):
                for k, dst in ((0, y_first), (1, y_second)):
                    for h in range(CHUNKS):
                        sp.dma_start(dst[:, p, 2 * h:2 * h + 2, :], halves[k, p, :, h]).then_inc(y_loaded[p], 16)
            outs = out.rearrange("(p b h n) c -> p n h b c", b=2, h=CHUNKS, n=P)
            for p in range(PAIRS):
                sp.wait_ge(S["sum_done"], p + 1)
                for h in range(CHUNKS):
                    sp.dma_start(outs[p, :, h], y_second[:, p, 2 * h:2 * h + 2, :]).then_inc(S["stored"], 16)
            sp.wait_ge(S["stored"], 16 * CHUNKS * PAIRS)

        @block.scalar
        def _(act):
            act.wait_ge(S["bias_ready"], 2)
            for k in range(3):
                act.dma_start(bias_rows[k:k + 1, :].rearrange("o (r f) -> o r f", f=P), bias_part[:, k, :]).then_inc(S["bias_sent"], 16)
                act.dma_start(b2_rows[k:k + 1, :].rearrange("o (r f) -> o r f", f=P), b2_part[:, k, :]).then_inc(S["bias_sent"], 16)

            def xst_copy(j, v, first):
                act.wait_ge(S["xst_psum"], j + 1)
                if not first:
                    act.wait_ge(S["h_psum"], j - 1)
                act.activation(xst[:, v, :], bank_x[v][:, 0:P], ACT.Copy).then_inc(S["xst_done"], 1)

            def step(j, u, it, first, last):
                if first and u == 0:
                    xst_copy(0, 0, True)
                if not (last and u == U - 1):
                    xst_copy(j + 1, (u + 1) % 2, first and u < 1)
                act.wait_ge(S["h_psum"], j + 1)
                if not (first and u < 2):
                    act.wait_ge(S["gated_done"], j - 1)
                act.activation(silu[:, u % 2, :], bank_h[u % 2][:, 0:HID], ACT.Silu).then_inc(S["silu_done"], 1)

            over_blocks(act, step)

        @block.vector
        def _(dve):
            n = [0]

            def then(instruction):
                n[0] += 1
                instruction.then_inc(S["chain"], 1)
                dve.wait_ge(S["chain"], n[0])

            dve.wait_ge(S["consts"], 1)
            then(dve.tensor_tensor(count[:, :], base[:, 0, :], region[:, :], ALU.subtract))
            dve.tensor_scalar(pad_at[:, :], base[:, 0, :], channel[:, 0:1], None, ALU.add).then_inc(S["table_ready"], 1)
            then(dve.tensor_tensor(more[:, :, :], spread(count[:, :], 2, NTHR), spread(threshold[:, :], 1, E), ALU.is_gt))
            then(dve.reduce_sum(nblk[:, :], more[:, :, :], AX.X))
            then(dve.tensor_tensor(upto[:, :, :], spread(iota8[:, :], 2, E), spread(iota8[:, :], 1, E), ALU.is_ge))
            then(dve.tensor_tensor(cumt[:, :, :], upto[:, :, :], spread(nblk[:, :], 1, E), ALU.mult))
            then(dve.reduce_sum(cum[:, :], cumt[:, :, :], AX.X))
            then(dve.tensor_tensor(cum_before[:, :], cum[:, :], nblk[:, :], ALU.subtract))
            then(dve.scalar_tensor_tensor(offset[:, :], cum_before[:, :], -float(P), region[:, :], ALU.mult, ALU.add))
            then(dve.tensor_tensor(past[:, :, :], spread(block_no[:, :], 2, E), spread(cum[:, :], 1, NB), ALU.is_ge))
            then(dve.reduce_sum(expert[:, :], past[:, :, :], AX.X))
            then(dve.tensor_tensor(mine[:, :, :], spread(expert[:, :], 2, E), spread(iota8[:, :], 1, NB), ALU.is_equal))
            then(dve.reduce_sum(used[:, :], mine[:, :, :], AX.X))
            then(dve.tensor_tensor(offs[:, :, :], mine[:, :, :], spread(offset[:, :], 1, NB), ALU.mult))
            then(dve.reduce_sum(start[:, :], offs[:, :, :], AX.X))
            then(dve.tensor_tensor(ujz[:, :], used[:, :], jz[:, :], ALU.mult))
            then(dve.tensor_tensor(start2[:, :], start[:, :], ujz[:, :], ALU.add))
            dve.tensor_scalar(table[:, 0, :], start2[:, :], float(ZERO), None, ALU.add)
            dve.tensor_scalar(table[:, 1, :], expert[:, :], float(E - 1), None, ALU.min).then_inc(S["table_ready"], 1)

            for full, rest, part in ((bias_full, bias_rest, bias_part), (b2, b2_rest, b2_part)):
                if full is bias_full:
                    dve.wait_ge(S["bias_psum"], 1)
                    then(dve.tensor_copy(full[:, :], bank_x[0][0:4 * E, 0:P]))
                then(dve.tensor_copy(part[:, 0, :], full[:, :]))
                then(dve.tensor_tensor(rest[:, 0, :], full[:, :], part[:, 0, :], ALU.subtract))
                then(dve.tensor_copy(part[:, 1, :], rest[:, 0, :]))
                then(dve.tensor_tensor(rest[:, 1, :], rest[:, 0, :], part[:, 1, :], ALU.subtract))
                dve.tensor_copy(part[:, 2, :], rest[:, 1, :]).then_inc(S["bias_ready"], 1)

            def gatedt_copy(j, v, early):
                dve.wait_ge(S["gt_psum"], j + 1)
                if not early:
                    dve.wait_ge(S["y_psum"], j - 1)
                dve.tensor_copy(gatedt[:, v, :], bank_g[v][:, 0:HID]).then_inc(S["gt_done"], 1)

            def scale(j, u, it, early, first_use):
                dve.wait_ge(S["y_psum"], j + 1)
                if not first_use:
                    dve.wait_ge(ys_sent[u], 16 * it)
                dve.tensor_scalar(ys[:, u, :], bank_y[u % 2][:, 0:C], xs[:, u, C:C + 1], None, ALU.mult).then_inc(S["ys_done"], 1)

            def step(j, u, it, first, last):
                if not (first and u < 1):
                    gatedt_copy(j - 1, (u - 1) % 2, first and u < 3)
                dve.wait_ge(S["silu_done"], j + 1)
                if not (first and u < 2):
                    dve.wait_ge(S["gt_psum"], j - 1)
                dve.tensor_tensor(gated[:, u % 2, :], bank_h[u % 2][:, HID:2 * HID], silu[:, u % 2, :], ALU.mult).then_inc(S["gated_done"], 1)
                if not (first and u < 2):
                    scale(j - 2, (u - 2) % U, it if u >= 2 else it - 1, False, first or (it == 1 if isinstance(it, int) else False) and u < 2)

            turns = NB // U

            def steps(it, first, last):
                for u in range(U):
                    step(it * U + u, u, it, first, last)

            steps(0, True, False)
            steps(1, False, False)
            with dve.Fori(2, turns - 1) as it:
                steps(it, False, False)
            steps(turns - 1, False, True)
            gatedt_copy(NB - 1, 1, False)
            scale(NB - 2, U - 2, turns - 1, False, False)
            scale(NB - 1, U - 1, turns - 1, False, False)

            for p in range(PAIRS):
                dve.wait_ge(y_loaded[p], 16 * 2 * CHUNKS)
                dve.tensor_tensor(t2[:, p, :, :], t2[:, p, :, :], y_first[:, p, :, :], ALU.add).then_inc(S["sum1_done"], 1)
                dve.wait_ge(S["sum1_done"], p + 1)
                dve.tensor_tensor(y_second[:, p, :, :], t2[:, p, :, :], y_second[:, p, :, :], ALU.add).then_inc(S["sum_done"], 1)

        @block.tensor
        def _(pe):
            pe.transpose(bank_x[0][0:4 * E, 0:P], bias_col[:, :], ident).then_inc(S["bias_psum"], 1)
            pe.wait_ge(S["bias_ready"], 1)
            pe.wait_ge(S["bias_sent"], 16 * 6)
            pe.wait_ge(S["table_ready"], 2)

            def x_transpose(j, u, it, early):
                pe.wait_ge(xs_loaded[u], 16 * (it + 1))
                if not early:
                    pe.wait_ge(S["xst_done"], j - 1)
                pe.transpose(bank_x[u % 2][:, 0:P], xs[:, u, 0:C], ident).then_inc(S["xst_psum"], 1)

            def hidden(j, u, early):
                e = pe.value_load(table[0:1, 1, bass.ds(j, 1)], min_val=0, max_val=E - 1)
                if not early:
                    pe.wait_ge(S["gated_done"], j - 1)
                pe.matmul(bank_h[u % 2][:, :], ones[0:3, :], bias_rows[:, bass.ds(e * (2 * HID), 2 * HID)], start=True, stop=False)
                pe.wait_ge(S["xst_done"], j + 1)
                pe.matmul(bank_h[u % 2][:, :], xst[:, u % 2, :], w_all[:, bass.ds(e * (2 * HID), 2 * HID)], start=False, stop=True).then_inc(S["h_psum"], 1)

            def gated_transpose(j, v, early):
                pe.wait_ge(S["gated_done"], j + 1)
                if not early:
                    pe.wait_ge(S["gt_done"], j - 1)
                for h in range(2):
                    last = pe.transpose(bank_g[v][:, h * P:(h + 1) * P], gated[:, v, h * P:(h + 1) * P], ident)
                last.then_inc(S["gt_psum"], 1)

            def down(j, v, early):
                e = pe.value_load(table[0:1, 1, bass.ds(j, 1)], min_val=0, max_val=E - 1)
                if not early:
                    pe.wait_ge(S["ys_done"], j - 1)
                pe.matmul(bank_y[v][:, 0:C], ones[0:3, :], b2_rows[:, bass.ds(e * C, C)], start=True, stop=False)
                pe.wait_ge(S["gt_done"], j + 1)
                for h in range(2):
                    last = pe.matmul(bank_y[v][:, 0:C], gatedt[:, v, h * P:(h + 1) * P], w2_all[:, bass.ds(e * (2 * C) + h * C, C)],
                                     start=False, stop=(h == 1))
                last.then_inc(S["y_psum"], 1)

            def step(j, u, it, first, last):
                if first and u == 0:
                    x_transpose(0, 0, 0, True)
                if not (last and u == U - 1):
                    x_transpose(j + 1, (u + 1) % U, it if u < U - 1 else it + 1, first and u < 1)
                hidden(j, u, first and u < 2)
                if not (first and u < 1):
                    gated_transpose(j - 1, (u - 1) % 2, first and u < 3)
                if not (first and u < 2):
                    down(j - 2, u % 2, first and u < 4)

            over_blocks(pe, step)
            gated_transpose(NB - 1, (NB - 1) % 2, False)
            down(NB - 2, NB % 2, False)
            down(NB - 1, (NB - 1) % 2, False)


def kernel(**inputs):
    import concourse.bacc as bacc
    from concourse.bass_utils import run_bass_kernel_spmd

    f = {k: np.asarray(v) for k, v in inputs.items()}
    x = f["x"].reshape(BATCH, C, HW)
    small = np.zeros((P, 428), np.float32)
    small[:, 0:KK] = f["L0_conv_K_w"].T
    small[:, 64:192] = f["L0_conv_conv0_w"].T
    small[:, 192:320] = f["L0_conv_conv1_w"].T
    small[:, 320:328] = f["L1_ffn_router_w"]
    small[:, 328:377] = f["L0_conv_ln_w"].reshape(C, KK)
    small[:, 377:426] = f["L0_conv_ln_b"].reshape(C, KK)
    small[0:KK, 426] = f["L0_conv_K_b"]
    small[KKP:KKP + KK, 426] = f["L0_conv_K_b"]
    small[:, 427] = f["L0_conv_conv0_b"]
    bgv = np.concatenate([f["L1_ffn_bg"].reshape(EXPERTS, 2, P), f["L1_ffn_bv"].reshape(EXPERTS, 2, P)], 1)
    const = constants()
    arrays = {
        "x": x,
        "xt": x.reshape(PAIRS, 2, C, CHUNKS, P).transpose(4, 0, 3, 1, 2).reshape(P, PAIRS, TILES, C),
        "const": np.concatenate([const[n] for n in WIDTHS], 1).astype(np.float32),
        "small": small,
        "c1_b": f["L0_conv_conv1_b"],
        "router_b": f["L1_ffn_router_b"],
        "w1t": f["L1_ffn_w1"].transpose(0, 2, 1),
        "wg": f["L1_ffn_wg"],
        "wv": f["L1_ffn_wv"],
        "b1c": f["L1_ffn_b1"].reshape(EXPERTS * 2, P).T,
        "bgv": bgv.reshape(EXPERTS * 4, P).T,
        "w2": f["L1_ffn_w2"].reshape(EXPERTS * 2, P, C).transpose(1, 0, 2).reshape(P, EXPERTS * 2 * C),
        "b2": f["L1_ffn_b2"],
    }
    arrays = {k: np.ascontiguousarray(v) for k, v in arrays.items()}
    nc = bacc.Bacc("TRN2", target_bir_lowering=False, num_devices=1)
    aps = {k: nc.dram_tensor("in_" + k, v.shape, mybir.dt.from_np(v.dtype), kind="ExternalInput").ap() for k, v in arrays.items()}
    out = nc.dram_tensor("out", (TOKENS, C), F32, kind="ExternalOutput").ap()
    build(nc, aps, out)
    got = run_bass_kernel_spmd(nc, [{"in_" + k: v for k, v in arrays.items()}], core_ids=[0]).results[0]["out"]
    return got.reshape(BATCH, HW, C).transpose(0, 2, 1).reshape(BATCH, C, SIDE_IN, SIDE_IN)
```

```python
from contextlib import ExitStack

import numpy as np

import concourse.bass as bass
from concourse import mybir

F32 = mybir.dt.float32
BF16 = mybir.dt.bfloat16
F32R = mybir.dt.float32r
U32 = mybir.dt.uint32
I32 = mybir.dt.int32
ALU = mybir.AluOpType
ACT = mybir.ActivationFunctionType
AX = mybir.AxisListType

P = 128
BATCH, C, SIDE_IN, TAPS = 16, 128, 16, 7
HW = SIDE_IN * SIDE_IN
KK = TAPS * TAPS
KKP = 64
GROUP = C // 32
PAIRS = BATCH // 2
CHUNKS = HW // P
TILES = 2 * CHUNKS
PAIR_TOKENS = 2 * HW
TOKENS = BATCH * HW
EXPERTS, HID = 8, 256
EPS = 1e-5

PAD = TAPS // 2
SIDE = SIDE_IN + PAD
FREQS = (SIDE * SIDE + 1) // 2
WIDE = 121
REST = FREQS - WIDE
IM_ROW = 64
BOTH = IM_ROW + REST

REGION = TOKENS + P
ROWS = EXPERTS * REGION + P
ROW = C + 4
UNROLL = 12
BLOCKS = -(-(2 * TOKENS // P + EXPERTS - 1) // UNROLL) * UNROLL
SKIP = 1 << 20


def constants():
    k = np.arange(P)
    ident = np.eye(P)
    group = (k[:, None] // GROUP == k[None, :] // GROUP) / GROUP
    mean = np.full((P, P), 1.0 / (C * KK))
    before = (k[:, None] < k[None, :]).astype(np.float64)

    freq = [(0, 0)] + [(u, v) for u in range(SIDE) for v in range(SIDE)
                       if (u, v) < ((-u) % SIDE, (-v) % SIDE)]
    u, v = np.array(freq).T
    pos = np.arange(HW)
    angle = 2 * np.pi / SIDE * (np.outer(pos // SIDE_IN, u) + np.outer(pos % SIDE_IN, v))
    tap = np.arange(KK)
    shift = 2 * np.pi / SIDE * (np.outer(PAD - tap // TAPS, u) + np.outer(PAD - tap % TAPS, v))
    weight = np.where(np.arange(FREQS) == 0, 1.0, 2.0) / SIDE ** 2

    def both(top, bottom):
        gap = np.zeros((top.shape[0], IM_ROW - REST))
        return np.concatenate([top[:, WIDE:], gap, bottom[:, WIDE:]], 1)

    re, im = np.cos(angle), -np.sin(angle)
    fwd = np.concatenate([re[:, :WIDE], im[:, :WIDE], both(re, im)], 1)
    fwd = fwd.reshape(CHUNKS, P, -1).transpose(1, 0, 2).reshape(P, -1)
    re, im = np.cos(shift), -np.sin(shift)
    tapf = np.zeros((P, 2 * WIDE + 2 * BOTH))
    tapf[:KK] = np.concatenate([re[:, :WIDE], im[:, :WIDE], both(re, im), both(im, re)], 1)
    re, im = np.cos(angle) * weight, -np.sin(angle) * weight
    inv = np.zeros((P, 4, HW))
    inv[:WIDE, 0], inv[:WIDE, 1] = re[:, :WIDE].T, im[:, :WIDE].T
    inv[:BOTH, 2], inv[:BOTH, 3] = both(re, -re).T, both(im, im).T
    return {"ident": ident, "group": group, "mean": mean, "before": before,
            "fwd": fwd, "tapf": tapf, "inv": inv.reshape(P, -1)}


WIDTHS = {"ident": P, "group": P, "mean": P, "before": P, "fwd": CHUNKS * (2 * WIDE + BOTH),
          "tapf": 2 * WIDE + 2 * BOTH, "inv": 4 * HW}
STARTS = dict(zip(WIDTHS, np.cumsum([0] + list(WIDTHS.values())).tolist()))
CONST_COLS = sum(WIDTHS.values())


def spread(ap, axis, n):
    ap = ap.unsqueeze(axis)
    shape = list(ap.shape)
    shape[axis] = n
    return ap.broadcast_to(shape)


def build(nc, a_in, out):
    ctx = ExitStack()

    def sb(name, shape, dt=F32):
        return ctx.enter_context(nc.sbuf_tensor(name, shape, dt))

    def sem(name):
        return ctx.enter_context(nc.semaphore(name))

    with ctx:
        rows_dram = nc.dram_tensor("rows_dram", (ROWS, ROW), F32, kind="Internal").ap()
        moe_dram = nc.dram_tensor("moe_dram", (2 * TOKENS, C), F32, kind="Internal").ap()

        const = sb("const", [P, CONST_COLS])

        def cst(name):
            return const[:, STARTS[name]:STARTS[name] + WIDTHS[name]]

        ident, group_avg, mean_all = cst("ident"), cst("group"), cst("mean")
        fwd = cst("fwd").rearrange("p (h f) -> p h f", h=CHUNKS)
        tapf = cst("tapf")
        tile_cols = (slice(0, WIDE), slice(WIDE, 2 * WIDE), slice(2 * WIDE, 2 * WIDE + BOTH),
                     slice(2 * WIDE + BOTH, 2 * WIDE + 2 * BOTH))
        tile_rows = (WIDE, WIDE, BOTH, BOTH)
        inv = cst("inv").rearrange("p (r n) -> p r n", r=4)
        before = sb("before", [P, P], BF16)
        ones = sb("ones", [P, P], BF16)
        small = sb("small", [P, a_in["small"].shape[1]])
        kw_t, c0_t, c1_t = small[:, 0:KKP], small[:, 64:192], small[:, 192:320]
        router_w, ln_w, ln_b = small[:, 320:328], small[:, 328:377], small[:, 377:426]
        key_b, c0_b = small[:, 426:427], small[:, 427:428]
        c1_b = sb("c1_b", [KK, C])
        router_b = sb("router_b", [P, EXPERTS])
        w1t = sb("w1t", [P, 2, 2, C])
        wgv = sb("wgv", [P, 2, 2, 2 * HID])
        b1c = sb("b1c", [P, EXPERTS * 2])
        bgv = sb("bgv", [P, EXPERTS * 4])
        w_high = sb("w_high", [P, EXPERTS * 2 * HID], F32R)
        w_low = sb("w_low", [P, EXPERTS * 2 * HID], F32R)
        w2_all = sb("w2_all", [P, EXPERTS * 2 * C])
        b2 = sb("b2", [EXPERTS, C])

        xc = sb("xc", [P, 2, PAIR_TOKENS])
        xt = sb("xt", [P, PAIRS, TILES, C])
        gn_raw = sb("gn_raw", [P, 2, 2, 6])
        gn_mv = sb("gn_mv", [P, 2, 2, 2])
        gn_mean = sb("gn_mean", [P, 2, 2])
        gn_dev = sb("gn_dev", [P, 2])
        gn_sq = sb("gn_sq", [P, 2])
        gn_e2 = sb("gn_e2", [P, 2])
        gn_var = sb("gn_var", [P, 2])
        gn_rstd = sb("gn_rstd", [P, 2, 2])
        gbuf = sb("gbuf", [P, 2, PAIR_TOKENS])
        gt = sb("gt", [P, 2, CHUNKS, 2 * C])
        kmax = sb("kmax", [P, 1])
        ksum_b = sb("ksum_b", [P, 1])
        kshift = sb("kshift", [P, 1])
        kexp = sb("kexp", [P, HW])
        ktot = sb("ktot", [P, 1])
        krec = sb("krec", [P, 1])
        kprob = sb("kprob", [P, HW])
        pt = sb("pt", [P, CHUNKS, 2 * KKP])
        fraw = sb("fraw", [P, 2, 2, KK])
        f0 = sb("f0", [P, 2, KK])
        fsum = sb("fsum", [P, 2])
        fcen = sb("fcen", [P, 2, KK])
        fsq = sb("fsq", [P, 2, KK])
        fsqs = sb("fsqs", [P, 2])
        fvar = sb("fvar", [P, 2])
        frstd = sb("frstd", [P, 2])
        flw = sb("flw", [P, 2, KK])
        fln = sb("fln", [P, 2, KK])
        frelu = sb("frelu", [P, 2, KK])
        filt = sb("filt", [KK, 2, C])
        ghat = sb("ghat", [P, 2, 3, 2 * C])
        prod = sb("prod", [WIDE, 4, 2 * C])
        zhat = sb("zhat", [P, 4, 2 * C])
        t1 = sb("t1", [P, 2, TILES, C])
        ln_raw = sb("ln_raw", [P, TILES, 6])
        ln_mv = sb("ln_mv", [P, TILES, 2])
        ln_var = sb("ln_var", [P, TILES])
        ln_rstd = sb("ln_rstd", [P, TILES])
        z = sb("z", [P, 2, TILES, C])
        qt = sb("qt", [P, PAIR_TOKENS])
        e_attn = sb("e_attn", [P, 2, CHUNKS, HW])
        asum = sb("asum", [P, 2, CHUNKS])
        arec = sb("arec", [P, 2, CHUNKS])
        t2 = sb("t2", [P, PAIRS, TILES, C])
        ln2_raw = sb("ln2_raw", [P, TILES, 6])
        ln2_mv = sb("ln2_mv", [P, TILES, 2])
        ln2_var = sb("ln2_var", [P, TILES])
        ln2_rstd = sb("ln2_rstd", [P, TILES])
        row = sb("row", [P, 2, TILES, 2, ROW])
        z2t = sb("z2t", [P, PAIR_TOKENS])
        minus_half = sb("minus_half", [P, TILES])

        iota8 = sb("iota8", [P, EXPERTS])
        dest = sb("dest", [P, PAIRS, TILES, 2], U32)
        logits = sb("logits", [P, TILES, EXPERTS])
        sorted8 = sb("sorted8", [P, TILES, 8])
        index8 = sb("index8", [P, TILES, 8], U32)
        lshift = sb("lshift", [P, TILES, 8])
        lexp = sb("lexp", [P, TILES, 8])
        lsum = sb("lsum", [P, TILES])
        lrec = sb("lrec", [P, TILES])
        chosen = sb("chosen", [P, TILES, 2, EXPERTS])
        either = sb("either", [P, TILES, EXPERTS], BF16)
        base = sb("base", [P, 2, EXPERTS])
        pos = sb("pos", [P, TILES, EXPERTS])
        posk = sb("posk", [P, TILES, 2, EXPERTS])
        slotf = sb("slotf", [P, TILES * 2])
        slot = sb("slot", [P, 2, TILES * 2], U32)

        banks = [ctx.enter_context(nc.psum_tensor(f"bank{i}", [P, 512], F32)) for i in range(8)]
        bank_k, bank_t, bank_b, bank_o, bank_s0, bank_s1, bank_d0, bank_d1 = banks
        bank_s = (bank_s0, bank_s1)
        bank_d = (bank_d0, bank_d1)

        ld_x = [sem("ld_x0"), sem("ld_x1")]
        ld_c1 = sem("ld_c1")
        ld_c2 = sem("ld_c2")
        ld_xt = [sem("ld_xt0"), sem("ld_xt1")]
        ld_w = [sem("ld_w0"), sem("ld_w1")]
        ld_bias = sem("ld_bias")
        ld_c1b, ld_router = sem("ld_c1b"), sem("ld_router")
        ld_w2 = sem("ld_w2")
        const_ready = sem("const_ready")
        iota_ready = sem("iota_ready")
        gn_step = sem("gn_step")
        gn_mv_done, gn_avg, gn_e2_done = sem("gn_mv_done"), sem("gn_avg"), sem("gn_e2_done")
        gn_avg2, gn_var_done, gn_rstd_done, g_done = sem("gn_avg2"), sem("gn_var_done"), sem("gn_rstd_done"), sem("g_done")
        wmul_psum, whigh_done, wlow_done = sem("wmul_psum"), sem("whigh_done"), sem("wlow_done")
        wbias_psum, wbias_done = sem("wbias_psum"), sem("wbias_done")
        keys_done, gt_psum, gt_done = sem("keys_done"), sem("gt_psum"), sem("gt_done")
        key_step = sem("key_step")
        kshift_done, kexp_done, krec_done, kprob_done = sem("kshift_done"), sem("kexp_done"), sem("krec_done"), sem("kprob_done")
        pt_psum, pt_done, fraw_psum, fraw_done = sem("pt_psum"), sem("pt_done"), sem("fraw_psum"), sem("fraw_done")
        conv0_psum, f0_done, fmean_psum, fcen_done = sem("conv0_psum"), sem("f0_done"), sem("fmean_psum"), sem("fcen_done")
        fsqs_done, fvar_psum, fvar_done, frstd_done = sem("fsqs_done"), sem("fvar_psum"), sem("fvar_done"), sem("frstd_done")
        flw_done, fln_done, frelu_done = sem("flw_done"), sem("fln_done"), sem("frelu_done")
        filt_psum, filt_done = sem("filt_psum"), sem("filt_done")
        ghat_psum, ghat_done = sem("ghat_psum"), sem("ghat_done")
        what_psum, zhat_done = sem("what_psum"), sem("zhat_done")
        prod_done = sem("prod_done")
        conv_psum, t1_done = sem("conv_psum"), sem("t1_done")
        ln_step = sem("ln_step")
        ln_var_done, ln_rstd_done = sem("ln_var_done"), sem("ln_rstd_done")
        z_done, zt_psum, qt_done = sem("z_done"), sem("zt_psum"), sem("qt_done")
        score_psum, e_done = sem("score_psum"), sem("e_done")
        arec_done, attn_psum, t2_done = sem("arec_done"), sem("attn_psum"), sem("t2_done")
        ln2_step = sem("ln2_step")
        ln2_var_done, ln2_rstd_done = sem("ln2_var_done"), sem("ln2_rstd_done")
        z2_done, row2_done, z2t_psum, z2t_done = sem("z2_done"), sem("row2_done"), sem("z2t_psum"), sem("z2t_done")
        logit_psum, logits_done = sem("logit_psum"), sem("logits_done")
        route_step = sem("route_step")
        lshift_done, lexp_done, either_done = sem("lshift_done"), sem("lexp_done"), sem("either_done")
        rank_psum, base_done, pos_done, row_done = sem("rank_psum"), sem("base_done"), sem("pos_done"), sem("row_done")
        sent = [sem("sent0"), sem("sent1")]

        bias_col = sb("bias_col", [P, EXPERTS * 4])
        STAGES = 7
        rounds = PAIRS + STAGES - 1
        B2_ROUND = PAIRS + 3
        experts = expert_programs(sb, sem, out, dict(
            rows_dram=rows_dram, moe_dram=moe_dram, ident=ident, ones=ones, iota8=iota8, base=base, bias_col=bias_col,
            b2=b2, w_high=w_high, w_low=w_low, w2_all=w2_all, t2=t2, first=xt, banks=banks, sent=sent, ld_w2=ld_w2,
            minus_half=minus_half, base_done=base_done, iota_ready=iota_ready, wbias_done=wbias_done, z2t_done=z2t_done))

        def stages(i):
            return [p if 0 <= p < PAIRS else None for p in range(i, i - STAGES, -1)]

        def through(i, stage):
            return min(max(i - stage + 1, 0), PAIRS)

        N, A, B, D, E = 0, 1, 2, 4, 5
        CC = 3
        expert_rounds = [1, 2, 3, 4, 5, 6, PAIRS + 3, PAIRS + 4]

        def experts_through(i):
            return sum(r <= i for r in expert_rounds)

        def expert_in(i):
            return experts_through(i) - 1 if i in expert_rounds else None

        def after(eng, semaphore, count):
            if count > 0:
                eng.wait_ge(semaphore, count)

        with nc.Block() as block:
            @block.sync
            def _(sp):
                def load_x(p):
                    sp.dma_start(xc[:, p % 2, :].rearrange("c (b n) -> c b n", b=2),
                                 a_in["x"][2 * p:2 * p + 2].rearrange("b c n -> c b n")).then_inc(ld_x[p % 2], 16)

                def load_w(e):
                    sp.dma_start(wgv[:, e % 2, :, 0:HID],
                                 a_in["wg"][e].rearrange("(h p) f -> p h f", p=P)).then_inc(ld_w[e % 2], 16)
                    sp.dma_start(wgv[:, e % 2, :, HID:2 * HID],
                                 a_in["wv"][e].rearrange("(h p) f -> p h f", p=P)).then_inc(ld_w[e % 2], 16)
                    sp.dma_start(w1t[:, e % 2, :, :],
                                 a_in["w1t"][e].rearrange("(h p) d -> p h d", p=P)).then_inc(ld_w[e % 2], 16)

                load_x(0)
                sp.dma_start(const[:, 0:STARTS["fwd"]], a_in["const"][:, 0:STARTS["fwd"]]).then_inc(ld_c1, 16)
                sp.dma_start(small[:, :], a_in["small"]).then_inc(ld_c1, 16)
                load_x(1)
                load_w(0)
                sp.dma_start(const[:, STARTS["fwd"]:CONST_COLS], a_in["const"][:, STARTS["fwd"]:CONST_COLS]).then_inc(ld_c2, 16)
                load_w(1)
                def reload_w(x):
                    sp.wait_ge(wbias_psum, x - 1)
                    load_w(x)

                for p in range(2, PAIRS):
                    sp.wait_ge(g_done, p - 1)
                    load_x(p)
                    if p < EXPERTS - 1:
                        reload_w(p)
                    if p < 2 + PAIRS // 2:
                        sp.dma_start(xt[:, 2 * p - 4:2 * p - 2], a_in["xt"][:, 2 * p - 4:2 * p - 2]).then_inc(ld_xt[p % 2], 16)
                sp.dma_start(w2_all[:, :], a_in["w2"]).then_inc(ld_w2, 16)
                reload_w(EXPERTS - 1)
                experts["sync"](sp)

            @block.gpsimd
            def _(pool):
                pool.memset(minus_half[:, :], -0.5)
                pool.memset(row[:, :, :, :, C:ROW], 0.0)
                pool.iota(iota8[:, :], pattern=[[1, EXPERTS]], base=0, channel_multiplier=0,
                          allow_small_or_imprecise_dtypes=True).then_inc(iota_ready, 1)
                pool.iota(base[:, 0, :], pattern=[[REGION, EXPERTS]], base=0, channel_multiplier=0,
                          allow_small_or_imprecise_dtypes=True).then_inc(iota_ready, 1)
                pool.iota(dest[:, :, :, :], pattern=[[TILES, PAIRS], [1, TILES], [TOKENS, 2]],
                          base=0, channel_multiplier=PAIRS * TILES).then_inc(iota_ready, 1)
                pool.wait_ge(iota_ready, 3)
                experts["constants"](pool)

                def dispatch(f, tiles):
                    for t in tiles:
                        for k in range(2):
                            pool.indirect_dma_start(
                                rows_dram, bass.IndirectOffsetOnAxis(ap=slot[:, f % 2, 2 * t + k:2 * t + k + 1], axis=0),
                                row[:, f % 2, t, k, :], None).then_inc(sent[f % 2], 16)

                for i in range(rounds):
                    n, a, b, c, d, e, f = stages(i)
                    if f is not None:
                        pool.wait_ge(row_done, f + 1)
                        pool.wait_ge(row2_done, f + 1)
                        dispatch(f, range(0, TILES // 2))
                    if b is not None:
                        pool.wait_ge(fvar_done, b + 1)
                        pool.tensor_tensor(frstd[:, :], fvar[:, :], minus_half[:, 0:2], ALU.pow).then_inc(frstd_done, 1)
                    if f is not None:
                        dispatch(f, range(TILES // 2, TILES))
                    if n is not None:
                        pool.wait_ge(gn_var_done, n + 1)
                        after(pool, g_done, n - 1)
                        pool.tensor_tensor(gn_rstd[:, n % 2, :], gn_var[:, :], minus_half[:, 0:2], ALU.pow).then_inc(gn_rstd_done, 1)
                    if c is not None:
                        pool.wait_ge(ln_var_done, c + 1)
                        after(pool, z_done, c)
                        pool.tensor_tensor(ln_rstd[:, :], ln_var[:, :], minus_half[:, :], ALU.pow).then_inc(ln_rstd_done, 1)
                    if d is not None:
                        pool.wait_ge(ln2_var_done, d + 1)
                        after(pool, z2_done, d)
                        pool.tensor_tensor(ln2_rstd[:, :], ln2_var[:, :], minus_half[:, :], ALU.pow).then_inc(ln2_rstd_done, 1)
                experts["gpsimd"](pool)

            @block.scalar
            def _(act):
                act.dma_start(b1c[:, :], a_in["b1c"]).then_inc(ld_bias, 16)
                act.dma_start(bgv[:, :], a_in["bgv"]).then_inc(ld_bias, 16)
                act.dma_start(c1_b[:, :], a_in["c1_b"].partition_broadcast(KK)).then_inc(ld_c1b, 16)
                act.dma_start(router_b[:, :], a_in["router_b"].partition_broadcast(P)).then_inc(ld_router, 16)
                act.dma_start(b2[:, :], a_in["b2"]).then_inc(ld_w2, 16)
                act.wait_ge(ld_c1, 32)

                def router_input(e):
                    act.wait_ge(z2t_psum, e + 1)
                    after(act, logit_psum, e)
                    act.activation(z2t[:, :], bank_t[:, :], ACT.Copy).then_inc(z2t_done, 1)
                    act.activation(row[:, e % 2, :, 1, 0:C], row[:, e % 2, :, 0, 0:C], ACT.Copy).then_inc(row2_done, 1)

                for i in range(rounds):
                    n, a, b, c, d, e, _ = stages(i)
                    x = expert_in(i)
                    if a is not None:
                        act.wait_ge(gt_psum, a + 1)
                        after(act, fraw_psum, a - 1)
                        after(act, ghat_psum, 2 * (a - 1))
                        act.activation(gt[:, a % 2, :, :].rearrange("p h c -> p (h c)"), bank_t[:, :], ACT.Copy).then_inc(gt_done, 1)
                    if x is not None and c is None and a is not None:
                        act.wait_ge(wmul_psum, x + 1)
                        act.activation(w_high[:, x * 2 * HID:(x + 1) * 2 * HID], bank_d0[:, :], ACT.Copy).then_inc(whigh_done, 1)
                    if b is not None:
                        act.wait_ge(conv0_psum, b + 1)
                        after(act, fcen_done, b)
                        after(act, fmean_psum, b)
                        for s in range(2):
                            last = act.activation(f0[:, s, :], bank_b[:, s * KK:(s + 1) * KK], ACT.Identity, bias=c0_b,
                                                  accum_out=fsum[:, s:s + 1])
                        last.then_inc(f0_done, 1)
                    if b is not None:
                        act.wait_ge(ghat_psum, 2 * b + 1)
                        after(act, zhat_done, 2 * (b - 1))
                        act.activation(ghat[0:WIDE, b % 2, 0:2, :].rearrange("p r c -> p (r c)"), bank_s0[0:WIDE, :], ACT.Copy).then_inc(ghat_done, 1)
                    if b is not None:
                        act.wait_ge(ghat_psum, 2 * b + 2)
                        act.activation(ghat[0:BOTH, b % 2, 2, :], bank_s1[0:BOTH, 0:2 * C], ACT.Copy).then_inc(ghat_done, 1)
                    if d is not None:
                        act.wait_ge(zt_psum, d + 1)
                        after(act, score_psum, 2 * d)
                        act.activation(qt[:, :], bank_t[:, :], ACT.Tanh).then_inc(qt_done, 1)
                    if b is not None:
                        act.wait_ge(fcen_done, b + 1)
                        after(act, fvar_psum, b)
                        for s in range(2):
                            last = act.activation(fsq[:, s, :], fcen[:, s, :], ACT.Square, accum_out=fsqs[:, s:s + 1])
                        last.then_inc(fsqs_done, 1)
                    if a is not None:
                        act.wait_ge(kshift_done, a + 1)
                        after(act, kprob_done, a)
                        act.activation(kexp[:, :], bank_k[:, 0:HW], ACT.Exp, bias=kshift[:, 0:1], accum_out=ktot[:, 0:1]).then_inc(kexp_done, 1)
                    if e is not None and b is not None:
                        router_input(e)
                    if d is not None:
                        after(act, attn_psum, d)
                        after(act, arec_done, d)
                        for s in range(2):
                            act.wait_ge(score_psum, 2 * d + s + 1)
                            for h in range(CHUNKS):
                                act.activation(e_attn[:, s, h, :], bank_s[s][:, h * HW:(h + 1) * HW], ACT.Exp,
                                               scale=float(C) ** -0.5, accum_out=asum[:, s, h:h + 1]).then_inc(e_done, 1)
                    if e is not None and b is None:
                        router_input(e)
                    if e is not None:
                        act.wait_ge(lshift_done, e + 1)
                        after(act, row_done, e)
                        act.activation(lexp[:, :, :].rearrange("p t e -> p (t e)"),
                                       lshift[:, :, :].rearrange("p t e -> p (t e)"), ACT.Exp).then_inc(lexp_done, 1)
                    if a is not None:
                        act.wait_ge(pt_psum, a + 1)
                        after(act, fraw_psum, a)
                        act.activation(pt[:, :, :].rearrange("p h k -> p (h k)"), bank_k[:, HW:2 * HW], ACT.Copy).then_inc(pt_done, 1)
                    if x is not None and c is not None and a is not None:
                        act.wait_ge(wmul_psum, x + 1)
                        act.activation(w_high[:, x * 2 * HID:(x + 1) * 2 * HID], bank_d0[:, :], ACT.Copy).then_inc(whigh_done, 1)
                    if a is not None:
                        act.wait_ge(fraw_psum, a + 1)
                        after(act, conv0_psum, a - 1)
                        act.activation(fraw[:, a % 2, :, :], bank_k[:, 0:2 * KKP].rearrange("p (s k) -> p s k", s=2)[:, :, 0:KK],
                                       ACT.Copy).then_inc(fraw_done, 1)
                    if x is not None and a is None:
                        act.wait_ge(wmul_psum, x + 1)
                        act.activation(w_high[:, x * 2 * HID:(x + 1) * 2 * HID], bank_d0[:, :], ACT.Copy).then_inc(whigh_done, 1)
                experts["scalar"](act)

            @block.vector
            def _(dve):
                dve.memset(ones[:, :], 1.0)

                def layer_norm_stats(src, raw, mv, var, stats_step, var_done, p):
                    for t in range(TILES):
                        last = dve.bn_stats(raw[:, t, :], src[:, t, :])
                    last.then_inc(stats_step, 1)
                    dve.wait_ge(stats_step, 2 * p + 1)
                    for t in range(TILES):
                        last = dve.bn_aggr(mv[:, t, :], raw[:, t, :])
                    last.then_inc(stats_step, 1)
                    dve.wait_ge(stats_step, 2 * p + 2)
                    dve.tensor_scalar(var[:, :], mv[:, :, 1], EPS, None, ALU.add).then_inc(var_done, 1)

                def low_part(x):
                    columns = slice(x * 2 * HID, (x + 1) * 2 * HID)
                    dve.wait_ge(whigh_done, x + 1)
                    dve.tensor_tensor(w_low[:, columns], bank_d0[:, :], w_high[:, columns], ALU.subtract).then_inc(wlow_done, 1)

                def products(c):
                    g = ghat[0:WIDE, c % 2, 0:2, :]
                    w = bank_d0[0:WIDE, :].rearrange("p (r c) -> p r c", r=2)
                    dve.wait_ge(ghat_done, 2 * c + 1)
                    dve.wait_ge(what_psum, 2 * c + 1)
                    dve.tensor_tensor(prod[:, 0:2, :], w, g, ALU.mult)
                    dve.tensor_tensor(prod[:, 2, :], w[:, 0, :], g[:, 1, :], ALU.mult)
                    dve.tensor_tensor(prod[:, 3, :], w[:, 1, :], g[:, 0, :], ALU.mult).then_inc(prod_done, 1)

                def spectrum(c):
                    dve.wait_ge(prod_done, c + 1)
                    after(dve, conv_psum, c)
                    dve.tensor_tensor(zhat[0:WIDE, 0, :], prod[:, 0, :], prod[:, 1, :], ALU.subtract)
                    dve.tensor_tensor(zhat[0:WIDE, 1, :], prod[:, 2, :], prod[:, 3, :], ALU.add).then_inc(zhat_done, 1)

                def rest_products(c):
                    dve.wait_ge(ghat_done, 2 * c + 2)
                    dve.wait_ge(what_psum, 2 * c + 2)
                    dve.tensor_tensor(zhat[0:BOTH, 2:4, :], bank_d1[0:BOTH, :].rearrange("p (r c) -> p r c", r=2),
                                      spread(ghat[0:BOTH, c % 2, 2, :], 1, 2), ALU.mult).then_inc(zhat_done, 1)

                for i in range(rounds):
                    n, a, b, c, d, e, _ = stages(i)
                    x = expert_in(i)
                    if i == 1:
                        dve.wait_ge(ld_c1, 32)
                        dve.tensor_copy(before[:, :], cst("before")).then_inc(const_ready, 1)
                        experts["triangle"](dve)
                    if b is not None:
                        dve.wait_ge(fmean_psum, b + 1)
                        after(dve, fsqs_done, b)
                        dve.tensor_tensor(fcen[:, :, :], f0[:, :, :], spread(bank_b[:, 128:130], 2, KK), ALU.subtract).then_inc(fcen_done, 1)
                    if a is not None:
                        dve.wait_ge(keys_done, a + 1)
                        dve.reduce_max(kmax[:, :], bank_k[:, 0:HW], AX.X).then_inc(key_step, 1)
                    if e is not None:
                        dve.wait_ge(ln2_rstd_done, e + 1)
                        if e >= 2:
                            dve.wait_ge(sent[e % 2], 16 * 2 * TILES * (e // 2))
                        for t in range(TILES):
                            last = dve.tensor_scalar(row[:, e % 2, t, 0, 0:C], t2[:, e, t, :], ln2_mv[:, t, 0:1], ln2_rstd[:, t:t + 1],
                                                     ALU.subtract, ALU.mult)
                        last.then_inc(z2_done, 1)
                    if i == B2_ROUND:
                        experts["b2_parts"](dve)
                    if a is not None:
                        dve.wait_ge(key_step, 2 * a + 1)
                        dve.tensor_tensor(ksum_b[:, :], kmax[:, :], key_b, ALU.add).then_inc(key_step, 1)
                        dve.wait_ge(key_step, 2 * a + 2)
                        after(dve, kexp_done, a)
                        dve.tensor_tensor(kshift[:, :], key_b, ksum_b[:, :], ALU.subtract).then_inc(kshift_done, 1)
                    if c is not None:
                        products(c)
                    if b is not None:
                        dve.wait_ge(fcen_done, b + 1)
                        dve.tensor_tensor(flw[:, :, :], fcen[:, :, :], spread(ln_w, 1, 2), ALU.mult).then_inc(flw_done, 1)
                    if c is not None:
                        spectrum(c)
                    if a is not None:
                        dve.wait_ge(kexp_done, a + 1)
                        dve.reciprocal(krec[:, :], ktot[:, :]).then_inc(krec_done, 1)
                    if c is not None:
                        rest_products(c)
                    if n is not None:
                        dve.wait_ge(ld_x[n % 2], 16 * (n // 2 + 1))
                        for s in range(2):
                            last = dve.bn_stats(gn_raw[:, n % 2, s, :], xc[:, n % 2, s * HW:(s + 1) * HW])
                        last.then_inc(gn_step, 1)
                    if e is not None:
                        if e == 0:
                            dve.wait_ge(iota_ready, 3)
                            dve.wait_ge(ld_router, 16)
                        dve.wait_ge(logit_psum, e + 1)
                        dve.tensor_tensor(logits[:, :, :], bank_b[:, 0:32].rearrange("p (t e) -> p t e", t=TILES),
                                          spread(router_b[:, :], 1, TILES), ALU.add).then_inc(logits_done, 1)
                        dve.tensor_copy(row[:, e % 2, :, :, C + 1:C + 2].bitcast(U32), dest[:, e, :, :].rearrange("p t (k o) -> p t k o", o=1))
                    if a is not None:
                        dve.wait_ge(krec_done, a + 1)
                        after(dve, pt_psum, a)
                        dve.tensor_scalar(kprob[:, :], kexp[:, :], krec[:, 0:1], None, ALU.mult).then_inc(kprob_done, 1)
                    if e is not None:
                        dve.wait_ge(logits_done, e + 1)
                        for t in range(TILES):
                            last = dve.max(sorted8[:, t, :], logits[:, t, :])
                        last.then_inc(route_step, 1)
                    if e is not None:
                        dve.wait_ge(route_step, 7 * e + 1)
                        for t in range(TILES):
                            last = dve.max_index(index8[:, t, :], sorted8[:, t, :], logits[:, t, :])
                        last.then_inc(route_step, 1)
                        dve.tensor_tensor(lshift[:, :, :], sorted8[:, :, :], spread(sorted8[:, :, 0], 2, 8), ALU.subtract).then_inc(lshift_done, 1)
                    if n is not None:
                        dve.wait_ge(gn_step, 3 * n + 1)
                        for s in range(2):
                            last = dve.bn_aggr(gn_mv[:, n % 2, s, :], gn_raw[:, n % 2, s, :])
                        last.then_inc(gn_mv_done, 1)
                    if e is not None:
                        dve.wait_ge(route_step, 7 * e + 2)
                        for t in range(TILES):
                            last = dve.tensor_tensor(chosen[:, t, :, :], spread(iota8[:, :], 1, 2),
                                                     spread(index8[:, t, 0:2], 2, EXPERTS), ALU.is_equal)
                        last.then_inc(route_step, 1)
                    if b is not None:
                        dve.wait_ge(fvar_psum, b + 1)
                        dve.tensor_scalar(fvar[:, :], bank_b[:, 132:134], EPS, None, ALU.add).then_inc(fvar_done, 1)
                    if e is not None:
                        dve.wait_ge(route_step, 7 * e + 3)
                        dve.tensor_tensor(either[:, :, :], chosen[:, :, 0, :], chosen[:, :, 1, :], ALU.add).then_inc(either_done, 1)
                    if e is not None:
                        dve.wait_ge(lexp_done, e + 1)
                        dve.reduce_sum(lsum[:, :], lexp[:, :, :], AX.X).then_inc(route_step, 1)
                    if x is not None and a is not None:
                        low_part(x)
                    if n is not None:
                        dve.wait_ge(gn_avg, n + 1)
                        dve.tensor_tensor(gn_dev[:, :], gn_mv[:, n % 2, :, 0], bank_d1[:, 0:2], ALU.subtract).then_inc(gn_step, 1)
                        dve.tensor_copy(gn_mean[:, n % 2, :], bank_d1[:, 0:2])
                        dve.wait_ge(gn_step, 3 * n + 2)
                        dve.tensor_tensor(gn_sq[:, :], gn_dev[:, :], gn_dev[:, :], ALU.mult).then_inc(gn_step, 1)
                    if e is not None:
                        dve.wait_ge(route_step, 7 * e + 4)
                        dve.reciprocal(lrec[:, :], lsum[:, :]).then_inc(route_step, 1)
                    if n is not None:
                        dve.wait_ge(gn_step, 3 * n + 3)
                        dve.tensor_tensor(gn_e2[:, :], gn_sq[:, :], gn_mv[:, n % 2, :, 1], ALU.add).then_inc(gn_e2_done, 1)
                    if b is not None:
                        dve.wait_ge(frstd_done, b + 1)
                        dve.wait_ge(flw_done, b + 1)
                        for s in range(2):
                            last = dve.scalar_tensor_tensor(fln[:, s, :], flw[:, s, :], frstd[:, s:s + 1], ln_b, ALU.mult, ALU.add)
                        last.then_inc(fln_done, 1)
                    if e is not None:
                        dve.wait_ge(route_step, 7 * e + 5)
                        dve.tensor_tensor(row[:, e % 2, :, :, C], lexp[:, :, 0:2], spread(lrec[:, :], 2, 2), ALU.mult)
                    if b is not None:
                        dve.wait_ge(fln_done, b + 1)
                        dve.tensor_scalar(frelu[:, :, :], fln[:, :, :], 0.0, None, ALU.max).then_inc(frelu_done, 1)
                    if c is not None:
                        dve.wait_ge(conv_psum, c + 1)
                        after(dve, t2_done, c - 1)
                        dve.wait_ge(ld_xt[c // 2 % 2], 16 * (c // 4 + 1))
                        dve.tensor_tensor(t1[:, c % 2, :, :].rearrange("p t c -> p (t c)"), bank_o[:, :],
                                          xt[:, c, :, :].rearrange("p t c -> p (t c)"), ALU.add).then_inc(t1_done, 1)
                    if e is not None:
                        dve.wait_ge(rank_psum, e + 1)
                        after(dve, base_done, e)
                        dve.tensor_tensor(base[:, (e + 1) % 2, :], base[:, e % 2, :], bank_b[:, 96:96 + EXPERTS], ALU.add).then_inc(base_done, 1)
                        dve.tensor_tensor(pos[:, :, :], bank_b[:, 64:96].rearrange("p (t e) -> p t e", t=TILES),
                                          spread(base[:, e % 2, :], 1, TILES), ALU.add).then_inc(pos_done, 1)
                    if n is not None:
                        dve.wait_ge(gn_avg2, n + 1)
                        dve.tensor_scalar(gn_var[:, :], bank_d1[:, 4:6], EPS, None, ALU.add).then_inc(gn_var_done, 1)
                    if e is not None:
                        dve.wait_ge(pos_done, e + 1)
                        for k in range(2):
                            last = dve.tensor_tensor(posk[:, :, k, :], chosen[:, :, k, :], pos[:, :, :], ALU.mult)
                        last.then_inc(route_step, 1)
                    if c is not None:
                        dve.wait_ge(t1_done, c + 1)
                        layer_norm_stats(t1[:, c % 2], ln_raw, ln_mv, ln_var, ln_step, ln_var_done, c)
                    if n is not None:
                        dve.wait_ge(gn_rstd_done, n + 1)
                        after(dve, keys_done, n - 1)
                        after(dve, gt_psum, n - 1)
                        for s in range(2):
                            last = dve.tensor_scalar(gbuf[:, n % 2, s * HW:(s + 1) * HW], xc[:, n % 2, s * HW:(s + 1) * HW],
                                                     gn_mean[:, n % 2, s:s + 1], gn_rstd[:, n % 2, s:s + 1],
                                                     ALU.subtract, ALU.mult)
                        last.then_inc(g_done, 1)
                    if d is not None:
                        dve.wait_ge(e_done, 4 * (d + 1))
                        dve.reciprocal(arec[:, :, :], asum[:, :, :]).then_inc(arec_done, 1)
                    if e is not None:
                        dve.wait_ge(route_step, 7 * e + 6)
                        dve.reduce_sum(slotf[:, :], posk[:, :, :, :].rearrange("p t k e -> p (t k) e"), AX.X).then_inc(route_step, 1)
                    if b is not None:
                        if b == 0:
                            dve.wait_ge(ld_c1b, 16)
                        dve.wait_ge(filt_psum, b + 1)
                        after(dve, what_psum, 2 * b)
                        dve.tensor_tensor(filt[:, :, :], bank_b[0:KK, 256:512].rearrange("k (s c) -> k s c", s=2),
                                          spread(c1_b[:, :], 1, 2), ALU.add).then_inc(filt_done, 1)
                    if e is not None:
                        dve.wait_ge(route_step, 7 * e + 7)
                        dve.tensor_copy(slot[:, e % 2, :], slotf[:, :]).then_inc(row_done, 1)
                    if x is not None and a is not None:
                        if x == 0:
                            dve.wait_ge(ld_bias, 32)
                        dve.wait_ge(wbias_psum, x + 1)
                        dve.tensor_tensor(bias_col[:, 4 * x:4 * x + 4], bank_d1[:, 8:12], bgv[:, 4 * x:4 * x + 4], ALU.add).then_inc(wbias_done, 1)
                    if c is not None:
                        dve.wait_ge(ln_rstd_done, c + 1)
                        after(dve, attn_psum, c - 1)
                        for t in range(TILES):
                            last = dve.tensor_scalar(z[:, c % 2, t, :], t1[:, c % 2, t, :], ln_mv[:, t, 0:1], ln_rstd[:, t:t + 1],
                                                     ALU.subtract, ALU.mult)
                        last.then_inc(z_done, 1)
                    if d is not None:
                        dve.wait_ge(arec_done, d + 1)
                        dve.wait_ge(attn_psum, d + 1)
                        for t in range(TILES):
                            h, s = divmod(t, 2)
                            last = dve.scalar_tensor_tensor(t2[:, d, t, :], bank_o[:, t * C:(t + 1) * C], arec[:, s, h:h + 1],
                                                            t1[:, d % 2, t, :], ALU.mult, ALU.add)
                        last.then_inc(t2_done, 1)
                        dve.wait_ge(t2_done, d + 1)
                        layer_norm_stats(t2[:, d], ln2_raw, ln2_mv, ln2_var, ln2_step, ln2_var_done, d)
                    if e == PAIRS - 1:
                        experts["tables"](dve)
                    if x is not None and a is None:
                        low_part(x)
                    if x is not None and a is None:
                        if x == 0:
                            dve.wait_ge(ld_bias, 32)
                        dve.wait_ge(wbias_psum, x + 1)
                        dve.tensor_tensor(bias_col[:, 4 * x:4 * x + 4], bank_d1[:, 8:12], bgv[:, 4 * x:4 * x + 4], ALU.add).then_inc(wbias_done, 1)
                experts["vector"](dve)

            @block.tensor
            def _(pe):
                pe.wait_ge(ld_c1, 32)

                def features_spectrum(b, tiles):
                    for r in tiles:
                        for h in range(CHUNKS):
                            last = pe.matmul(bank_s[r // 2][0:tile_rows[r], r % 2 * 2 * C:(r % 2 + 1) * 2 * C],
                                             fwd[:, h, tile_cols[r]], gt[:, b % 2, h, :],
                                             start=(h == 0), stop=(h == CHUNKS - 1))
                    last.then_inc(ghat_psum, 1)

                def router_input(i, e):
                    pe.wait_ge(z2_done, e + 1)
                    after(pe, gt_done, through(i, A))
                    after(pe, qt_done, through(i, D))
                    for t in range(TILES):
                        last = pe.transpose(bank_t[:, t * P:(t + 1) * P], row[:, e % 2, t, 0, 0:C], ident)
                    last.then_inc(z2t_psum, 1)

                def router(i, e):
                    pe.wait_ge(z2t_done, e + 1)
                    after(pe, fcen_done, through(i, B))
                    after(pe, filt_done, through(i - 1, B))
                    after(pe, pos_done, e)
                    for t in range(TILES):
                        last = pe.matmul(bank_b[:, t * EXPERTS:(t + 1) * EXPERTS], z2t[:, t * P:(t + 1) * P], router_w, start=True, stop=True)
                    last.then_inc(logit_psum, 1)

                def features_of_z(i, d):
                    pe.wait_ge(z_done, d + 1)
                    after(pe, gt_done, through(i, A))
                    after(pe, z2t_done, through(i - 1, E))
                    after(pe, qt_done, d)
                    for t in range(TILES):
                        h, s = divmod(t, 2)
                        last = pe.transpose(bank_t[:, s * HW + h * P:s * HW + (h + 1) * P], z[:, d % 2, t, :], ident)
                    last.then_inc(zt_psum, 1)

                def expert_weights(i, x):
                    pe.wait_ge(ld_w[x % 2], 48 * (x // 2 + 1))
                    after(pe, prod_done, through(i, CC))
                    after(pe, wlow_done, x)
                    for h in range(2):
                        last = pe.matmul(bank_d0[:, :], w1t[:, x % 2, h, :], wgv[:, x % 2, h, :], start=(h == 0), stop=(h == 1))
                    last.then_inc(wmul_psum, 1)

                for i in range(rounds):
                    n, a, b, c, d, e, _ = stages(i)
                    x = expert_in(i)
                    if a is not None:
                        pe.wait_ge(g_done, a + 1)
                        after(pe, gt_done, a)
                        after(pe, qt_done, through(i - 1, D))
                        after(pe, z2t_done, through(i - 1, E))
                        for h in range(CHUNKS):
                            for s in range(2):
                                last = pe.transpose(bank_t[:, h * 2 * C + s * C:h * 2 * C + (s + 1) * C],
                                                    gbuf[:, a % 2, s * HW + h * P:s * HW + (h + 1) * P], ident)
                        last.then_inc(gt_psum, 1)
                        after(pe, fraw_done, a)
                        for s in range(2):
                            last = pe.matmul(bank_k[s * KKP:(s + 1) * KKP, 0:HW], kw_t, gbuf[:, a % 2, s * HW:(s + 1) * HW], start=True, stop=True)
                        last.then_inc(keys_done, 1)
                    if x is not None and c is None and a is not None:
                        expert_weights(i, x)
                    if b is not None:
                        pe.wait_ge(fraw_done, b + 1)
                        after(pe, filt_done, b)
                        after(pe, pos_done, through(i - 1, E))
                        pe.matmul(bank_b[:, 0:2 * KK], c0_t, fraw[:, b % 2, :, :].rearrange("p s k -> p (s k)"), start=True, stop=True).then_inc(conv0_psum, 1)
                    if c is not None:
                        pe.wait_ge(filt_done, c + 1)
                        if c == 0:
                            pe.wait_ge(ld_c2, 16)
                        after(pe, prod_done, c)
                        after(pe, zhat_done, 2 * c)
                        after(pe, wlow_done, experts_through(i - 1))
                        after(pe, wbias_done, experts_through(i - 1))
                        for r in range(4):
                            last = pe.matmul(bank_d[r // 2][0:tile_rows[r], r % 2 * 2 * C:(r % 2 + 1) * 2 * C],
                                             tapf[0:KK, tile_cols[r]], filt[:, :, :].rearrange("k s c -> k (s c)"),
                                             start=True, stop=True)
                            if r % 2:
                                last.then_inc(what_psum, 1)
                    if b is not None:
                        pe.wait_ge(f0_done, b + 1)
                        pe.matmul(bank_b[:, 128:130], mean_all, fsum[:, :], start=True, stop=True).then_inc(fmean_psum, 1)
                        pe.wait_ge(gt_done, b + 1)
                        if b == 0:
                            pe.wait_ge(ld_c2, 16)
                        after(pe, ghat_done, 2 * b)
                        after(pe, e_done, 4 * through(i - 1, D))
                        features_spectrum(b, (0, 1))
                    if b is not None:
                        features_spectrum(b, (2,))
                    if d is not None:
                        features_of_z(i, d)
                    if e is not None and b is not None:
                        router_input(i, e)
                    if d is not None:
                        pe.wait_ge(qt_done, d + 1)
                        after(pe, ghat_done, 2 * through(i, B))
                        after(pe, e_done, 4 * d)
                        for s in range(2):
                            for h in range(CHUNKS):
                                last = pe.matmul(bank_s[s][:, h * HW:(h + 1) * HW], qt[:, s * HW + h * P:s * HW + (h + 1) * P],
                                                 qt[:, s * HW:(s + 1) * HW], start=True, stop=True)
                            last.then_inc(score_psum, 1)
                    if e is not None and b is None:
                        router_input(i, e)
                        router(i, e)
                    if e is not None and b is not None:
                        router(i, e)
                    if b is not None:
                        pe.wait_ge(fsqs_done, b + 1)
                        after(pe, logits_done, through(i, E))
                        pe.matmul(bank_b[:, 132:134], mean_all, fsqs[:, :], start=True, stop=True).then_inc(fvar_psum, 1)
                    if x is not None and c is not None and a is not None:
                        expert_weights(i, x)
                    if a is not None:
                        pe.wait_ge(kprob_done, a + 1)
                        for h in range(CHUNKS):
                            last = pe.transpose(bank_k[:, HW + h * P:HW + (h + 1) * P], kprob[:, h * P:(h + 1) * P], ident)
                        last.then_inc(pt_psum, 1)
                    if n is not None:
                        pe.wait_ge(gn_mv_done, n + 1)
                        after(pe, zhat_done, 2 * through(i, CC))
                        after(pe, wbias_done, experts_through(i - 1))
                        pe.matmul(bank_d1[:, 0:2], group_avg, gn_mv[:, n % 2, :, 0], start=True, stop=True).then_inc(gn_avg, 1)
                    if c is not None:
                        pe.wait_ge(zhat_done, 2 * (c + 1))
                        after(pe, t2_done, through(i - 1, D))
                        after(pe, t1_done, c)
                        for h in range(CHUNKS):
                            for r in range(4):
                                last = pe.matmul(bank_o[:, h * 2 * C:(h + 1) * 2 * C], inv[0:tile_rows[r], r, h * P:(h + 1) * P],
                                                 zhat[0:tile_rows[r], r, :], start=(r == 0), stop=(r == 3))
                        last.then_inc(conv_psum, 1)
                    if e is not None:
                        if e == 0:
                            pe.wait_ge(const_ready, 1)
                        pe.wait_ge(either_done, e + 1)
                        after(pe, fvar_done, through(i, B))
                        for t in range(TILES):
                            for u in range(t):
                                pe.matmul(bank_b[:, 64 + t * EXPERTS:64 + (t + 1) * EXPERTS], ones[:, :], either[:, u, :], start=(u == 0), stop=False)
                            pe.matmul(bank_b[:, 64 + t * EXPERTS:64 + (t + 1) * EXPERTS], before[:, :], either[:, t, :], start=(t == 0), stop=True)
                        for u in range(TILES):
                            last = pe.matmul(bank_b[:, 96:96 + EXPERTS], ones[:, :], either[:, u, :], start=(u == 0), stop=(u == TILES - 1))
                        last.then_inc(rank_psum, 1)
                    if n is not None:
                        pe.wait_ge(gn_e2_done, n + 1)
                        pe.matmul(bank_d1[:, 4:6], group_avg, gn_e2[:, :], start=True, stop=True).then_inc(gn_avg2, 1)
                    if a is not None:
                        pe.wait_ge(pt_done, a + 1)
                        pe.wait_ge(gt_done, a + 1)
                        for s in range(2):
                            for h in range(CHUNKS):
                                last = pe.matmul(bank_k[:, s * KKP:(s + 1) * KKP], gt[:, a % 2, h, s * C:(s + 1) * C],
                                                 pt[:, h, s * KKP:(s + 1) * KKP], start=(h == 0), stop=(h == CHUNKS - 1))
                        last.then_inc(fraw_psum, 1)
                    if d is not None:
                        pe.wait_ge(e_done, 4 * (d + 1))
                        after(pe, t1_done, through(i, CC))
                        after(pe, t2_done, d)
                        for h in range(CHUNKS):
                            for s in range(2):
                                for k in range(CHUNKS):
                                    last = pe.matmul(bank_o[:, (h * 2 + s) * C:(h * 2 + s + 1) * C], e_attn[:, s, k, h * P:(h + 1) * P],
                                                     z[:, d % 2, k * 2 + s, :], start=(k == 0), stop=(k == CHUNKS - 1))
                        last.then_inc(attn_psum, 1)
                    if b is not None:
                        pe.wait_ge(frelu_done, b + 1)
                        after(pe, pos_done, through(i, E))
                        for s in range(2):
                            last = pe.matmul(bank_b[0:KK, 256 + s * C:256 + (s + 1) * C], frelu[:, s, :], c1_t, start=True, stop=True)
                        last.then_inc(filt_psum, 1)
                    if x is not None and a is None:
                        expert_weights(i, x)
                    if x is not None:
                        after(pe, gn_var_done, through(i, N))
                        after(pe, zhat_done, 2 * through(i, CC))
                        if x == 0:
                            pe.wait_ge(ld_bias, 32)
                        for q in range(4):
                            for h in range(2):
                                last = pe.matmul(bank_d1[:, 8 + q:9 + q], wgv[:, x % 2, h, q * P:(q + 1) * P], b1c[:, 2 * x + h:2 * x + h + 1],
                                                 start=(h == 0), stop=(h == 1))
                        last.then_inc(wbias_psum, 1)
                experts["tensor"](pe)


def expert_programs(sb, sem, out, g):
    rows_dram, moe_dram, ident, ones, banks = g["rows_dram"], g["moe_dram"], g["ident"], g["ones"], g["banks"]
    iota8, base, w_high, w_low, w2_all, t2, y_first = g["iota8"], g["base"], g["w_high"], g["w_low"], g["w2_all"], g["t2"], g["first"]
    bias_col, b2 = g["bias_col"], g["b2"]
    E, NB, U = EXPERTS, BLOCKS, UNROLL
    NTHR = TOKENS // P
    ZERO = EXPERTS * REGION
    TURNS = NB // U

    region = sb("region", [P, E])
    threshold = sb("threshold", [P, NTHR])
    channel = sb("channel", [P, 1])
    channel_rows = sb("channel_rows", [P, 1])
    iota9 = sb("iota9", [P, E + 1])
    count = sb("count", [P, E])
    more = sb("more", [P, E, NTHR])
    nblk = sb("nblk", [P, E])
    upto = sb("upto", [P, E, E])
    cumt = sb("cumt", [P, E, E])
    cum = sb("cum", [P, E])
    cum_before = sb("cum_before", [P, E])
    offset = sb("offset", [P, E + 1])
    past = sb("past", [P, E])
    expert = sb("expert", [P, 1])
    offs = sb("offs", [P, E + 1])
    start = sb("start", [P, 1])
    block_row = sb("block_row", [P, 1])
    block_expert = sb("block_expert", [P, 1])
    table = sb("table", [1, 2, P], I32)
    pad_at = sb("pad_at", [1, E], I32)
    pad_row = sb("pad_row", [P, ROW])
    warm = sb("warm", [P, 1])

    def parts_of(name, rows):
        return sb(f"{name}_rest", [rows, 2, P]), sb(f"{name}_part", [rows, 3, P], BF16)

    bias_full = sb("bias_full", [4 * E, P])
    bias_rest, bias_part = parts_of("bias", 4 * E)
    b2_rest, b2_part = parts_of("b2", E)
    bias_rows = sb("bias_rows", [3, E * 2 * HID], BF16)
    b2_rows = sb("b2_rows", [3, E * C], BF16)

    xs = sb("xs", [P, U, ROW])
    x_high = sb("x_high", [P, 2, P], F32R)
    x_low = sb("x_low", [P, 2, P], F32R)
    silu = sb("silu", [P, 2, HID])
    gated = sb("gated", [P, 2, HID])
    gatedt = sb("gatedt", [P, 2, HID])
    ys = sb("ys", [P, U, C])
    y_second = w_high.bitcast(F32)[:, :].rearrange("p (b t c) -> p b t c", b=PAIRS, t=TILES)
    bank_k, bank_t = banks[0:2]
    bank_x, bank_h, bank_g, bank_y = banks[0:2], banks[2:4], banks[4:6], banks[6:8]

    names = ("consts triangle pads_sent zeros_sent pad_at_ready bias_psum bias_copied b2_ready bias_ready bias_sent chain bias_chain "
             "block_ready table_psum table_ready "
             "xt_psum xhigh_done xlow_done h_psum silu_done gated_done gt_psum gt_done y_psum ys_done "
             "sending sum1_done sum_done stored").split()
    S = {n: sem("moe_" + n) for n in names}
    xs_loaded = [sem(f"moe_xs_loaded{u}") for u in range(U)]
    ys_sent = [sem(f"moe_ys_sent{u}") for u in range(U)]
    y_loaded = [sem(f"moe_y_loaded{p}") for p in range(PAIRS)]

    def over_blocks(eng, step):
        for u in range(U):
            step(u, u, 0, True, False)
        with eng.Fori(1, TURNS - 1) as it:
            for u in range(U):
                step(it * U + u, u, it, False, False)
        for u in range(U):
            step((TURNS - 1) * U + u, u, TURNS - 1, False, True)

    def write_pads(queue, some_experts):
        queue.wait_ge(S["pad_at_ready"], 1)
        queue.wait_ge(S["consts"], 2)
        for e in some_experts:
            row0 = queue.value_load(pad_at[0:1, e:e + 1], min_val=0, max_val=ZERO)
            queue.dma_start(rows_dram[bass.ds(row0, P), :], pad_row[:, :]).then_inc(S["pads_sent"], 16)

    def constants_(pool):
        pool.memset(pad_row[:, :], 0.0)
        pool.iota(region[:, :], pattern=[[REGION, E]], base=0, channel_multiplier=0, allow_small_or_imprecise_dtypes=True)
        pool.iota(threshold[:, :], pattern=[[P, NTHR]], base=0, channel_multiplier=0, allow_small_or_imprecise_dtypes=True)
        pool.iota(channel[:, :], pattern=[[0, 1]], base=0, channel_multiplier=1, allow_small_or_imprecise_dtypes=True)
        pool.iota(channel_rows[:, :], pattern=[[0, 1]], base=0, channel_multiplier=P, allow_small_or_imprecise_dtypes=True)
        pool.iota(iota9[:, :], pattern=[[1, E + 1]], base=0, channel_multiplier=0, allow_small_or_imprecise_dtypes=True)
        pool.iota(offset[:, E:E + 1], pattern=[[0, 1]], base=ZERO, channel_multiplier=-P,
                  allow_small_or_imprecise_dtypes=True).then_inc(S["consts"], 1)
        pool.wait_ge(S["consts"], 1)
        pool.iota(pad_row[:, C + 1:C + 2].bitcast(U32), pattern=[[0, 1]], base=SKIP, channel_multiplier=1).then_inc(S["consts"], 1)
        pool.wait_ge(S["consts"], 2)
        pool.dma_start(rows_dram[ZERO:ZERO + P, :], pad_row[:, :]).then_inc(S["zeros_sent"], 16)

    def gpsimd(pool):
        def send(j, u, it, first, last):
            pool.wait_ge(S["ys_done"], j + 1)
            pool.sem_inc(S["sending"], 1)
            pool.indirect_dma_start(moe_dram, bass.IndirectOffsetOnAxis(ap=xs[:, u, C + 1:C + 2].bitcast(U32), axis=0),
                                    ys[:, u, :], None, bounds_check=2 * TOKENS - 1, oob_is_err=False).then_inc(ys_sent[u], 16)

        over_blocks(pool, send)

    def sync(sp):
        write_pads(sp, range(0, E // 2))
        sp.wait_ge(S["table_ready"], 1)
        sp.wait_ge(S["zeros_sent"], 16)
        sp.wait_ge(S["pads_sent"], 16 * E)
        for s in range(2):
            sp.wait_ge(g["sent"][s], 16 * 2 * TILES * (PAIRS // 2))

        def load(j, u, it, first, last):
            if not first:
                sp.wait_ge(ys_sent[u], 16 * it)
            row0 = sp.value_load(table[0:1, 0, bass.ds(j, 1)], min_val=0, max_val=ZERO)
            sp.dma_start(xs[:, u, :], rows_dram[bass.ds(row0, P), :]).then_inc(xs_loaded[u], 16)

        over_blocks(sp, load)
        for u in range(U):
            sp.wait_ge(ys_sent[u], 16 * TURNS)
        halves = moe_dram.rearrange("(k n p t) c -> k n p (t c)", k=2, n=P, t=TILES)
        for p in range(PAIRS):
            for k, dst in ((0, y_first), (1, y_second)):
                sp.dma_start(dst[:, p, :, :].rearrange("n t c -> n (t c)"), halves[k, :, p]).then_inc(y_loaded[p], 16)
        sp.wait_ge(S["stored"], 16 * PAIRS)

    def scalar(act):
        act.wait_ge(S["b2_ready"], 1)
        for k in range(3):
            act.dma_start(b2_rows[k:k + 1, :].rearrange("o (r f) -> o r f", f=P), b2_part[:, k, :]).then_inc(S["bias_sent"], 16)
        write_pads(act, range(E // 2, E))
        act.wait_ge(S["bias_ready"], 1)
        for k in range(3):
            act.dma_start(bias_rows[k:k + 1, :].rearrange("o (r f) -> o r f", f=P), bias_part[:, k, :]).then_inc(S["bias_sent"], 16)
        act.activation(warm[:, :], g["minus_half"][:, 0:1], ACT.Silu)

        def high_part(j, v):
            act.wait_ge(S["xt_psum"], j + 1)
            act.activation(x_high[:, v, :], bank_x[v][:, 0:P], ACT.Copy).then_inc(S["xhigh_done"], 1)

        def step(j, u, it, first, last):
            if first and u == 0:
                high_part(0, 0)
            if not (last and u == U - 1):
                high_part(j + 1, (u + 1) % 2)
            act.wait_ge(S["h_psum"], j + 1)
            act.activation(silu[:, u % 2, :], bank_h[u % 2][:, 0:HID], ACT.Silu).then_inc(S["silu_done"], 1)

        over_blocks(act, step)
        for p in range(PAIRS):
            act.wait_ge(S["sum_done"], p + 1)
            act.dma_start(out[:, p], y_second[:, p, :, :]).then_inc(S["stored"], 16)

    def triangle(dve):
        dve.wait_ge(g["iota_ready"], 3)
        dve.tensor_tensor(upto[:, :, :], spread(iota8[:, :], 2, E), spread(iota8[:, :], 1, E), ALU.is_ge).then_inc(S["triangle"], 1)

    def b2_parts(dve):
        bias_parts(dve, b2, b2_rest, b2_part, 0, S["b2_ready"])

    def bias_parts(dve, full, rest, part, steps, ready):
        n = [steps]

        def then(instruction):
            n[0] += 1
            instruction.then_inc(S["bias_chain"], 1)
            dve.wait_ge(S["bias_chain"], n[0])

        if full is b2:
            dve.wait_ge(g["ld_w2"], 32)
        else:
            dve.wait_ge(S["bias_psum"], 1)
            dve.tensor_copy(bias_full[:, :], bank_t[0:4 * E, 0:P]).then_inc(S["bias_copied"], 1)
            dve.wait_ge(S["bias_copied"], 1)
        then(dve.tensor_copy(part[:, 0, :], full[:, :]))
        then(dve.tensor_tensor(rest[:, 0, :], full[:, :], part[:, 0, :], ALU.subtract))
        then(dve.tensor_copy(part[:, 1, :], rest[:, 0, :]))
        then(dve.tensor_tensor(rest[:, 1, :], rest[:, 0, :], part[:, 1, :], ALU.subtract))
        dve.tensor_copy(part[:, 2, :], rest[:, 1, :]).then_inc(ready, 1)

    def tables(dve):
        n = [0]

        def then(instruction):
            n[0] += 1
            instruction.then_inc(S["chain"], 1)
            dve.wait_ge(S["chain"], n[0])

        dve.wait_ge(S["consts"], 1)
        dve.wait_ge(S["triangle"], 1)
        dve.wait_ge(g["base_done"], PAIRS)
        dve.tensor_copy(pad_at[:, :], base[0:1, 0, :]).then_inc(S["pad_at_ready"], 1)
        then(dve.tensor_tensor(count[:, :], base[:, 0, :], region[:, :], ALU.subtract))
        then(dve.tensor_tensor(more[:, :, :], spread(count[:, :], 2, NTHR), spread(threshold[:, :], 1, E), ALU.is_gt))
        then(dve.reduce_sum(nblk[:, :], more[:, :, :], AX.X))
        then(dve.tensor_tensor(cumt[:, :, :], upto[:, :, :], spread(nblk[:, :], 1, E), ALU.mult))
        then(dve.reduce_sum(cum[:, :], cumt[:, :, :], AX.X))
        dve.tensor_tensor(cum_before[:, :], cum[:, :], nblk[:, :], ALU.subtract)
        then(dve.tensor_scalar(past[:, :], cum[:, :], channel[:, 0:1], None, ALU.is_le))
        dve.scalar_tensor_tensor(offset[:, 0:E], cum_before[:, :], -float(P), region[:, :], ALU.mult, ALU.add)
        then(dve.reduce_sum(expert[:, :], past[:, :], AX.X))
        then(dve.scalar_tensor_tensor(offs[:, :], iota9[:, :], expert[:, 0:1], offset[:, :], ALU.is_equal, ALU.mult))
        then(dve.reduce_sum(start[:, :], offs[:, :], AX.X))
        dve.tensor_scalar(block_expert[:, :], expert[:, :], float(E - 1), None, ALU.min)
        dve.tensor_tensor(block_row[:, :], start[:, :], channel_rows[:, :], ALU.add).then_inc(S["block_ready"], 1)

    def vector(dve):
        dve.wait_ge(S["table_psum"], 1)
        dve.tensor_copy(table[:, :, :].rearrange("o r j -> o (r j)"), bank_k[0:1, 0:2 * P]).then_inc(S["table_ready"], 1)
        bias_parts(dve, bias_full, bias_rest, bias_part, 4, S["bias_ready"])

        def low_part(j, v):
            dve.wait_ge(S["xhigh_done"], j + 1)
            dve.tensor_tensor(x_low[:, v, :], bank_x[v][:, 0:P], x_high[:, v, :], ALU.subtract).then_inc(S["xlow_done"], 1)

        def gatedt_copy(j, v):
            dve.wait_ge(S["gt_psum"], j + 1)
            dve.tensor_copy(gatedt[:, v, :], bank_g[v][:, 0:HID]).then_inc(S["gt_done"], 1)

        def scale(j, u, it, first_use):
            dve.wait_ge(S["y_psum"], j + 1)
            if not first_use:
                dve.wait_ge(ys_sent[u], 16 * it)
            dve.tensor_scalar(ys[:, u, :], bank_y[u % 2][:, 0:C], xs[:, u, C:C + 1], None, ALU.mult).then_inc(S["ys_done"], 1)

        def step(j, u, it, turn):
            if turn == 0 and u == 0:
                low_part(0, 0)
            if not (turn == 3 and u == U - 1):
                low_part(j + 1, (u + 1) % 2)
            if not (turn == 0 and u < 1):
                gatedt_copy(j - 1, (u - 1) % 2)
            dve.wait_ge(S["silu_done"], j + 1)
            dve.tensor_tensor(gated[:, u % 2, :], bank_h[u % 2][:, HID:2 * HID], silu[:, u % 2, :], ALU.mult).then_inc(S["gated_done"], 1)
            if not (turn == 0 and u < 2):
                scale(j - 2, (u - 2) % U, it if u >= 2 else it - 1, turn == 0 or (turn == 1 and u < 2))

        for turn in range(2):
            for u in range(U):
                step(turn * U + u, u, turn, turn)
        with dve.Fori(2, TURNS - 1) as it:
            for u in range(U):
                step(it * U + u, u, it, 2)
        for u in range(U):
            step((TURNS - 1) * U + u, u, TURNS - 1, 3)
        gatedt_copy(NB - 1, 1)
        scale(NB - 2, U - 2, TURNS - 1, False)
        scale(NB - 1, U - 1, TURNS - 1, False)

        for p in range(PAIRS):
            dve.wait_ge(y_loaded[p], 16 * 2)
            dve.tensor_tensor(t2[:, p, :, :], t2[:, p, :, :], y_first[:, p, :, :], ALU.add).then_inc(S["sum1_done"], 1)
            dve.wait_ge(S["sum1_done"], p + 1)
            dve.tensor_tensor(y_second[:, p, :, :], t2[:, p, :, :], y_second[:, p, :, :], ALU.add).then_inc(S["sum_done"], 1)

    def tensor(pe):
        pe.wait_ge(S["block_ready"], 1)
        pe.transpose(bank_k[0:1, 0:P], block_row[:, :], ident)
        pe.transpose(bank_k[0:1, P:2 * P], block_expert[:, :], ident).then_inc(S["table_psum"], 1)
        pe.wait_ge(g["wbias_done"], E)
        pe.wait_ge(g["z2t_done"], PAIRS)
        pe.transpose(bank_t[0:4 * E, 0:P], bias_col[:, :], ident).then_inc(S["bias_psum"], 1)
        pe.wait_ge(S["bias_sent"], 16 * 6)
        pe.wait_ge(S["table_ready"], 1)

        def expert_of(j):
            return pe.value_load(table[0:1, 1, bass.ds(j, 1)], min_val=0, max_val=E - 1)

        def x_transpose(u, it):
            pe.wait_ge(xs_loaded[u], 16 * (it + 1))
            pe.transpose(bank_x[u % 2][:, 0:P], xs[:, u, 0:C], ident).then_inc(S["xt_psum"], 1)

        def hidden_high(j, u, e):
            pe.matmul(bank_h[u % 2][:, :], ones[0:3, :], bias_rows[:, bass.ds(e * (2 * HID), 2 * HID)], start=True, stop=False)
            pe.wait_ge(S["xhigh_done"], j + 1)
            pe.matmul(bank_h[u % 2][:, :], x_high[:, u % 2, :], w_high[:, bass.ds(e * (2 * HID), 2 * HID)], start=False, stop=False)
            pe.matmul(bank_h[u % 2][:, :], x_high[:, u % 2, :], w_low[:, bass.ds(e * (2 * HID), 2 * HID)], start=False, stop=False)

        def hidden_low(j, u, e):
            pe.wait_ge(S["xlow_done"], j + 1)
            pe.matmul(bank_h[u % 2][:, :], x_low[:, u % 2, :], w_high[:, bass.ds(e * (2 * HID), 2 * HID)], start=False, stop=True).then_inc(S["h_psum"], 1)

        def gated_transpose(j, v):
            pe.wait_ge(S["gated_done"], j + 1)
            for h in range(2):
                last = pe.transpose(bank_g[v][:, h * P:(h + 1) * P], gated[:, v, h * P:(h + 1) * P], ident)
            last.then_inc(S["gt_psum"], 1)

        def down(j, v, e):
            pe.wait_ge(S["gt_done"], j + 1)
            pe.matmul(bank_y[v][:, 0:C], ones[0:3, :], b2_rows[:, bass.ds(e * C, C)], start=True, stop=False)
            for h in range(2):
                last = pe.matmul(bank_y[v][:, 0:C], gatedt[:, v, h * P:(h + 1) * P], w2_all[:, bass.ds(e * (2 * C) + h * C, C)],
                                 start=False, stop=(h == 1))
            last.then_inc(S["y_psum"], 1)

        known = {}
        carried = [pe.alloc_register(f"carried{k}") for k in range(3)]

        def step(j, u, it, first, last):
            if first and u == 0:
                known[0] = expert_of(j)
                x_transpose(0, 0)
            elif u == 0:
                for k in range(3):
                    known[k - 2] = pe.snap(carried[k], min_val=0, max_val=E - 1)
            if not (last and u == U - 1):
                x_transpose((u + 1) % U, it if u < U - 1 else it + 1)
            hidden_high(j, u, known[u])
            if not (last and u == U - 1):
                known[u + 1] = expert_of(j + 1)
            if not last and u == U - 1:
                for k in range(3):
                    pe.reg_mov(carried[k], known[U - 2 + k])
            hidden_low(j, u, known[u])
            if not (first and u < 1):
                gated_transpose(j - 1, (u - 1) % 2)
            if not (first and u < 2):
                down(j - 2, u % 2, known[u - 2])

        over_blocks(pe, step)
        gated_transpose(NB - 1, (NB - 1) % 2)
        down(NB - 2, NB % 2, known[U - 2])
        down(NB - 1, (NB - 1) % 2, known[U - 1])

    return {"constants": constants_, "gpsimd": gpsimd, "sync": sync, "scalar": scalar, "triangle": triangle,
            "b2_parts": b2_parts, "tables": tables, "vector": vector, "tensor": tensor}


def kernel(**inputs):
    import concourse.bacc as bacc
    from concourse.bass_utils import run_bass_kernel_spmd

    f = {k: np.asarray(v) for k, v in inputs.items()}
    x = f["x"].reshape(BATCH, C, HW)
    small = np.zeros((P, 428), np.float32)
    small[:, 0:KK] = f["L0_conv_K_w"].T
    small[:, 64:192] = f["L0_conv_conv0_w"].T
    small[:, 192:320] = f["L0_conv_conv1_w"].T
    small[:, 320:328] = f["L1_ffn_router_w"]
    small[:, 328:377] = f["L0_conv_ln_w"].reshape(C, KK)
    small[:, 377:426] = f["L0_conv_ln_b"].reshape(C, KK)
    small[0:KK, 426] = f["L0_conv_K_b"]
    small[KKP:KKP + KK, 426] = f["L0_conv_K_b"]
    small[:, 427] = f["L0_conv_conv0_b"]
    bgv = np.concatenate([f["L1_ffn_bg"].reshape(EXPERTS, 2, P), f["L1_ffn_bv"].reshape(EXPERTS, 2, P)], 1)
    const = constants()
    arrays = {
        "x": x,
        "xt": x.reshape(PAIRS, 2, C, CHUNKS, P).transpose(4, 0, 3, 1, 2).reshape(P, PAIRS, TILES, C),
        "const": np.concatenate([const[n] for n in WIDTHS], 1).astype(np.float32),
        "small": small,
        "c1_b": f["L0_conv_conv1_b"],
        "router_b": f["L1_ffn_router_b"],
        "w1t": f["L1_ffn_w1"].transpose(0, 2, 1),
        "wg": f["L1_ffn_wg"],
        "wv": f["L1_ffn_wv"],
        "b1c": f["L1_ffn_b1"].reshape(EXPERTS * 2, P).T,
        "bgv": bgv.reshape(EXPERTS * 4, P).T,
        "w2": f["L1_ffn_w2"].reshape(EXPERTS * 2, P, C).transpose(1, 0, 2).reshape(P, EXPERTS * 2 * C),
        "b2": f["L1_ffn_b2"],
    }
    arrays = {k: np.ascontiguousarray(v) for k, v in arrays.items()}
    nc = bacc.Bacc("TRN2", target_bir_lowering=False, num_devices=1)
    aps = {k: nc.dram_tensor("in_" + k, v.shape, mybir.dt.from_np(v.dtype), kind="ExternalInput").ap() for k, v in arrays.items()}
    out = nc.dram_tensor("out", (P, PAIRS, TILES, C), F32, kind="ExternalOutput").ap()
    build(nc, aps, out)
    got = run_bass_kernel_spmd(nc, [{"in_" + k: v for k, v in arrays.items()}], core_ids=[0]).results[0]["out"]
    got = got.reshape(P, PAIRS, CHUNKS, 2, C).transpose(1, 3, 4, 2, 0)
    return got.reshape(BATCH, C, SIDE_IN, SIDE_IN)
```
